# Optimizing a Trainium2 kernel written in Bass

```python
import numpy as np
import jax
import jax.numpy as jnp

def _softmax(x, axis=-1):
    return jax.nn.softmax(x, axis=axis)

def _gelu(x):
    return jax.nn.gelu(x, approximate=True)

def _silu(x):
    return jax.nn.silu(x)

def _sigmoid(x):
    return jax.nn.sigmoid(x)

def _layernorm(x, axis=-1, eps=1e-05):
    m = jnp.mean(x, axis=axis, keepdims=True)
    v = jnp.var(x, axis=axis, keepdims=True)
    return (x - m) / jnp.sqrt(v + eps)

def _scatter_add(tgt, idx, src, axis=0):
    return tgt.at[idx].add(src)

def _segment_sum(src, seg, n):
    return jax.ops.segment_sum(src, seg, n)
kernel_name = 'mk_adaln_ffn_d1_seqx_r8_3cc887'

def setup_inputs(seed: int=0):
    np.random.seed(seed)
    _w = jnp.asarray

    def _rec_inputs():
        import jax
        import jax.numpy as jnp
        _rk = jax.random.key(seed)
        x = -0.0002928 + 1 * jax.random.normal(jax.random.fold_in(_rk, 1), (4, 256, 128), jnp.float32)
        _lenS = 256 - jax.random.randint(jax.random.fold_in(_rk, 7), (4,), 0, max(1, 256 // 4) + 1, jnp.int32)
        _lenS2 = 256 - jax.random.randint(jax.random.fold_in(_rk, 8), (4,), 0, max(1, 256 // 4) + 1, jnp.int32)
        cond_64 = -0.0184271 + 1.00439 * jax.random.normal(jax.random.fold_in(_rk, 12), (4, 64), jnp.float32)
        _validS = jnp.arange(256)[None, :] < _lenS[:, None]
        _validS2 = jnp.arange(256)[None, :] < _lenS2[:, None]
        _causal = jnp.tril(jnp.ones((256, 256), dtype=bool))
        mask_BxS_bf1 = jnp.ones((4, 256), dtype=bool)
        return (x, cond_64, mask_BxS_bf1)
    x, cond_64, mask_BxS_bf1 = _rec_inputs()

    def _L0_cond_setup():
        import jax, jax.numpy as jnp
        import numpy as np
        DIM = 128
        HEADS = 16
        DIM_HEAD = 64
        SCALE = 8.0

        def ln(x, g, eps=1e-05):
            mean = x.mean(axis=-1, keepdims=True)
            var = ((x - mean) ** 2).mean(axis=-1, keepdims=True)
            return (x - mean) * jax.lax.rsqrt(var + eps) * g

        def l2norm(t):
            n = jnp.maximum(jnp.linalg.norm(t, axis=-1, keepdims=True), 1e-12)
            return t / n

        def rel_pos_bias(n, w0, b0, g0, w1, b1, g1, w2, b2, dtype):
            pos = jnp.arange(-n + 1, n, dtype=dtype)[:, None]
            h = jax.nn.silu(ln(pos @ w0 + b0, g0))
            h = jax.nn.silu(ln(h @ w1 + b1, g1))
            h = h @ w2 + b2
            i = jnp.arange(n)
            idx = i[:, None] - i[None, :] + n - 1
            bias = h[idx]
            return jnp.transpose(bias, (2, 0, 1))
        key = jax.random.key(seed)
        ks = jax.random.split(key, 16)
        b, n = (2, 256)
        inner = HEADS * DIM_HEAD
        s = 0.02
        return {'x': jax.random.normal(ks[0], (b, n, DIM), jnp.float32), 'mask': jnp.ones((b, n), dtype=bool), 'g_norm': jnp.ones((DIM,), jnp.float32), 'Wq': jax.random.normal(ks[1], (DIM, inner), jnp.float32) * s, 'Wkv': jax.random.normal(ks[2], (DIM, 2 * DIM_HEAD), jnp.float32) * s, 'q_scale': jnp.ones((DIM_HEAD,), jnp.float32), 'k_scale': jnp.ones((DIM_HEAD,), jnp.float32), 'null_kv': jax.random.normal(ks[3], (2, DIM_HEAD), jnp.float32), 'null_attn_bias': jax.random.normal(ks[4], (HEADS,), jnp.float32), 'w0': jax.random.normal(ks[5], (1, DIM), jnp.float32) * s, 'b0': jnp.zeros((DIM,), jnp.float32), 'g0': jnp.ones((DIM,), jnp.float32), 'w1': jax.random.normal(ks[6], (DIM, DIM), jnp.float32) * s, 'b1': jnp.zeros((DIM,), jnp.float32), 'g1': jnp.ones((DIM,), jnp.float32), 'w2': jax.random.normal(ks[7], (DIM, HEADS), jnp.float32) * s, 'b2': jnp.zeros((HEADS,), jnp.float32), 'Wout': jax.random.normal(ks[8], (inner, DIM), jnp.float32) * s, 'g_out': jnp.ones((DIM,), jnp.float32)}
    _L0_cond_all = _L0_cond_setup()
    _L0_cond_in = {k: v for k, v in _L0_cond_all.items() if k in ('g_norm', 'Wq', 'Wkv', 'q_scale', 'k_scale', 'null_attn_bias', 'w0', 'b0', 'g0', 'w1', 'b1', 'g1', 'w2', 'b2', 'Wout', 'g_out')}
    del _L0_cond_all

    def _L0_ffn_setup():
        import jax, jax.numpy as jnp
        import numpy as np
        DIM = 128
        HEADS = 16
        HD = DIM // HEADS
        M = 32
        E = 4
        K = 2
        HID = 256
        MID = 256
        LB = 0.01
        EPS = 1.1920929e-07

        def _rms(x, w):
            return x * jax.lax.rsqrt(jnp.mean(x * x, axis=-1, keepdims=True) + EPS) * w

        def _gelu(x):
            return jax.nn.gelu(x, approximate=False)
        key = jax.random.key(seed)
        ks = jax.random.split(key, 20)
        d = DIM
        w = lambda k, s: jax.random.normal(k, s, jnp.float32) * 0.02
        return {'x': jax.random.normal(ks[0], (4, 128, d), jnp.float32), 'n1_w': jnp.ones((d,), jnp.float32), 'n2_w': jnp.ones((d,), jnp.float32), 'wq': w(ks[1], (d, d)), 'wk': w(ks[2], (d, d)), 'wv': w(ks[3], (d, d)), 'wo': w(ks[4], (d, d)), 'qn_w': jnp.ones((HD,), jnp.float32), 'kn_w': jnp.ones((HD,), jnp.float32), 'gate_w': w(ks[5], (E, d)), 'e0_up': w(ks[6], (HID, d)), 'e0_down': w(ks[7], (d, HID)), 'e1_w1': w(ks[8], (HID, d)), 'e1_w2': w(ks[9], (HID, d)), 'e1_down': w(ks[10], (d, HID)), 'e2_l1': w(ks[11], (MID, d)), 'e2_l2': w(ks[12], (HID, MID)), 'e2_l3': w(ks[13], (MID, HID)), 'e2_l4': w(ks[14], (d, MID)), 'e3_down': w(ks[15], (d, d)), 'e3_up': w(ks[16], (HID, d)), 'e3_out': w(ks[17], (d, HID))}
    _L0_ffn_all = _L0_ffn_setup()
    _L0_ffn_in = {k: v for k, v in _L0_ffn_all.items() if k in ('n1_w', 'n2_w', 'wq', 'wk', 'wv', 'wo', 'qn_w', 'kn_w', 'gate_w', 'e0_up', 'e0_down', 'e1_w1', 'e1_w2', 'e1_down', 'e2_l1', 'e2_l2', 'e2_l3', 'e2_l4', 'e3_down', 'e3_up', 'e3_out')}
    del _L0_ffn_all
    return {'x': x, 'cond_64': cond_64, 'mask_BxS_bf1': mask_BxS_bf1, 'L0_cond_g_norm': _L0_cond_in['g_norm'], 'L0_cond_Wq': _L0_cond_in['Wq'], 'L0_cond_Wkv': _L0_cond_in['Wkv'], 'L0_cond_q_scale': _L0_cond_in['q_scale'], 'L0_cond_k_scale': _L0_cond_in['k_scale'], 'L0_cond_null_attn_bias': _L0_cond_in['null_attn_bias'], 'L0_cond_w0': _L0_cond_in['w0'], 'L0_cond_b0': _L0_cond_in['b0'], 'L0_cond_g0': _L0_cond_in['g0'], 'L0_cond_w1': _L0_cond_in['w1'], 'L0_cond_b1': _L0_cond_in['b1'], 'L0_cond_g1': _L0_cond_in['g1'], 'L0_cond_w2': _L0_cond_in['w2'], 'L0_cond_b2': _L0_cond_in['b2'], 'L0_cond_Wout': _L0_cond_in['Wout'], 'L0_cond_g_out': _L0_cond_in['g_out'], 'L0_ffn_n1_w': _L0_ffn_in['n1_w'], 'L0_ffn_n2_w': _L0_ffn_in['n2_w'], 'L0_ffn_wq': _L0_ffn_in['wq'], 'L0_ffn_wk': _L0_ffn_in['wk'], 'L0_ffn_wv': _L0_ffn_in['wv'], 'L0_ffn_wo': _L0_ffn_in['wo'], 'L0_ffn_qn_w': _L0_ffn_in['qn_w'], 'L0_ffn_kn_w': _L0_ffn_in['kn_w'], 'L0_ffn_gate_w': _L0_ffn_in['gate_w'], 'L0_ffn_e0_up': _L0_ffn_in['e0_up'], 'L0_ffn_e0_down': _L0_ffn_in['e0_down'], 'L0_ffn_e1_w1': _L0_ffn_in['e1_w1'], 'L0_ffn_e1_w2': _L0_ffn_in['e1_w2'], 'L0_ffn_e1_down': _L0_ffn_in['e1_down'], 'L0_ffn_e2_l1': _L0_ffn_in['e2_l1'], 'L0_ffn_e2_l2': _L0_ffn_in['e2_l2'], 'L0_ffn_e2_l3': _L0_ffn_in['e2_l3'], 'L0_ffn_e2_l4': _L0_ffn_in['e2_l4'], 'L0_ffn_e3_down': _L0_ffn_in['e3_down'], 'L0_ffn_e3_up': _L0_ffn_in['e3_up'], 'L0_ffn_e3_out': _L0_ffn_in['e3_out']}

def reference(x, cond_64, mask_BxS_bf1, L0_cond_g_norm, L0_cond_Wq, L0_cond_Wkv, L0_cond_q_scale, L0_cond_k_scale, L0_cond_null_attn_bias, L0_cond_w0, L0_cond_b0, L0_cond_g0, L0_cond_w1, L0_cond_b1, L0_cond_g1, L0_cond_w2, L0_cond_b2, L0_cond_Wout, L0_cond_g_out, L0_ffn_n1_w, L0_ffn_n2_w, L0_ffn_wq, L0_ffn_wk, L0_ffn_wv, L0_ffn_wo, L0_ffn_qn_w, L0_ffn_kn_w, L0_ffn_gate_w, L0_ffn_e0_up, L0_ffn_e0_down, L0_ffn_e1_w1, L0_ffn_e1_w2, L0_ffn_e1_down, L0_ffn_e2_l1, L0_ffn_e2_l2, L0_ffn_e2_l3, L0_ffn_e2_l4, L0_ffn_e3_down, L0_ffn_e3_up, L0_ffn_e3_out):
    import jax
    import jax.numpy as jnp

    def _L0_cond_ref(x, mask, g_norm, Wq, Wkv, q_scale, k_scale, null_kv, null_attn_bias, w0, b0, g0, w1, b1, g1, w2, b2, Wout, g_out):
        import jax, jax.numpy as jnp
        import numpy as np
        DIM = 128
        HEADS = 16
        DIM_HEAD = 64
        SCALE = 8.0

        def ln(x, g, eps=1e-05):
            mean = x.mean(axis=-1, keepdims=True)
            var = ((x - mean) ** 2).mean(axis=-1, keepdims=True)
            return (x - mean) * jax.lax.rsqrt(var + eps) * g

        def l2norm(t):
            n = jnp.maximum(jnp.linalg.norm(t, axis=-1, keepdims=True), 1e-12)
            return t / n

        def rel_pos_bias(n, w0, b0, g0, w1, b1, g1, w2, b2, dtype):
            pos = jnp.arange(-n + 1, n, dtype=dtype)[:, None]
            h = jax.nn.silu(ln(pos @ w0 + b0, g0))
            h = jax.nn.silu(ln(h @ w1 + b1, g1))
            h = h @ w2 + b2
            i = jnp.arange(n)
            idx = i[:, None] - i[None, :] + n - 1
            bias = h[idx]
            return jnp.transpose(bias, (2, 0, 1))
        b, n, _ = x.shape
        xn = ln(x, g_norm)
        q = (xn @ Wq).reshape(b, n, HEADS, DIM_HEAD).transpose(0, 2, 1, 3)
        kv = xn @ Wkv
        k, v = (kv[..., :DIM_HEAD], kv[..., DIM_HEAD:])
        nk = jnp.broadcast_to(null_kv[0], (b, 1, DIM_HEAD))
        nv = jnp.broadcast_to(null_kv[1], (b, 1, DIM_HEAD))
        k = jnp.concatenate([nk, k], axis=1)
        v = jnp.concatenate([nv, v], axis=1)
        q = l2norm(q) * q_scale
        k = l2norm(k) * k_scale
        sim = jnp.einsum('bhid,bjd->bhij', q, k) * SCALE
        bias = rel_pos_bias(n, w0, b0, g0, w1, b1, g1, w2, b2, q.dtype)
        null_bias = jnp.broadcast_to(null_attn_bias[:, None, None], (HEADS, n, 1))
        attn_bias = jnp.concatenate([null_bias, bias], axis=-1)
        sim = sim + attn_bias
        neg = -jnp.finfo(sim.dtype).max
        causal = jnp.triu(jnp.ones((n, n + 1), dtype=bool), k=2)
        sim = jnp.where(causal, neg, sim)
        m = jnp.pad(mask, ((0, 0), (1, 0)), constant_values=True)[:, None, None, :]
        sim = jnp.where(m, sim, neg)
        attn = jax.nn.softmax(sim, axis=-1)
        out = jnp.einsum('bhij,bjd->bhid', attn, v)
        out = out.transpose(0, 2, 1, 3).reshape(b, n, HEADS * DIM_HEAD)
        return ln(out @ Wout, g_out)

    def _L0_ffn_ref(x, n1_w, n2_w, wq, wk, wv, wo, qn_w, kn_w, gate_w, e0_up, e0_down, e1_w1, e1_w2, e1_down, e2_l1, e2_l2, e2_l3, e2_l4, e3_down, e3_up, e3_out):
        import jax, jax.numpy as jnp
        import numpy as np
        DIM = 128
        HEADS = 16
        HD = DIM // HEADS
        M = 32
        E = 4
        K = 2
        HID = 256
        MID = 256
        LB = 0.01
        EPS = 1.1920929e-07

        def _rms(x, w):
            return x * jax.lax.rsqrt(jnp.mean(x * x, axis=-1, keepdims=True) + EPS) * w

        def _gelu(x):
            return jax.nn.gelu(x, approximate=False)
        B, T, C = x.shape
        h = _rms(x, n1_w)
        heads = lambda w_: (h @ w_.T).reshape(B, T, HEADS, HD).transpose(0, 2, 1, 3)
        q = _rms(heads(wq), qn_w)
        k = _rms(heads(wk), kn_w)
        v = heads(wv)
        scores = jnp.einsum('bhqd,bhkd->bhqk', q, k) * HD ** (-0.5)
        causal = jnp.tril(jnp.ones((T, T), bool))
        scores = jnp.where(causal[None, None], scores, -jnp.inf)
        attn = jax.nn.softmax(scores, axis=-1)
        ao = jnp.einsum('bhqk,bhkd->bhqd', attn, v).transpose(0, 2, 1, 3).reshape(B, T, C) @ wo.T
        ao = ao.at[:, :, :M].set(0.0)
        x = x + ao
        xf = _rms(x, n2_w).reshape(-1, C)
        N = xf.shape[0]
        logits = jnp.nan_to_num(xf @ gate_w.T)
        probs = jax.nn.softmax(logits, axis=-1)
        topv, topi = jax.lax.top_k(probs, K)
        topv = topv / (topv.sum(-1, keepdims=True) + 1e-08)
        wts = jnp.zeros((N, E), x.dtype).at[jnp.arange(N)[:, None], topi].add(topv)
        o0 = _gelu(xf @ e0_up.T) @ e0_down.T
        o1 = jax.nn.silu(xf @ e1_w1.T) * (xf @ e1_w2.T) @ e1_down.T
        o2 = _gelu(_gelu(_gelu(xf @ e2_l1.T) @ e2_l2.T) @ e2_l3.T) @ e2_l4.T
        o3 = _gelu(_gelu(xf @ e3_down.T) @ e3_up.T) @ e3_out.T
        moe = wts[:, 0:1] * o0 + wts[:, 1:2] * o1 + wts[:, 2:3] * o2 + wts[:, 3:4] * o3
        moe = moe.reshape(B, T, C).at[:, :, :M].set(0.0)
        return x + moe
    x = x + _L0_ffn_ref(_L0_cond_ref(x, mask_BxS_bf1, L0_cond_g_norm, L0_cond_Wq, L0_cond_Wkv, L0_cond_q_scale, L0_cond_k_scale, cond_64, L0_cond_null_attn_bias, L0_cond_w0, L0_cond_b0, L0_cond_g0, L0_cond_w1, L0_cond_b1, L0_cond_g1, L0_cond_w2, L0_cond_b2, L0_cond_Wout, L0_cond_g_out), L0_ffn_n1_w, L0_ffn_n2_w, L0_ffn_wq, L0_ffn_wk, L0_ffn_wv, L0_ffn_wo, L0_ffn_qn_w, L0_ffn_kn_w, L0_ffn_gate_w, L0_ffn_e0_up, L0_ffn_e0_down, L0_ffn_e1_w1, L0_ffn_e1_w2, L0_ffn_e1_down, L0_ffn_e2_l1, L0_ffn_e2_l2, L0_ffn_e2_l3, L0_ffn_e2_l4, L0_ffn_e3_down, L0_ffn_e3_up, L0_ffn_e3_out)
    return x

_drawn_inputs = setup_inputs


def setup_inputs(seed=0):
    import zlib

    import numpy as np

    out = dict(_drawn_inputs(seed))
    spreads = {'L0_cond_g_norm': (1.0, 0.2),
     'L0_cond_q_scale': (1.0, 0.2),
     'L0_cond_k_scale': (1.0, 0.2),
     'L0_cond_b0': (0.0, 0.588),
     'L0_cond_g0': (1.0, 0.6),
     'L0_cond_b1': (0.0, 0.389),
     'L0_cond_g1': (1.0, 0.6),
     'L0_cond_b2': (0.0, 0.497),
     'L0_cond_g_out': (1.0, 0.2),
     'L0_ffn_n1_w': (1.0, 0.6),
     'L0_ffn_n2_w': (1.0, 0.6),
     'L0_ffn_qn_w': (1.0, 0.6),
     'L0_ffn_kn_w': (1.0, 0.6)}
    factors = {'L0_ffn_wq': 8.0,
     'L0_ffn_wk': 8.0,
     'L0_ffn_wo': 2.735,
     'L0_ffn_gate_w': 8.0,
     'L0_ffn_e0_up': 8.0,
     'L0_ffn_e0_down': 8.0,
     'L0_ffn_e1_w1': 8.0,
     'L0_ffn_e1_w2': 8.0,
     'L0_ffn_e1_down': 8.0,
     'L0_ffn_e2_l1': 8.0,
     'L0_ffn_e2_l2': 8.0,
     'L0_ffn_e2_l3': 8.0,
     'L0_ffn_e2_l4': 8.0,
     'L0_ffn_e3_down': 8.0,
     'L0_ffn_e3_up': 8.0,
     'L0_ffn_e3_out': 8.0}
    for name, (base, spread) in spreads.items():
        noise = np.random.default_rng([zlib.crc32(name.encode()), seed]).standard_normal(out[name].shape)
        drawn = base * np.exp(spread * noise) if base else spread * noise
        out[name] = jnp.asarray(drawn.astype(out[name].dtype))
    for name, factor in factors.items():
        out[name] = (out[name] * factor).astype(out[name].dtype)
    return out
```

```python
from contextlib import ExitStack

import concourse.bass as bass
from concourse import mybir

F32 = mybir.dt.float32
U8 = mybir.dt.uint8
ALU = mybir.AluOpType
ACT = mybir.ActivationFunctionType
AX = mybir.AxisListType

P = 128
B, S, D = 4, 256, 128
T = S // P
H, DH = 16, 64
M = H // 2
HD = D // H
HID = 256
E = 4
OFF = 32
DN = D - OFF
KEYS = S + 1
GT = 3 * P
EPS = 1.1920929e-07
ROOM = 60.0

C_GN, C_N1, C_N2, C_QS, C_KS, C_NK, C_QN, C_KN = range(8)
R_GO, R_W0, R_B0, R_G0, R_B1, R_G1 = (D * i for i in range(6))
R_QS, R_KS, R_NV = (6 * D + DH * i for i in range(3))
R_QN, R_KN = 6 * D + 3 * DH, 6 * D + 3 * DH + HD
R_ALL = R_KN + HD
A_KK, A_V, A_W1, A_W2 = 0, P, P + DH, 2 * P + DH
A_Q = A_W2 + H
A_O = A_Q + H * DH
A_ALL = A_O + M * D
W_QKV = 0
W_O = W_QKV + 3 * D
W_G = W_O + DN
W_E0 = W_G + E
W_E11 = W_E0 + HID
W_E12 = W_E11 + HID
W_L1 = W_E12 + HID
W_L2 = W_L1 + HID
W_L3 = W_L2 + 2 * HID
W_D3 = W_L3 + 2 * HID
W_U3 = W_D3 + D
W_DN = W_U3 + HID
W_ALL = W_DN + E * 2 * DN


def adaln_ffn(nc, x_d, cols_d, rows_d, small_d, mask_d, wa_d, wb_d, out_d):
    with ExitStack() as ctx:
        def sb(name, shape, dt=F32):
            return ctx.enter_context(nc.sbuf_tensor(name, shape, dt))

        def ps(name, shape):
            return ctx.enter_context(nc.psum_tensor(name, shape, F32))

        def sem(name):
            return ctx.enter_context(nc.semaphore(name))

        table_d = nc.dram_tensor("bias_table", (H, GT), F32, kind="Internal").ap()
        qinv_d = nc.dram_tensor("q_inverse_norms", (B, P, S), F32, kind="Internal").ap()
        null_d = nc.dram_tensor("null_weights", (H, S), F32, kind="Internal").ap()
        zinv_d = nc.dram_tensor("softmax_inverse_sums", (B, P, S), F32, kind="Internal").ap()

        x = sb("x", [P, B * T, D])
        cols = sb("cols", [P, 8])
        rows = sb("rows", [P, R_ALL])
        small = sb("small", [H, 2])
        mask_u8 = sb("mask_u8", [P, B, 3], U8)
        mask = sb("mask", [P, B, 3])
        wa = sb("wa", [P, A_ALL])
        wb = sb("wb", [P, W_ALL])
        ident = sb("ident", [P, P])
        half_ones = sb("half_ones", [P, P])
        pair_rows = sb("pair_rows", [P, 2, 32])
        sum_rows = sb("sum_rows", [P, 4, 32])
        causal = sb("causal", [P, P])
        head_of = sb("head_of", [P, H])
        minus_half = sb("minus_half", [P, B * T])
        ln_eps = sb("ln_eps", [P, B * T])
        rms_eps = sb("rms_eps", [P, T])
        zeros = sb("zeros", [P, S])
        shift1 = sb("shift1", [P, 4])
        shift2 = sb("shift2", [P, 4])
        qk_scale = sb("qk_scale", [P, 1])
        qk2_scale = sb("qk2_scale", [P, 1])
        pos = sb("pos", [P, T])
        hb = sb("hb", [P, T, D])
        ht = sb("ht", [P, T, D])
        hT = sb("hT", [P, S])
        bst = sb("bst", [P, T, 6])
        bmv = sb("bmv", [P, T, 2])
        bve = sb("bve", [P, T])
        brs = sb("brs", [P, T])
        top = sb("top", [H, 4])
        table = sb("table", [H, GT])
        null_row = sb("null_row", [H, S])
        eb0 = sb("eb0", [P, 2, M, S])
        eb1 = sb("eb1", [P, 2, M, P])
        ebx = sb("ebx", [2, 2, M, 2])
        st_x = sb("st_x", [P, B * T, 6])
        mv_x = sb("mv_x", [P, B * T, 2])
        ve_x = sb("ve_x", [P, B * T])
        rs_x = sb("rs_x", [P, B * T])
        st = sb("st", [P, T, 6])
        mv = sb("mv", [P, T, 2])
        ve = sb("ve", [P, T])
        rs = sb("rs", [P, T])
        xc = sb("xc", [P, T, D])
        xb = sb("xb", [P, S])
        xk = sb("xk", [P, KEYS])
        last_row = sb("last_row", [1, P])
        kr = sb("kr", [P, KEYS])
        ksq = sb("ksq", [P, KEYS])
        kmx = sb("kmx", [P, KEYS])
        ksr = sb("ksr", [P, KEYS])
        kin = sb("kin", [P, KEYS])
        keo = sb("keo", [P, B, 2, KEYS])
        qt = sb("qt", [P, B, M, S])
        qmx = sb("qmx", [P, S])
        qsr = sb("qsr", [P, S])
        qin = sb("qin", [P, S])
        spread = sb("spread", [P, M, S])
        vn = sb("vn", [P, B, 3, DH])
        kf = sb("kf", [P, 2, KEYS])
        vf = sb("vf", [P, 3, DH])
        ocm = sb("ocm", [P, 3, 4, 32])
        pb = [sb(f"pb{i}", [P, 1024]) for i in range(6)]
        px = sb("px", [P, 2, M, 2])
        o_raw = sb("o_raw", [P, M, S])
        qsq = o_raw[:]
        on = sb("on", [P, M, S])
        zmx = sb("zmx", [P, S])
        zin = sb("zin", [P, S])
        yn = sb("yn", [P, T, D])
        x2 = sb("x2", [P, B * T, D])
        hT2 = sb("hT2", [P, S])
        sq2 = sb("sq2", [P, T, 2 * D])
        s64 = sb("s64", [P, T, 2 * H])
        v64 = sb("v64", [P, T, 2 * H])
        r64 = sb("r64", [P, T, 2 * H])
        i64 = sb("i64", [P, T, 2 * H])
        qkn = sb("qkn", [P, T, 2 * D])
        v2 = sb("v2", [P, B, T, H, HD])
        k2f = sb("k2f", [P, S])
        v2f = sb("v2f", [P, T, H, 32])
        o2s = sb("o2s", [P, 2, 512])
        rz2 = sb("rz2", [P, T * 4, 4, 1])
        ao = sb("ao", [P, T, D])
        aoT = sb("aoT", [P, S])
        xf1 = sb("xf1", [P, S])
        lg = sb("lg", [P, B * T, E])
        ga = [sb(f"ga{i}", [P, B * T, E]) for i in range(6)]
        g1 = [sb(f"g1_{i}", [P, B * T]) for i in range(4)]
        gc = [sb(f"gc{i}", [P, B * T, E, E]) for i in range(3)]
        tri = sb("tri", [P, E, E])
        qm = qt[:, 0:2, :, :]
        xfT = qt[:, 2, 0:4, :]
        qt2 = qt[:, 2, 4:8, :]
        kt2 = qt[:, 3, 0:4, :]
        h0 = o_raw[:, 0:2, :]
        h1 = o_raw[:, 2:4, :]
        h2a = o_raw[:, 4:6, :]
        h2b = o_raw[:, 6:8, :]
        h2c = on[:, 0:2, :]
        h3a = on[:, 2, :]
        h3b = on[:, 3:5, :]
        th1 = on[:, 5:7, :]
        si1 = spread[:, 0:2, :]

        sc = ps("sc", [P, 2048])
        oa = ps("oa", [P, 1024])
        tm = ps("tm", [P, 1024])
        zb = tm[:, 0:512]
        mb = tm[:, 512:1024]

        names = """ld_x ld_cols ld_rows ld_small ld_mask ld_wa ld_wb
            consts zeroed mask_ready shifts pos_ready
            bias_dve bias_pool bias_var bias_rstd bias_tanh_in bias_tanh bias_turn_in bias_turned bias_hT bias_mm1 bias_mm2
            bias_top table_ready null_ready table_stored bias_loaded null_loaded
            x_parts x_stat x_var x_rstd xc_ready xt_done xb_ready k_proj v_proj q_proj kr_ready ksq_ready kss_done
            q_raw qsq_ready qss_done kmax_ready ksqrt_ready qmax_ready qsqrt_ready qinv_ready qinv_stored
            qinv_spread q_done keo_done vn_done p1_dve
            kf_ready vf_ready ocm_ready qk_chunk qk_x exp_done px_exp px_ready mult_done pv_done z_done o_evac
            zmax_done zinv_ready zinv_stored zinv_spread on_ready y_done y_parts y_stat y_var y_rstd y_norm x2_done
            r_stat r_var r_rstd h2_ready h2_turned hT2_ready qkv_done sq2_ready s64_ready r64_ready qkn_ready
            v2_done qk_turned qt2_done kt2_done p3_dve
            k2f_ready v2f_ready qm_ready qk2_chunk exp2_done masked pv2_done o2_evac o2_turned ao_ready ao_turned
            aoT_ready wo_done x3_done p4_dve
            f_stat f_var f_rstd f_ready f_turned xf1_ready xfT_ready gate_done lg_ready gate_w xs_ready p5_dve gates
            gate_exp res_part u_done u_act silu_a h1_ready down_done res_done stored""".split()
        s = {n: sem(n) for n in names}

        block = ctx.enter_context(nc.Block())


        def spread_from(dram, b, g, e):
            src = dram[b]
            return bass.AP(tensor=src.tensor, offset=src.offset + (2 * g + e) * S, ap=[[0, DH], [32 * S, 4], [1, S]])

        def nulls_in(e):
            return bass.AP(tensor=null_d.tensor, offset=e * S, ap=[[2 * S, 1], [2 * S, M], [1, S]])

        def tiles(a, b):
            return a[:, bass.ds(T * b, T)]

        def halves(a, n):
            return a.rearrange("p (a c) -> p a c", a=n)

        @block.sync
        def _(sp):
            sp.dma_start(x[:], x_d.rearrange("(n p) d -> p n d", p=P)).then_inc(s["ld_x"], 16)
            sp.dma_start(rows[:], bass.AP(tensor=rows_d.tensor, offset=0, ap=[[0, P], [1, R_ALL]])).then_inc(s["ld_rows"], 16)
            sp.dma_start(cols[:], cols_d).then_inc(s["ld_cols"], 16)
            sp.dma_start(small[:], small_d).then_inc(s["ld_small"], 16)
            sp.dma_start(wa[:], wa_d).then_inc(s["ld_wa"], 16)
            sp.dma_start(mask_u8[:], mask_d).then_inc(s["ld_mask"], 16)
            sp.dma_start(wb[:], wb_d).then_inc(s["ld_wb"], 16)

            sp.wait_ge(s["table_ready"], 1)
            sp.dma_start(table_d, table[:]).then_inc(s["table_stored"], 16)
            sp.wait_ge(s["table_stored"], 16)
            for e in range(2):
                base = e * GT + 1
                sp.dma_start(eb0[:, e], bass.AP(tensor=table_d.tensor, offset=base,
                                                ap=[[1, P], [2 * GT, M], [1, S]])).then_inc(s["bias_loaded"], 16)
                sp.dma_start(eb1[:, e], bass.AP(tensor=table_d.tensor, offset=base,
                                                ap=[[1, P], [2 * GT, M], [1, P]])).then_inc(s["bias_loaded"], 16)
            sp.wait_ge(s["zeroed"], 1)
            for e in range(2):
                for k in range(2):
                    src = bass.AP(tensor=table_d.tensor, offset=e * GT + P - 1, ap=[[2 * GT, 1], [2 * GT, M], [1, 1]])
                    sp.dma_start(ebx[k:k + 1, e, :, k:k + 1], src, allow_slow_non_contiguous=True).then_inc(s["bias_loaded"], 16)
            sp.wait_ge(s["bias_loaded"], 8 * 16)
            sp.wait_ge(s["null_ready"], 1)
            sp.dma_start(null_d, null_row[:]).then_inc(s["null_loaded"], 16)
            sp.wait_ge(s["null_loaded"], 16)
            for e in range(2):
                sp.dma_start(eb0[P - 1:P, e], nulls_in(e)).then_inc(s["null_loaded"], 16)

            with sp.Fori(0, B) as b:
                sp.wait_ge(s["qinv_ready"], b + 1)
                sp.dma_start(qinv_d[b], qin[:]).then_inc(s["qinv_stored"], 16)
                sp.wait_ge(s["qinv_stored"], 16 * (b + 1))
                sp.wait_ge(s["q_done"], b)
                for g in range(2):
                    for e in range(2):
                        sp.dma_start(spread[DH * e:DH * (e + 1), 4 * g:4 * g + 4], spread_from(qinv_d, b, g, e)).then_inc(s["qinv_spread"], 16)
            sp.wait_ge(s["q_done"], B)
            with sp.Fori(0, B) as b:
                sp.wait_ge(s["zinv_ready"], b + 1)
                sp.dma_start(zinv_d[b], zin[:]).then_inc(s["zinv_stored"], 16)
                sp.wait_ge(s["zinv_stored"], 16 * (b + 1))
                sp.wait_ge(s["on_ready"], b)
                for g in range(2):
                    for e in range(2):
                        sp.dma_start(spread[DH * e:DH * (e + 1), 4 * g:4 * g + 4], spread_from(zinv_d, b, g, e)).then_inc(s["zinv_spread"], 16)
            with sp.Fori(0, B) as b:
                sp.wait_ge(s["res_done"], b + 1)
                sp.dma_start(out_d.rearrange("(b n p) d -> p b n d", p=P, n=T)[:, b], tiles(x, b)).then_inc(s["stored"], 16)
            sp.wait_ge(s["stored"], 16 * B)


        @block.gpsimd
        def _(pool):
            n = [0]

            def step(ins):
                n[0] += 1
                ins.then_inc(s["zeroed"], 1)
                pool.wait_ge(s["zeroed"], n[0])

            pool.iota(pos[:], pattern=[[P, T]], base=0, channel_multiplier=1,
                      allow_small_or_imprecise_dtypes=True).then_inc(s["pos_ready"], 1)
            for buf, value in ((half_ones, 0.5), (minus_half, -0.5), (ln_eps, 1e-5), (rms_eps, EPS * D), (ident, 0.0), (sum_rows, 0.0),
                               (head_of, 1.0), (causal, 1.0), (xk, 0.0), (last_row, 0.0), (px, 0.0), (v2f, 0.0), (keo, 0.0), (tri, 1.0), (vn, 0.0)):
                pool.memset(buf[:], value)
            pool.memset(table[:], 0.0)
            pool.memset(ebx[:], 0.0)
            step(pool.memset(zeros[:], 0.0))
            pool.affine_select(out=ident[:], in_=ident[:], compare_op=ALU.not_equal, fill=1.0, base=0,
                               pattern=[[-1, P]], channel_multiplier=1)
            pool.affine_select(out=causal[:], in_=causal[:], compare_op=ALU.is_ge, fill=0.0, base=0,
                               pattern=[[1, P]], channel_multiplier=-1)
            pool.memset(last_row[:, P - 1:P], 1.0)
            for k in range(4):
                pool.memset(sum_rows[:, k, k:k + 1], 1.0)
            pool.affine_select(out=tri[:], in_=tri[:], compare_op=ALU.is_ge, fill=0.0, base=-1,
                               pattern=[[1, E], [-1, E]], channel_multiplier=0)
            step(pool.affine_select(out=head_of[:], in_=head_of[:], compare_op=ALU.is_ge, fill=0.0, base=0,
                                    pattern=[[-HD, H]], channel_multiplier=1))
            pool.affine_select(out=head_of[:], in_=head_of[:], compare_op=ALU.is_ge, fill=0.0, base=HD - 1,
                               pattern=[[HD, H]], channel_multiplier=-1).then_inc(s["consts"], 1)
            pool.wait_ge(s["consts"], 1)

            def rstd(var, eps, ve_, out, ready, done, count, base):
                pool.wait_ge(ready, base + 1)
                pool.tensor_tensor(ve_, var, eps[:, 0:var.shape[1]], ALU.add).then_inc(count, 1)
                pool.wait_ge(count, base + 1)
                pool.tensor_tensor(out, ve_, minus_half[:, 0:var.shape[1]], ALU.pow).then_inc(done, 1)

            for layer in range(2):
                rstd(bmv[:, :, 1], ln_eps, bve[:], brs[:], s["bias_var"], s["bias_rstd"], s["bias_pool"], layer)

            def queries(b):
                pool.wait_ge(s["qinv_spread"], 64 * (b + 1))
                pool.tensor_tensor(qt[:, b], qt[:, b], spread[:], ALU.mult).then_inc(s["q_done"], 1)

            rstd(mv_x[:, :, 1], ln_eps, ve_x[:], rs_x[:], s["x_stat"], s["x_rstd"], s["x_var"], 0)
            with pool.Fori(0, B) as b:
                queries(b)

            def operands(b):
                pool.wait_ge(s["keo_done"], 2 * B)
                pool.wait_ge(s["vn_done"], B)
                pool.wait_ge(s["mask_ready"], 1)
                pool.wait_ge(s["qk_chunk"], 6 * b)
                pool.wait_ge(s["qk_x"], b)
                pool.tensor_copy(kf[:], keo[:, b]).then_inc(s["kf_ready"], 1)
                pool.wait_ge(s["z_done"], 2 * b)
                pool.tensor_copy(vf[:], vn[:, b])
                pool.tensor_tensor(ocm[:], sum_rows[:, None, :, :].to_broadcast([P, 3, 4, 32]),
                                   mask[:, b, :, None, None].to_broadcast([P, 3, 4, 32]), ALU.mult).then_inc(s["vf_ready"], 1)

            def normalised(b):
                pool.wait_ge(s["zinv_spread"], 64 * (b + 1))
                pool.wait_ge(s["o_evac"], 2 * (b + 1))
                pool.wait_ge(s["y_done"], b)
                pool.tensor_tensor(on[:], o_raw[:], spread[:], ALU.mult).then_inc(s["on_ready"], 1)
                rstd(mv[:, :, 1], ln_eps, ve[:], rs[:], s["y_stat"], s["y_rstd"], s["y_var"], b)

            operands(0)
            with pool.Fori(1, B) as b:
                operands(b)
                normalised(b - 1)
            normalised(B - 1)

            with pool.Fori(0, B) as b:
                rstd(mv[:, :, 1], rms_eps, ve[:], rs[:], s["r_stat"], s["r_rstd"], s["r_var"], b)

            with pool.Fori(0, B) as b:
                pool.wait_ge(s["v2_done"], B)
                pool.wait_ge(s["kt2_done"], B)
                pool.wait_ge(s["qk2_chunk"], 6 * b)
                pool.tensor_copy(k2f[:], kt2[:, b]).then_inc(s["k2f_ready"], 1)
                pool.wait_ge(s["pv2_done"], 2 * b)
                pool.tensor_copy(v2f[:, :, :, 0:HD], v2[:, b]).then_inc(s["v2f_ready"], 1)
                for c in range(6):
                    pool.wait_ge(s["exp2_done"], 6 * b + c + 1)
                    heads = 4 if c % 3 < 2 else 8
                    diag = halves(pb[c], heads)[:, :, 0:P]
                    pool.tensor_tensor(diag, diag, causal[:, None, :].to_broadcast([P, heads, P]), ALU.mult).then_inc(s["masked"], 1)

            with pool.Fori(0, B) as b:
                rstd(mv[:, :, 1], rms_eps, ve[:], rs[:], s["f_stat"], s["f_rstd"], s["f_var"], b)
            pool.wait_ge(s["x3_done"], B)
            pool.tensor_tensor(x[:], x[:], x2[:], ALU.add).then_inc(s["xs_ready"], 1)

        @block.scalar
        def _(act):
            nc_ = nc.scalar
            for layer in range(2):
                act.wait_ge(s["bias_tanh_in"], layer + 1)
                nc_.activation(ht[:], hb[:], ACT.Tanh, scale=0.5).then_inc(s["bias_tanh"], 1)
            act.wait_ge(s["bias_top"], 1)
            nc_.activation(table[:, P - 1:P - 1 + S], zb[0:H, 0:S], ACT.Exp, bias=top[:, 3:4]).then_inc(s["table_ready"], 1)
            nc_.activation(null_row[:], zeros[0:H, :], ACT.Exp, bias=top[:, 0:1]).then_inc(s["null_ready"], 1)

            act.wait_ge(s["ld_cols"], 16)
            nc_.copy(kr[:, P - 1:P], cols[:, C_NK:C_NK + 1])
            with act.Fori(0, B) as b:
                act.wait_ge(s["k_proj"], b + 1)
                nc_.copy(kr[:, 0:P - 1], oa[:, 0:P - 1])
                nc_.copy(kr[:, P:KEYS], oa[:, P:KEYS]).then_inc(s["kr_ready"], 1)
                act.wait_ge(s["kr_ready"], b + 1)
                nc_.activation(ksq[:], kr[:], ACT.Square).then_inc(s["ksq_ready"], 1)
                for g in range(2):
                    act.wait_ge(s["q_proj"], 2 * b + g + 1)
                    nc_.copy(qt[:, b, 4 * g:4 * g + 4], halves(sc[:, 1024 * g:1024 * (g + 1)], 4)).then_inc(s["q_raw"], 1)
                    act.wait_ge(s["consts"], 1)
                    act.wait_ge(s["qss_done"], 2 * b)
                    act.wait_ge(s["q_raw"], 2 * b + g + 1)
                    nc_.activation(qsq[:, 4 * g:4 * g + 4], qt[:, b, 4 * g:4 * g + 4], ACT.Square).then_inc(s["qsq_ready"], 1)
                act.wait_ge(s["kmax_ready"], b + 1)
                nc_.activation(ksr[:], kmx[:], ACT.Sqrt).then_inc(s["ksqrt_ready"], 1)
                act.wait_ge(s["qmax_ready"], b + 1)
                nc_.activation(qsr[:], qmx[:], ACT.Sqrt).then_inc(s["qsqrt_ready"], 1)

            act.wait_ge(s["shifts"], 1)
            nc_.preload_act_table(ACT.Exp)

            def exps(b):
                def chunk(c):
                    act.wait_ge(s["qk_chunk"], 6 * b + c + 1)
                    act.wait_ge(s["z_done"], 2 * b)
                    nc_.activation(pb[c][:], sc[:, 1024 * (c % 2):1024 * (c % 2 + 1)], ACT.Exp,
                                   bias=shift1[:, 3:4]).then_inc(s["exp_done"], 1)

                def evacuate(g):
                    act.wait_ge(s["pv_done"], 2 * b + g + 1)
                    act.wait_ge(s["on_ready"], b)
                    nc_.copy(o_raw[:, 4 * g:4 * g + 4], halves(oa[:], 4)).then_inc(s["o_evac"], 1)

                chunk(0)
                chunk(1)
                act.wait_ge(s["qk_x"], b + 1)
                nc_.activation(px[0:2], mb[0:2, 0:32].rearrange("p (e m q) -> p e m q", e=2, m=M), ACT.Exp,
                               bias=shift1[0:2, 3:4]).then_inc(s["px_exp"], 1)
                chunk(2)
                chunk(3)
                evacuate(0)
                chunk(4)
                chunk(5)
                evacuate(1)

            with act.Fori(0, B) as b:
                exps(b)

            with act.Fori(0, B) as b:
                act.wait_ge(s["qkv_done"], b + 1)
                both = halves(sc[:, 0:1024], T)
                nc_.activation(sq2[:], both[:, :, 0:2 * D], ACT.Square).then_inc(s["sq2_ready"], 1)
                nc_.copy(v2[:, b], both[:, :, 2 * D:3 * D].rearrange("p t (h d) -> p t h d", h=H)).then_inc(s["v2_done"], 1)
                act.wait_ge(s["s64_ready"], b + 1)
                nc_.activation(r64[:], v64[:], ACT.Sqrt).then_inc(s["r64_ready"], 1)
                act.wait_ge(s["qk_turned"], b + 1)
                nc_.copy(qt2[:, b], oa[:, 0:S]).then_inc(s["qt2_done"], 1)

            nc_.preload_act_table(ACT.Exp)

            def attend(b, tail):
                def chunk(c):
                    act.wait_ge(s["qk2_chunk"], 6 * b + c + 1)
                    act.wait_ge(s["pv2_done"], 2 * b)
                    nc_.activation(pb[c][:], sc[:, 1024 * (c % 2):1024 * (c % 2 + 1)], ACT.Exp,
                                   bias=shift2[:, 3:4]).then_inc(s["exp2_done"], 1)

                def evacuate(g):
                    act.wait_ge(s["pv2_done"], 2 * b + g + 1)
                    act.wait_ge(s["o2_turned"], b)
                    nc_.copy(o2s[:, g], oa[:, 512 * g:512 * (g + 1)]).then_inc(s["o2_evac"], 1)

                for c in range(4):
                    chunk(c)
                if tail:
                    turned(b - 1)
                evacuate(0)
                chunk(4)
                chunk(5)
                evacuate(1)

            def turned(b):
                act.wait_ge(s["ao_turned"], b + 1)
                nc_.copy(aoT[:], tm[:, 0:S]).then_inc(s["aoT_ready"], 1)

            attend(0, False)
            with act.Fori(1, B) as b:
                attend(b, True)
            turned(B - 1)

            with act.Fori(0, B) as b:
                act.wait_ge(s["xf1_ready"], b + 1)
                nc_.copy(xfT[:, b], xf1[:]).then_inc(s["xfT_ready"], 1)
            act.wait_ge(s["gates"], 7)
            nc_.activation(ga[2][:], lg[:], ACT.Exp).then_inc(s["gate_exp"], 1)
            nc_.preload_act_table(ACT.Gelu)
            with act.Fori(0, B) as b:
                def unit(n, out, func=ACT.Gelu, scale=1.0, width=512):
                    act.wait_ge(s["u_done"], 8 * b + n + 1)
                    src = sc[:, 512 * (n % 4):512 * (n % 4) + width]
                    nc_.activation(out, src if width < 512 else halves(src, 2), func, scale=scale).then_inc(s["u_act"], 1)

                unit(0, h2a)
                unit(1, h3a, width=S)
                act.wait_ge(s["down_done"], 2 * b)
                unit(2, h0)
                unit(3, h2b)
                unit(4, th1, ACT.Tanh, 0.5)
                unit(6, h3b)
                unit(7, h2c)

        @block.vector
        def _(dve):
            v = nc.vector
            n = [0]

            def step(ins):
                n[0] += 1
                ins.then_inc(s["bias_dve"], 1)
                dve.wait_ge(s["bias_dve"], n[0])

            def row(r, width=D):
                return rows[:, r:r + width]

            step(v.memset(pair_rows[:], 0.0))
            for g in range(2):
                for e in range(2):
                    v.memset(pair_rows[DH * e:DH * (e + 1), g, 2 * g + e:2 * g + e + 1], 1.0)
            dve.wait_ge(s["ld_rows"], 16)
            dve.wait_ge(s["pos_ready"], 1)
            for t in range(T):
                last = v.scalar_tensor_tensor(hb[:, t], row(R_W0), pos[:, t:t + 1], row(R_B0), ALU.mult, ALU.add)
            step(last)
            for layer, gain in ((0, R_G0), (1, R_G1)):
                if layer:
                    dve.wait_ge(s["bias_mm1"], 1)
                    step(v.tensor_tensor(hb[:], halves(zb[:, 0:S], T), row(R_B1)[:, None, :].to_broadcast([P, T, D]), ALU.add))
                for t in range(T):
                    last = v.bn_stats(bst[:, t], hb[:, t])
                step(last)
                for t in range(T):
                    last = v.bn_aggr(bmv[:, t], bst[:, t])
                last.then_inc(s["bias_var"], 1)
                dve.wait_ge(s["bias_rstd"], layer + 1)
                for t in range(T):
                    last = v.tensor_scalar(hb[:, t], hb[:, t], bmv[:, t, 0:1], brs[:, t:t + 1], ALU.subtract, ALU.mult)
                step(last)
                v.tensor_tensor(hb[:], hb[:], row(gain)[:, None, :].to_broadcast([P, T, D]), ALU.mult).then_inc(s["bias_tanh_in"], 1)
                dve.wait_ge(s["bias_tanh"], layer + 1)
                v.scalar_tensor_tensor(hb[:], ht[:], 1.0, hb[:], ALU.add, ALU.mult).then_inc(s["bias_turn_in"], 1)
                dve.wait_ge(s["bias_turned"], layer + 1)
                v.tensor_scalar(hT[:], mb[:, 0:S], 0.5, None, ALU.mult).then_inc(s["bias_hT"], 1)
            dve.wait_ge(s["ld_small"], 16)
            dve.wait_ge(s["bias_mm2"], 1)
            v.tensor_reduce(top[:, 0:1], zb[0:H, 0:S], AX.X, ALU.max)
            step(v.tensor_tensor(top[:, 1:2], small[:, 1:2], small[:, 0:1], ALU.subtract))
            step(v.tensor_tensor(top[:, 2:3], top[:, 0:1], top[:, 1:2], ALU.max))
            v.tensor_scalar(top[:, 3:4], top[:, 2:3], -1.0, None, ALU.mult)
            step(v.tensor_tensor(top[:, 0:1], top[:, 1:2], top[:, 2:3], ALU.subtract))
            dve.wait_ge(s["ld_cols"], 16)
            for sh, (rq, rk, width), bound in ((shift1, (R_QS, R_KS, DH), 8.0), (shift2, (R_QN, R_KN, HD), HD ** 0.5)):
                for i, r in enumerate((rq, rk)):
                    last = v.tensor_reduce(sh[:, i:i + 1], row(r, width), AX.X, ALU.max, apply_absolute_value=True)
                step(last)
                step(v.tensor_tensor(sh[:, 2:3], sh[:, 0:1], sh[:, 1:2], ALU.mult))
                v.tensor_scalar(sh[:, 3:4], sh[:, 2:3], -bound, ROOM, ALU.mult, ALU.add)
            v.scalar_tensor_tensor(qk_scale[:], cols[:, C_QS:C_QS + 1], 8.0, cols[:, C_KS:C_KS + 1], ALU.mult, ALU.mult)
            step(v.scalar_tensor_tensor(qk2_scale[:], cols[:, C_QN:C_QN + 1], HD ** -0.5, cols[:, C_KN:C_KN + 1], ALU.mult, ALU.mult))
            v.tensor_copy(top[:, 2:3], top[:, 1:2]).then_inc(s["bias_top"], 1)
            dve.wait_ge(s["ld_mask"], 16)
            v.tensor_copy(mask[:], mask_u8[:]).then_inc(s["mask_ready"], 1)
            v.memset(zmx[:], 1.0).then_inc(s["shifts"], 1)
            dve.wait_ge(s["consts"], 1)
            dve.wait_ge(s["mask_ready"], 1)
            dve.wait_ge(s["ld_x"], 16)

            for t in range(B * T):
                last = v.bn_stats(st_x[:, t], x[:, t])
            last.then_inc(s["x_parts"], 1)
            dve.wait_ge(s["x_parts"], 1)
            for t in range(B * T):
                last = v.bn_aggr(mv_x[:, t], st_x[:, t])
            last.then_inc(s["x_stat"], 1)
            dve.wait_ge(s["x_rstd"], 1)
            with dve.Fori(0, B) as b:
                dve.wait_ge(s["xt_done"], b)
                for t in range(T):
                    last = v.tensor_scalar(xc[:, t], x[:, T * b + t], mv_x[:, T * b + t, 0:1], rs_x[:, bass.ds(T * b + t, 1)], ALU.subtract, ALU.mult)
                last.then_inc(s["xc_ready"], 1)
                dve.wait_ge(s["xt_done"], b + 1)
                dve.wait_ge(s["q_proj"], 2 * b)
                gain = cols[:, C_GN:C_GN + 1]
                v.tensor_scalar(xb[:], mb[:, 0:S], gain, None, ALU.mult)
                v.tensor_scalar(xk[:, 0:P - 1], mb[:, P - 2::-1], gain, None, ALU.mult)
                v.tensor_scalar(xk[:, P:S], mb[:, S - 2:P - 2:-1], gain, None, ALU.mult)
                v.tensor_scalar(xk[:, S:KEYS], mb[:, S - 1:S], gain, None, ALU.mult).then_inc(s["xb_ready"], 1)
                dve.wait_ge(s["v_proj"], b + 1)
                v.tensor_tensor(vn[:, b, 0:2], halves(oa[:, 512:512 + 2 * DH], 2), mask[:, b, 0:2, None].to_broadcast([P, 2, DH]), ALU.mult)
                v.tensor_tensor(vn[0:2, b, 2:3], oa[0:2, None, 512 + 2 * DH:512 + 3 * DH], mask[0:2, b, 2:3, None].to_broadcast([2, 1, DH]),
                                ALU.mult).then_inc(s["vn_done"], 1)
                dve.wait_ge(s["kss_done"], b + 1)
                v.tensor_scalar(kmx[:], oa[:, 0:KEYS], 1e-24, None, ALU.max).then_inc(s["kmax_ready"], 1)
                dve.wait_ge(s["qss_done"], 2 * b + 2)
                v.tensor_scalar(qmx[:], zb[:, 0:S], 1e-24, None, ALU.max).then_inc(s["qmax_ready"], 1)
                dve.wait_ge(s["ksqrt_ready"], b + 1)
                v.reciprocal(kin[:], ksr[:]).then_inc(s["p1_dve"], 1)
                dve.wait_ge(s["qsqrt_ready"], b + 1)
                dve.wait_ge(s["qinv_stored"], 16 * b)
                v.reciprocal(qin[:], qsr[:]).then_inc(s["qinv_ready"], 1)
                dve.wait_ge(s["p1_dve"], b + 1)
                for e in range(2):
                    r = slice(DH * e, DH * (e + 1))
                    v.scalar_tensor_tensor(keo[r, b, e], kr[r, :], qk_scale[r, 0:1], kin[r, :], ALU.mult, ALU.mult).then_inc(s["keo_done"], 1)

            dve.wait_ge(s["bias_loaded"], 16 * 8)
            dve.wait_ge(s["null_loaded"], 16 * 3)

            def weigh(b, tail):
                def chunk(c):
                    g, k = divmod(c, 3)
                    dve.wait_ge(s["exp_done"], 6 * b + c + 1)
                    if k < 2:
                        p, w = pb[c][:].rearrange("p (e m i) -> p e m i", e=2, m=2), eb0[:, :, 4 * g + 2 * k:4 * g + 2 * k + 2]
                    else:
                        p, w = pb[c][:].rearrange("p (e m i) -> p e m i", e=2, m=4), eb1[:, :, 4 * g:4 * g + 4]
                    v.tensor_tensor(p, p, w, ALU.mult).then_inc(s["mult_done"], 1)

                chunk(0)
                chunk(1)
                dve.wait_ge(s["px_exp"], b + 1)
                v.tensor_tensor(px[0:2], px[0:2], ebx[:], ALU.mult).then_inc(s["px_ready"], 1)
                for c in range(2, 6):
                    chunk(c)
                if tail:
                    norm_y(b - 1)
                dve.wait_ge(s["z_done"], 2 * b + 2)
                v.tensor_scalar(zmx[:], zb[:, 0:S], 1e-37, None, ALU.max).then_inc(s["zmax_done"], 1)
                dve.wait_ge(s["zmax_done"], b + 1)
                dve.wait_ge(s["zinv_stored"], 16 * b)
                v.reciprocal(zin[:], zmx[:]).then_inc(s["zinv_ready"], 1)

            def norm_y(b):
                dve.wait_ge(s["y_done"], b + 1)
                for t in range(T):
                    last = v.bn_stats(st[:, t], mb[:, S + D * t:S + D * (t + 1)])
                last.then_inc(s["y_parts"], 1)
                dve.wait_ge(s["consts"], 1)
                dve.wait_ge(s["y_parts"], b + 1)
                for t in range(T):
                    last = v.bn_aggr(mv[:, t], st[:, t])
                last.then_inc(s["y_stat"], 1)
                dve.wait_ge(s["y_rstd"], b + 1)
                for t in range(T):
                    last = v.tensor_scalar(yn[:, t], mb[:, S + D * t:S + D * (t + 1)], mv[:, t, 0:1], rs[:, t:t + 1], ALU.subtract, ALU.mult)
                last.then_inc(s["y_norm"], 1)
                dve.wait_ge(s["y_norm"], b + 1)
                v.tensor_tensor(tiles(x2, b), yn[:], row(R_GO)[:, None, :].to_broadcast([P, T, D]), ALU.mult).then_inc(s["x2_done"], 1)

            weigh(0, False)
            with dve.Fori(1, B) as b:
                weigh(b, True)
            norm_y(B - 1)

            def square_sum(b, stat, own, k, base):
                v.tensor_tensor(yn[:], tiles(x2, b), tiles(x2, b), ALU.mult).then_inc(own, 1)
                dve.wait_ge(own, base + k)
                v.tensor_reduce(mv[:, :, 1:2], yn[:], AX.X, ALU.add).then_inc(stat, 1)

            dve.wait_ge(s["x2_done"], B)
            with dve.Fori(0, B) as b:
                square_sum(b, s["r_stat"], s["p3_dve"], 1, 4 * b)
                dve.wait_ge(s["r_rstd"], b + 1)
                dve.wait_ge(s["h2_turned"], b)
                v.tensor_tensor(xc[:], tiles(x2, b), rs[:, :, None].to_broadcast([P, T, D]), ALU.mult).then_inc(s["h2_ready"], 1)
                dve.wait_ge(s["h2_turned"], b + 1)
                dve.wait_ge(s["qkv_done"], b)
                v.tensor_scalar(hT2[:], mb[:, 0:S], cols[:, C_N1:C_N1 + 1], D ** 0.5, ALU.mult, ALU.mult).then_inc(s["hT2_ready"], 1)
                dve.wait_ge(s["sq2_ready"], b + 1)
                v.tensor_reduce(s64[:], sq2[:].rearrange("p t (h d) -> p t h d", d=HD), AX.X, ALU.add).then_inc(s["p3_dve"], 1)
                dve.wait_ge(s["p3_dve"], 4 * b + 2)
                v.tensor_scalar(v64[:], s64[:], 1.0 / HD, EPS, ALU.mult, ALU.add).then_inc(s["s64_ready"], 1)
                dve.wait_ge(s["r64_ready"], b + 1)
                v.reciprocal(i64[:], r64[:]).then_inc(s["p3_dve"], 1)
                dve.wait_ge(s["p3_dve"], 4 * b + 3)
                dve.wait_ge(s["v2_done"], b + 1)
                dve.wait_ge(s["qk_turned"], b)
                for t in range(T):
                    last = v.tensor_tensor(qkn[:, t].rearrange("p (h d) -> p h d", d=HD),
                                           sc[:, 512 * t:512 * t + 2 * D].rearrange("p (h d) -> p h d", d=HD),
                                           i64[:, t, :, None].to_broadcast([P, 2 * H, HD]), ALU.mult)
                last.then_inc(s["qkn_ready"], 1)
                dve.wait_ge(s["qk_turned"], b + 1)
                dve.wait_ge(s["qt2_done"], b + 1)
                v.tensor_scalar(kt2[:, b], oa[:, S:2 * S], qk2_scale[:, 0:1], None, ALU.mult).then_inc(s["kt2_done"], 1)
                v.tensor_copy(s64[:, 0, 0:1], i64[:, 0, 0:1]).then_inc(s["p3_dve"], 1)

            for_ones = v.memset(v2f[:, :, :, HD:HD + 1], 1.0)
            for_ones.then_inc(s["p4_dve"], 1)

            def masked_queries(b):
                dve.wait_ge(s["qt2_done"], B)
                for g in range(2):
                    dve.wait_ge(s["qk2_chunk"], 6 * b)
                    for k in range(M):
                        last = v.tensor_scalar(qm[:, g, k], qt2[:, b], head_of[:, M * g + k:M * g + k + 1], None, ALU.mult)
                    last.then_inc(s["qm_ready"], 1)

            def weigh2(b, tail):
                masked_queries(b)
                if tail:
                    project(b - 1)

            def project(b):
                dve.wait_ge(s["o2_turned"], b + 1)
                view = tm[:].rearrange("p (n r k) -> p n r k", n=2 * 4, r=4)
                v.reciprocal(rz2[:], view[:, :, :, HD:HD + 1]).then_inc(s["p4_dve"], 1)
                dve.wait_ge(s["p4_dve"], b + 2)
                v.tensor_tensor(ao[:].rearrange("p t (g r d) -> p (t g) r d", g=4, r=4), view[:, :, :, 0:HD],
                                rz2[:].to_broadcast([P, 2 * 4, 4, HD]), ALU.mult).then_inc(s["ao_ready"], 1)
                dve.wait_ge(s["wo_done"], b + 1)
                v.tensor_tensor(tiles(x2, b)[:, :, OFF:D], tiles(x2, b)[:, :, OFF:D],
                                halves(tm[:, 512:512 + T * DN], T), ALU.add).then_inc(s["x3_done"], 1)

            weigh2(0, False)
            with dve.Fori(1, B) as b:
                weigh2(b, True)
            project(B - 1)

            dve.wait_ge(s["x3_done"], B)
            with dve.Fori(0, B) as b:
                square_sum(b, s["f_stat"], s["p5_dve"], 1, b)
                dve.wait_ge(s["f_rstd"], b + 1)
                dve.wait_ge(s["f_turned"], b)
                v.tensor_tensor(xc[:], tiles(x2, b), rs[:, :, None].to_broadcast([P, T, D]), ALU.mult).then_inc(s["f_ready"], 1)
                dve.wait_ge(s["f_turned"], b + 1)
                dve.wait_ge(s["gate_done"], b)
                dve.wait_ge(s["xfT_ready"], b)
                v.tensor_scalar(xf1[:], mb[:, 0:S], cols[:, C_N2:C_N2 + 1], D ** 0.5, ALU.mult, ALU.mult).then_inc(s["xf1_ready"], 1)
                dve.wait_ge(s["gate_done"], b + 1)
                v.tensor_copy(tiles(lg, b), halves(zb[:, 0:T * E], T)).then_inc(s["lg_ready"], 1)

            m = [0]

            def gate(ins):
                m[0] += 1
                ins.then_inc(s["gates"], 1)
                dve.wait_ge(s["gates"], m[0])

            NT = B * T
            dve.wait_ge(s["lg_ready"], B)
            clean, num, prob, sel, wts, isn = ga
            gate(v.tensor_scalar(num[:], lg[:], 3.4028235e38, -3.4028235e38, ALU.min, ALU.max))
            gate(v.tensor_tensor(isn[:].bitcast(mybir.dt.int32), lg[:], lg[:], ALU.is_equal))
            gate(v.memset(clean[:], 0.0))
            gate(v.copy_predicated(clean[:], isn[:].bitcast(mybir.dt.int32), num[:]))
            gate(v.tensor_reduce(g1[0][:], clean[:], AX.X, ALU.max))
            gate(v.tensor_tensor(num[:], clean[:], g1[0][:, :, None].to_broadcast([P, NT, E]), ALU.subtract))
            gate(v.tensor_copy(lg[:], num[:]))
            dve.wait_ge(s["gate_exp"], 1)
            gate(v.tensor_reduce(g1[1][:], prob[:], AX.X, ALU.add))
            gate(v.reciprocal(g1[2][:], g1[1][:]))
            gate(v.tensor_tensor(sel[:], prob[:], g1[2][:, :, None].to_broadcast([P, NT, E]), ALU.mult))
            mine = sel[:, :, :, None].to_broadcast([P, NT, E, E])
            other = sel[:, :, None, :].to_broadcast([P, NT, E, E])
            before = tri[:, None, :, :].to_broadcast([P, NT, E, E])
            gate(v.tensor_tensor(gc[0][:], other, mine, ALU.is_gt))
            gate(v.tensor_tensor(gc[1][:], other, mine, ALU.is_equal))
            gate(v.tensor_tensor(gc[2][:], gc[1][:], before, ALU.mult))
            gate(v.tensor_tensor(gc[1][:], gc[0][:], gc[2][:], ALU.add))
            gate(v.tensor_reduce(num[:], gc[1][:], AX.X, ALU.add))
            gate(v.scalar_tensor_tensor(clean[:], num[:], 2.0, sel[:], ALU.is_lt, ALU.mult))
            gate(v.tensor_reduce(g1[0][:], clean[:], AX.X, ALU.add))
            gate(v.tensor_scalar(g1[1][:], g1[0][:], 1e-8, None, ALU.add))
            gate(v.reciprocal(g1[2][:], g1[1][:]))
            gate(v.tensor_tensor(wts[:], clean[:], g1[2][:, :, None].to_broadcast([P, NT, E]), ALU.mult))
            gate(v.tensor_scalar(wts[:, :, 1:2], wts[:, :, 1:2], 0.5, None, ALU.mult))

            dve.wait_ge(s["xs_ready"], 1)
            with dve.Fori(0, B) as b:
                dve.wait_ge(s["u_act"], 7 * b + 5)
                v.scalar_tensor_tensor(si1, th1, 1.0, halves(sc[:, 0:512], 2), ALU.add, ALU.mult).then_inc(s["silu_a"], 1)
                dve.wait_ge(s["silu_a"], b + 1)
                dve.wait_ge(s["u_done"], 8 * b + 6)
                dve.wait_ge(s["down_done"], 2 * b)
                v.tensor_tensor(h1, si1, halves(sc[:, 512:1024], 2), ALU.mult).then_inc(s["h1_ready"], 1)
                for t in range(T):
                    dve.wait_ge(s["down_done"], 2 * b + t + 1)
                    for i in range(E):
                        dst = x[:, T * b + t, OFF:D]
                        v.scalar_tensor_tensor(dst, oa[:, 512 * t + DN * i:512 * t + DN * (i + 1)],
                                               wts[:, T * b + t, i:i + 1], dst, ALU.mult, ALU.add).then_inc(s["res_part"], 1)
                        dve.wait_ge(s["res_part"], 8 * b + 4 * t + i + 1)
                v.tensor_copy(g1[3][:, 0:1], g1[0][:, 0:1]).then_inc(s["res_done"], 1)

        @block.tensor
        def _(pe):
            mm, turn = nc.tensor.matmul, nc.tensor.transpose
            pe.wait_ge(s["consts"], 1)
            for layer in range(2):
                pe.wait_ge(s["bias_turn_in"], layer + 1)
                for t in range(T):
                    last = turn(mb[:, D * t:D * (t + 1)], hb[:, t], ident[:])
                last.then_inc(s["bias_turned"], 1)
                pe.wait_ge(s["bias_hT"], layer + 1)
                pe.wait_ge(s["ld_wa"], 16)
                if layer == 0:
                    for t in range(T):
                        last = mm(zb[:, D * t:D * (t + 1)], hT[:, P * t:P * (t + 1)], wa[:, A_W1:A_W1 + D], start=True, stop=True)
                    last.then_inc(s["bias_mm1"], 1)
                else:
                    mm(zb[0:H, 0:S], wa[:, A_W2:A_W2 + H], hT[:], start=True, stop=True).then_inc(s["bias_mm2"], 1)
            pe.wait_ge(s["table_ready"], 1)
            pe.wait_ge(s["ld_rows"], 16)

            with pe.Fori(0, B) as b:
                pe.wait_ge(s["xc_ready"], b + 1)
                for t in range(T):
                    last = turn(mb[:, D * t:D * (t + 1)], xc[:, t], ident[:])
                last.then_inc(s["xt_done"], 1)
                pe.wait_ge(s["xb_ready"], b + 1)
                pe.wait_ge(s["keo_done"], 2 * b)
                mm(oa[:, 0:KEYS], wa[:, A_KK:A_KK + P], xk[:], start=True, stop=True).then_inc(s["k_proj"], 1)
                wv = wa[:, A_V:A_V + DH]
                mm(oa[:, 512:512 + DH], xk[:, 0:P], wv, start=True, stop=False)
                mm(oa[:, 512:512 + DH], last_row[:], rows[0:1, R_NV:R_NV + DH], start=False, stop=True)
                mm(oa[:, 512 + DH:512 + 2 * DH], xk[:, P:2 * P], wv, start=True, stop=True)
                mm(oa[0:2, 512 + 2 * DH:512 + 3 * DH], xk[:, S - 1:KEYS], wv, start=True, stop=True).then_inc(s["v_proj"], 1)
                for g in range(2):
                    pe.wait_ge(s["q_raw"], 2 * b + g)
                    for m in range(4 * g, 4 * g + 4):
                        last = mm(sc[:, S * m:S * (m + 1)], wa[:, A_Q + P * m:A_Q + P * (m + 1)], xb[:], start=True, stop=True)
                    last.then_inc(s["q_proj"], 1)
                pe.wait_ge(s["ksq_ready"], b + 1)
                mm(oa[:, 0:KEYS], half_ones[:], ksq[:], start=True, stop=True).then_inc(s["kss_done"], 1)
                for g in range(2):
                    pe.wait_ge(s["qsq_ready"], 2 * b + g + 1)
                    for r in range(4):
                        last = mm(zb[32 * r:32 * (r + 1), 0:S], pair_rows[:, g], qsq[:, 4 * g + r], start=(g == 0), stop=(g == 1))
                    last.then_inc(s["qss_done"], 1)

            def scores(b, c):
                g, k = divmod(c, 3)
                if not (isinstance(b, int) and 6 * b + c < 2):
                    pe.wait_ge(s["exp_done"], 6 * b + c - 1)
                for e in range(2):
                    if k < 2:
                        m0 = 4 * g + 2 * k
                        lhs, rhs = kf[:, e, 0:P], qt[:, b, m0:m0 + 2]
                    else:
                        lhs, rhs = kf[:, e, P:2 * P], qt[:, b, 4 * g:4 * g + 4, P:S]
                    out = sc[:, 1024 * (c % 2) + 512 * e:1024 * (c % 2) + 512 * (e + 1)]
                    last = mm(out.rearrange("p (m i) -> p m i", m=rhs.shape[1]), lhs, rhs, start=True, stop=True)
                last.then_inc(s["qk_chunk"], 1)

            def extra_scores(b):
                if not isinstance(b, int):
                    pe.wait_ge(s["y_norm"], b - 1)
                for e in range(2):
                    last = mm(mb[0:2, 16 * e:16 * (e + 1)].rearrange("p (m q) -> p m q", q=2), kf[:, e, S - 1:KEYS],
                              qt[:, b, :, P - 1:S:P], start=True, stop=True)
                last.then_inc(s["qk_x"], 1)

            def values(b, g):
                pe.wait_ge(s["mult_done"], 6 * b + 3 * g + 3)
                pe.wait_ge(s["px_ready"], b + 1)
                pe.wait_ge(s["vf_ready"], b + 1)
                pe.wait_ge(s["o_evac"], 2 * b + g)
                late = pb[3 * g + 2][:].rearrange("p (e m i) -> p e m i", e=2, m=4)
                for k in range(2):
                    for part in range(3):
                        for e in range(2):
                            out = oa[DH * e:DH * (e + 1), 512 * k:512 * (k + 1)]
                            by_pair = out.rearrange("p (m i) -> p m i", m=2)
                            if part == 0:
                                rhs = pb[3 * g + k][:, 512 * e:512 * (e + 1)]
                            elif part == 1:
                                out, rhs = by_pair[:, :, P:S], late[:, e, 2 * k:2 * k + 2]
                            else:
                                out, rhs = by_pair[:, :, P - 1:S:P], px[:, e, 4 * g + 2 * k:4 * g + 2 * k + 2]
                            last = mm(out, vf[:, part], rhs, start=(part == 0), stop=(part == 2))
                last.then_inc(s["pv_done"], 1)

            def sums(b, g):
                if g == 0:
                    pe.wait_ge(s["zmax_done"], b)
                late = pb[3 * g + 2][:].rearrange("p (e m i) -> p e m i", e=2, m=4)
                for e in range(2):
                    for part in range(3):
                        for r in range(4):
                            out = zb[32 * r:32 * (r + 1), 0:S]
                            if part == 0:
                                rhs = pb[3 * g + r // 2][:, 512 * e + S * (r % 2):512 * e + S * (r % 2 + 1)]
                            elif part == 1:
                                out, rhs = out[:, P:S], late[:, e, r]
                            else:
                                out, rhs = out[:, P - 1:S:P], px[:, e, 4 * g + r]
                            last = mm(out, ocm[:, part, 2 * g + e], rhs, start=(g == 0 and e == 0 and part == 0),
                                      stop=(g == 1 and e == 1 and part == 2), skip_group_check=True)
                last.then_inc(s["z_done"], 1)

            def out_product(b):
                pe.wait_ge(s["on_ready"], b + 1)
                for t in range(T):
                    for m in range(M):
                        last = mm(mb[:, S + D * t:S + D * (t + 1)], on[:, m, P * t:P * (t + 1)],
                                  wa[:, A_O + D * m:A_O + D * (m + 1)], start=(m == 0), stop=(m == M - 1))
                last.then_inc(s["y_done"], 1)

            def attend(b, tail):
                pe.wait_ge(s["kf_ready"], b + 1)
                scores(b, 0)
                scores(b, 1)
                extra_scores(b)
                scores(b, 2)
                scores(b, 3)
                values(b, 0)
                sums(b, 0)
                scores(b, 4)
                scores(b, 5)
                if tail:
                    out_product(b - 1)
                values(b, 1)
                sums(b, 1)

            pe.wait_ge(s["q_done"], B)
            attend(0, False)
            with pe.Fori(1, B) as b:
                attend(b, True)
            pe.wait_ge(s["y_norm"], B - 1)
            out_product(B - 1)

            pe.wait_ge(s["ld_wb"], 16)
            with pe.Fori(0, B) as b:
                pe.wait_ge(s["h2_ready"], b + 1)
                for t in range(T):
                    last = turn(mb[:, D * t:D * (t + 1)], xc[:, t], ident[:])
                last.then_inc(s["h2_turned"], 1)
                pe.wait_ge(s["hT2_ready"], b + 1)
                pe.wait_ge(s["qkn_ready"], b)
                for t in range(T):
                    last = mm(sc[:, 512 * t:512 * t + 3 * D], hT2[:, P * t:P * (t + 1)], wb[:, W_QKV:W_QKV + 3 * D], start=True, stop=True)
                last.then_inc(s["qkv_done"], 1)
                pe.wait_ge(s["qkn_ready"], b + 1)
                pe.wait_ge(s["kt2_done"], b)
                for which in range(2):
                    for t in range(T):
                        last = turn(oa[:, S * which + P * t:S * which + P * (t + 1)], qkn[:, t, D * which:D * (which + 1)], ident[:])
                last.then_inc(s["qk_turned"], 1)

            def scores2(b, c):
                g, k = divmod(c, 3)
                if not (isinstance(b, int) and 6 * b + c < 2):
                    pe.wait_ge(s["exp2_done"], 6 * b + c - 1)
                for j in range(2):
                    if k < 2:
                        lhs, rhs = k2f[:, 0:P], qm[:, g, 4 * k + 2 * j:4 * k + 2 * j + 2]
                    else:
                        lhs, rhs = k2f[:, P:S], qm[:, g, 4 * j:4 * j + 4, P:S]
                    out = sc[:, 1024 * (c % 2) + 512 * j:1024 * (c % 2) + 512 * (j + 1)]
                    last = mm(out.rearrange("p (m i) -> p m i", m=rhs.shape[1]), lhs, rhs, start=True, stop=True)
                last.then_inc(s["qk2_chunk"], 1)

            def values2(b, g):
                pe.wait_ge(s["masked"], 6 * b + 3 * g + 3)
                pe.wait_ge(s["v2f_ready"], b + 1)
                pe.wait_ge(s["p4_dve"], 1)
                pe.wait_ge(s["o2_evac"], 2 * b)
                for k in range(2):
                    for part in range(2):
                        for r in range(4):
                            out = oa[32 * r:32 * (r + 1), 512 * g + S * k:512 * g + S * (k + 1)]
                            if part == 0:
                                rhs = pb[3 * g + k][:, S * r:S * (r + 1)]
                            else:
                                out, rhs = out[:, P:S], pb[3 * g + 2][:, P * (4 * k + r):P * (4 * k + r + 1)]
                            last = mm(out, v2f[:, part, 8 * g + 4 * k + r], rhs, start=(k == 0 and part == 0), stop=(part == 1),
                                      skip_group_check=True)
                last.then_inc(s["pv2_done"], 1)

            def turn_outputs(b):
                pe.wait_ge(s["o2_evac"], 2 * (b + 1))
                if not (isinstance(b, int) and b == 0):
                    pe.wait_ge(s["x3_done"], b)
                for t in range(T):
                    for k in range(4):
                        last = turn(tm[:, 512 * t + P * k:512 * t + P * (k + 1)], o2s[:, k // 2, S * (k % 2) + P * t:S * (k % 2) + P * (t + 1)], ident[:])
                last.then_inc(s["o2_turned"], 1)

            def turn_back(b):
                pe.wait_ge(s["ao_ready"], b + 1)
                for t in range(T):
                    last = turn(tm[:, P * t:P * (t + 1)], ao[:, t], ident[:])
                last.then_inc(s["ao_turned"], 1)

            def out_product2(b):
                pe.wait_ge(s["aoT_ready"], b + 1)
                for t in range(T):
                    last = mm(tm[:, 512 + DN * t:512 + DN * (t + 1)], aoT[:, P * t:P * (t + 1)], wb[:, W_O:W_O + DN], start=True, stop=True)
                last.then_inc(s["wo_done"], 1)

            def attend2(b, tail):
                pe.wait_ge(s["k2f_ready"], b + 1)
                pe.wait_ge(s["qm_ready"], 2 * b + 1)
                scores2(b, 0)
                if tail:
                    turn_outputs(b - 1)
                scores2(b, 1)
                scores2(b, 2)
                if tail:
                    turn_back(b - 1)
                pe.wait_ge(s["qm_ready"], 2 * b + 2)
                scores2(b, 3)
                if tail:
                    out_product2(b - 1)
                values2(b, 0)
                scores2(b, 4)
                scores2(b, 5)
                values2(b, 1)

            attend2(0, False)
            with pe.Fori(1, B) as b:
                attend2(b, True)
            turn_outputs(B - 1)
            turn_back(B - 1)
            out_product2(B - 1)

            with pe.Fori(0, B) as b:
                pe.wait_ge(s["f_ready"], b + 1)
                for t in range(T):
                    last = turn(mb[:, D * t:D * (t + 1)], xc[:, t], ident[:])
                last.then_inc(s["f_turned"], 1)
                pe.wait_ge(s["xf1_ready"], b + 1)
                pe.wait_ge(s["lg_ready"], b)
                for t in range(T):
                    last = mm(zb[:, E * t:E * (t + 1)], xf1[:, P * t:P * (t + 1)], wb[:, W_G:W_G + E], start=True, stop=True)
                last.then_inc(s["gate_done"], 1)

            pe.wait_ge(s["xfT_ready"], B)
            with pe.Fori(0, B) as b:
                def layer(n, w, src, outs=2):
                    chunks = len(src)
                    for o in range(outs):
                        for i, part in enumerate(src):
                            last = mm(sc[:, 512 * (n % 4) + S * o:512 * (n % 4) + S * (o + 1)],
                                      wb[:, w + HID * i + P * o:w + HID * i + P * (o + 1)], part, start=(i == 0), stop=(i == chunks - 1))
                    last.then_inc(s["u_done"], 1)

                xin = [xfT[:, b]]
                pe.wait_ge(s["silu_a"], b)
                layer(0, W_L1, xin)
                pe.wait_ge(s["h1_ready"], b)
                layer(1, W_D3, xin, 1)
                pe.wait_ge(s["u_act"], 7 * b)
                layer(2, W_E0, xin)
                pe.wait_ge(s["u_act"], 7 * b + 1)
                layer(3, W_L2, [h2a[:, 0], h2a[:, 1]])
                layer(4, W_E11, xin)
                pe.wait_ge(s["u_act"], 7 * b + 2)
                layer(5, W_E12, xin)
                pe.wait_ge(s["u_act"], 7 * b + 3)
                layer(6, W_U3, [h3a])
                pe.wait_ge(s["u_act"], 7 * b + 4)
                layer(7, W_L3, [h2b[:, 0], h2b[:, 1]])
                pe.wait_ge(s["h1_ready"], b + 1)
                pe.wait_ge(s["u_act"], 7 * b + 7)
                pe.wait_ge(s["res_done"], b)
                for t in range(T):
                    for i, h in enumerate((h0, h1, h2c, h3b)):
                        for k in range(2):
                            w = W_DN + (2 * i + k) * DN
                            last = mm(oa[:, 512 * t + DN * i:512 * t + DN * (i + 1)], h[:, k, P * t:P * (t + 1)], wb[:, w:w + DN],
                                      start=(k == 0), stop=(k == 1))
                    last.then_inc(s["down_done"], 1)


def kernel(**a):
    import numpy as np
    from concourse import bacc
    from concourse.bass_utils import run_bass_kernel_spmd

    a = {k: np.asarray(v) for k, v in a.items()}
    c = {k[len("L0_cond_"):]: v for k, v in a.items() if k.startswith("L0_cond_")}
    f = {k[len("L0_ffn_"):]: v for k, v in a.items() if k.startswith("L0_ffn_")}
    cond = a["cond_64"]

    def chunks(w):
        return np.concatenate([w[i:i + P] for i in range(0, w.shape[0], P)], axis=1)

    cols = np.stack([c["g_norm"], f["n1_w"], f["n2_w"], np.tile(c["q_scale"], 2), np.tile(c["k_scale"], 2),
                     np.tile(cond[0], 2), np.tile(f["qn_w"], H), np.tile(f["kn_w"], H)], axis=1)
    rows = np.concatenate([c["g_out"], c["w0"][0], c["b0"], c["g0"], c["b1"], c["g1"], c["q_scale"], c["k_scale"],
                           cond[1], f["qn_w"], f["kn_w"]])[None]
    wk = c["Wkv"][:, :DH]
    wa = np.concatenate([wk, wk, c["Wkv"][:, DH:], c["w1"], c["w2"], c["Wq"], chunks(c["Wout"])], axis=1)
    downs = [chunks(f[n][OFF:].T) for n in ("e0_down", "e1_down", "e2_l4", "e3_out")]
    wb = np.concatenate([f["wq"].T, f["wk"].T, f["wv"].T, f["wo"][OFF:].T, f["gate_w"].T, f["e0_up"].T, f["e1_w1"].T,
                         f["e1_w2"].T, f["e2_l1"].T, chunks(f["e2_l2"].T), chunks(f["e2_l3"].T), f["e3_down"].T,
                         f["e3_up"].T] + downs, axis=1)
    assert wa.shape[1] == A_ALL and wb.shape[1] == W_ALL and rows.shape[1] == R_ALL
    told = a["mask_BxS_bf1"]
    mask = np.zeros((P, B, 3), told.dtype)
    mask[P - 1, :, 0] = True
    mask[:P - 1, :, 0] = told[:, P - 2::-1].T
    mask[:, :, 1] = told[:, S - 2:P - 2:-1].T
    mask[:2, :, 2] = told[:, P - 1::P].T
    arrays = {"x": a["x"].reshape(B * S, D), "cols": cols, "rows": rows, "small": np.stack([c["b2"], c["null_attn_bias"]], axis=1),
              "mask": mask, "wa": wa, "wb": wb}
    arrays = {f"in_{k}": np.ascontiguousarray(v) for k, v in arrays.items()}

    nc = bacc.Bacc("TRN2", target_bir_lowering=False, num_devices=1)
    ins = [nc.dram_tensor(k, v.shape, mybir.dt.from_np(v.dtype), kind="ExternalInput").ap() for k, v in arrays.items()]
    out = nc.dram_tensor("out", (B * S, D), F32, kind="ExternalOutput").ap()
    adaln_ffn(nc, *ins, out)
    r = run_bass_kernel_spmd(nc, [arrays], core_ids=[0])
    return r.results[0]["out"].reshape(B, S, D)
```

```python
from contextlib import ExitStack

import concourse.bass as bass
from concourse import mybir

F32 = mybir.dt.float32
U8 = mybir.dt.uint8
ALU = mybir.AluOpType
ACT = mybir.ActivationFunctionType
AX = mybir.AxisListType

P = 128
B, S, D = 4, 256, 128
T = S // P
H, DH = 16, 64
M = H // 2
HD = D // H
HID = 256
E = 4
OFF = 32
DN = D - OFF
KEYS = S + 1
GT = 3 * P
EPS = 1.1920929e-07
ROOM = 60.0

C_GN, C_N1, C_N2, C_QS, C_KS, C_NK, C_QN, C_KN = range(8)
R_GO, R_W0, R_B0, R_G0, R_B1, R_G1 = (D * i for i in range(6))
R_QS, R_KS, R_NV = (6 * D + DH * i for i in range(3))
R_QN, R_KN = 6 * D + 3 * DH, 6 * D + 3 * DH + HD
R_ALL = R_KN + HD
A_KK, A_V, A_W1, A_W2 = 0, P, P + DH, 2 * P + DH
A_Q = A_W2 + H
A_O = A_Q + H * DH
A_ALL = A_O + M * D
W_QKV = 0
W_O = W_QKV + 3 * D
W_G = W_O + DN
W_E0 = W_G + E
W_E11 = W_E0 + HID
W_E12 = W_E11 + HID
W_L1 = W_E12 + HID
W_L2 = W_L1 + HID
W_L3 = W_L2 + 2 * HID
W_D3 = W_L3 + 2 * HID
W_U3 = W_D3 + D
W_DN = W_U3 + HID
W_ALL = W_DN + E * 2 * DN


def adaln_ffn(nc, x_d, cols_d, rows_d, small_d, mask_d, wa_d, wb_d, out_d):
    with ExitStack() as ctx:
        def sb(name, shape, dt=F32):
            return ctx.enter_context(nc.sbuf_tensor(name, shape, dt))

        def ps(name, shape):
            return ctx.enter_context(nc.psum_tensor(name, shape, F32))

        def sem(name):
            return ctx.enter_context(nc.semaphore(name))

        table_d = nc.dram_tensor("bias_table", (H, GT), F32, kind="Internal").ap()
        qinv_d = nc.dram_tensor("q_inverse_norms", (B, P, S), F32, kind="Internal").ap()
        null_d = nc.dram_tensor("null_weights", (H, S), F32, kind="Internal").ap()
        zinv_d = nc.dram_tensor("softmax_inverse_sums", (B, P, S), F32, kind="Internal").ap()

        x = sb("x", [P, B * T, D])
        cols = sb("cols", [P, 8])
        rows = sb("rows", [P, R_ALL])
        small = sb("small", [H, 2])
        mask_u8 = sb("mask_u8", [P, B, 3], U8)
        mask = sb("mask", [P, B, 3])
        wa = sb("wa", [P, A_ALL])
        wb = sb("wb", [P, W_ALL])
        ident = sb("ident", [P, P])
        half_ones = sb("half_ones", [P, P])
        pair_rows = sb("pair_rows", [P, 2, 32])
        sum_rows = sb("sum_rows", [P, 4, 32])
        causal = sb("causal", [P, P])
        head_of = sb("head_of", [P, H])
        minus_half = sb("minus_half", [P, B * T])
        ln_eps = sb("ln_eps", [P, B * T])
        rms_eps = sb("rms_eps", [P, 4])
        zeros = sb("zeros", [P, S])
        shift1 = sb("shift1", [P, 4])
        shift2 = sb("shift2", [P, 4])
        qk_scale = sb("qk_scale", [P, 1])
        qk2_scale = sb("qk2_scale", [P, 1])
        pos = sb("pos", [P, T])
        hb = sb("hb", [P, T, D])
        ht = sb("ht", [P, T, D])
        hT = sb("hT", [P, S])
        bst = sb("bst", [P, T, 6])
        bmv = sb("bmv", [P, T, 2])
        bve = sb("bve", [P, T])
        brs = sb("brs", [P, T])
        top = sb("top", [H, 4])
        table = sb("table", [H, GT])
        null_row = sb("null_row", [H, S])
        eb0 = sb("eb0", [P, 2, M, S])
        eb1 = sb("eb1", [P, 2, M, P])
        ebx = sb("ebx", [2, 2, M, 2])
        st_x = sb("st_x", [P, B * T, 6])
        mv_x = sb("mv_x", [P, B * T, 2])
        ve_x = sb("ve_x", [P, B * T])
        rs_x = sb("rs_x", [P, B * T])
        st = sb("st", [P, T, 6])
        mv = sb("mv", [P, T, 2])
        ve = sb("ve", [P, T])
        rs = sb("rs", [P, T])
        xc = sb("xc", [P, B * T, D])
        last_row = sb("last_row", [1, P])
        kr = sb("kr", [P, KEYS])
        ksq = sb("ksq", [P, KEYS])
        kmx = sb("kmx", [P, KEYS])
        ksr = sb("ksr", [P, KEYS])
        kin = sb("kin", [P, KEYS])
        keo = sb("keo", [P, B, 2, KEYS])
        qt = sb("qt", [P, B, M, S])
        qmx = sb("qmx", [P, S])
        qsr = sb("qsr", [P, S])
        spread = sb("spread", [P, M, S])
        vn = sb("vn", [P, B, 3, DH])
        kf = sb("kf", [P, 2, KEYS])
        vf = sb("vf", [P, 3, DH])
        ocm = sb("ocm", [P, 3, 4, 32])
        probs = sb("probs", [P, 6, 1024])
        pb = [probs[:, i] for i in range(6)]
        px = sb("px", [P, 2, M, 2])
        o_raw = sb("o_raw", [P, M, S])
        qsq = o_raw[:]
        on = sb("on", [P, M, S])
        xb = on[:, 0:B, :]
        xk = probs[:, 0:2, :].rearrange("p a c -> p (a c)")[:, 0:B * KEYS].rearrange("p (b j) -> p b j", b=B)
        zmx = sb("zmx", [P, S])
        zin = sb("zin", [P, S])
        yn = sb("yn", [P, T, D])
        x2 = sb("x2", [P, B * T, D])
        qin = x2[:].rearrange("p (b t) d -> p b (t d)", b=B)
        sq_x = sb("sq_x", [P, 4, D])
        sum_sq = sb("sum_sq", [P, 4])
        ve_rms = sb("ve_rms", [P, 4])
        rs_rms = sb("rs_rms", [P, 4])
        hT2 = sb("hT2", [P, 4 * D])
        s64 = sb("s64", [P, 4, 2 * H])
        v64 = sb("v64", [P, 4, 2 * H])
        r64 = sb("r64", [P, 4, 2 * H])
        i64 = sb("i64", [P, 4, 2 * H])
        keys_space = keo[:].rearrange("p b e j -> p (b e j)")
        sq2 = keys_space[:, 0:4 * 2 * D].rearrange("p (t c) -> p t c", t=4)
        qkn = keys_space[:, 4 * 2 * D:8 * 2 * D].rearrange("p (t c) -> p t c", t=4)
        v2 = sb("v2", [P, B, T, H, HD])
        k2f = sb("k2f", [P, S])
        v2f = sb("v2f", [P, T, H, 32])
        o2s = sb("o2s", [P, 2, 512])
        rz2 = sb("rz2", [P, T * 4, 4, 1])
        ao = sb("ao", [P, T, D])
        aoT = sb("aoT", [P, S])
        lg = sb("lg", [P, B * T, E])
        ga = [sb(f"ga{i}", [P, B * T, E]) for i in range(6)]
        g1 = [sb(f"g1_{i}", [P, B * T]) for i in range(4)]
        gc = [sb(f"gc{i}", [P, B * T, E, E]) for i in range(3)]
        tri = sb("tri", [P, E, E])
        qm = qt[:, 0:2, :, :]
        xfT = qt[:, 2, 0:4, :]
        qt2 = qt[:, 2, 4:8, :]
        kt2 = qt[:, 3, 0:4, :]
        h0 = o_raw[:, 0:2, :]
        h1 = o_raw[:, 2:4, :]
        h2a = o_raw[:, 4:6, :]
        h2b = o_raw[:, 6:8, :]
        h2c = on[:, 0:2, :]
        h3a = on[:, 2, :]
        h3b = on[:, 3:5, :]
        th1 = on[:, 5:7, :]
        si1 = spread[:, 0:2, :]

        sc = ps("sc", [P, 2048])
        oa = ps("oa", [P, 1024])
        tm = ps("tm", [P, 1024])
        zb = tm[:, 0:512]
        mb = tm[:, 512:1024]

        names = """ld_x ld_cols ld_rows ld_small ld_mask ld_wa ld_wb
            consts zeroed mask_ready shifts pos_ready
            bias_dve bias_pool bias_var bias_rstd bias_tanh_in bias_tanh bias_turn_in bias_turned bias_hT bias_mm1 bias_mm2
            bias_top table_ready null_ready table_stored bias_loaded
            x_parts x_stat x_var x_rstd xc_ready xt_done xb_ready k_proj v_proj q_proj kr_ready ksq_ready kss_done
            q_raw qsq_ready qss_done kmax_ready ksqrt_ready qmax_ready qsqrt_ready qinv_ready qinv_stored
            qinv_spread q_done keo_done vn_done kin_ready
            kf_ready vf_ready ocm_ready qk_chunk qk_x exp_done px_exp px_ready mult_done pv_done z_done o_evac
            zmax_done zinv_ready zinv_stored zinv_spread on_ready y_done y_parts y_stat y_var y_rstd y_norm x2_done
            r_stat r_var r_rstd h2_ready h2_turned hT2_ready qkv_done sq2_ready s64_ready r64_ready qkn_ready
            v2_done qk_turned qt2_done kt2_done sq_x_ready p3_dve
            k2f_ready v2f_ready qm_ready qk2_chunk exp2_done masked pv2_done o2_evac o2_turned ao_ready ao_turned
            aoT_ready wo_done x3_done p4_dve
            f_stat f_var f_rstd f_ready f_turned xfT_ready gate_done lg_ready gate_w xs_ready gates
            gate_exp res_part u_done u_act silu_a h1_ready down_done res_done stored""".split()
        s = {n: sem(n) for n in names}

        block = ctx.enter_context(nc.Block())


        def spread_from(dram, b, g, e):
            src = dram[b]
            return bass.AP(tensor=src.tensor, offset=src.offset + (2 * g + e) * S, ap=[[0, DH], [32 * S, 4], [1, S]])

        def nulls_in(e):
            return bass.AP(tensor=null_d.tensor, offset=e * S, ap=[[2 * S, 1], [2 * S, M], [1, S]])

        def tiles(a, b):
            return a[:, bass.ds(T * b, T)]

        def quarter(a, h):
            return a[:, 4 * h:4 * (h + 1)]

        def halves(a, n):
            return a.rearrange("p (a c) -> p a c", a=n)

        @block.sync
        def _(sp):
            sp.dma_start(x[:], x_d.rearrange("(n p) d -> p n d", p=P)).then_inc(s["ld_x"], 16)
            sp.dma_start(rows[:], bass.AP(tensor=rows_d.tensor, offset=0, ap=[[0, P], [1, R_ALL]])).then_inc(s["ld_rows"], 16)
            sp.dma_start(cols[:], cols_d).then_inc(s["ld_cols"], 16)
            sp.dma_start(small[:], small_d).then_inc(s["ld_small"], 16)
            sp.dma_start(wa[:], wa_d).then_inc(s["ld_wa"], 16)
            sp.dma_start(mask_u8[:], mask_d).then_inc(s["ld_mask"], 16)
            sp.dma_start(wb[:], wb_d).then_inc(s["ld_wb"], 16)

            sp.wait_ge(s["table_ready"], 1)
            sp.dma_start(table_d, table[:]).then_inc(s["table_stored"], 16)
            sp.wait_ge(s["null_ready"], 1)
            sp.dma_start(null_d, null_row[:]).then_inc(s["table_stored"], 16)
            sp.wait_ge(s["table_stored"], 32)
            for e in range(2):
                base = e * GT + 1
                sp.dma_start(eb0[0:P - 1, e], bass.AP(tensor=table_d.tensor, offset=base,
                                                      ap=[[1, P - 1], [2 * GT, M], [1, S]])).then_inc(s["bias_loaded"], 16)
                sp.dma_start(eb0[P - 1:P, e], nulls_in(e)).then_inc(s["bias_loaded"], 16)
                sp.dma_start(eb1[:, e], bass.AP(tensor=table_d.tensor, offset=base,
                                                ap=[[1, P], [2 * GT, M], [1, P]])).then_inc(s["bias_loaded"], 16)
            sp.wait_ge(s["zeroed"], 1)
            for e in range(2):
                for k in range(2):
                    src = bass.AP(tensor=table_d.tensor, offset=e * GT + P - 1, ap=[[2 * GT, 1], [2 * GT, M], [1, 1]])
                    sp.dma_start(ebx[k:k + 1, e, :, k:k + 1], src, allow_slow_non_contiguous=True).then_inc(s["bias_loaded"], 16)

            with sp.Fori(0, B) as b:
                sp.wait_ge(s["qinv_ready"], b + 1)
                sp.dma_start(qinv_d[b], qin[:, b]).then_inc(s["qinv_stored"], 16)
                sp.wait_ge(s["qinv_stored"], 16 * (b + 1))
                sp.wait_ge(s["q_done"], b)
                for g in range(2):
                    for e in range(2):
                        sp.dma_start(spread[DH * e:DH * (e + 1), 4 * g:4 * g + 4], spread_from(qinv_d, b, g, e)).then_inc(s["qinv_spread"], 16)
            sp.wait_ge(s["q_done"], B)
            with sp.Fori(0, B) as b:
                sp.wait_ge(s["zinv_ready"], b + 1)
                sp.dma_start(zinv_d[b], zin[:]).then_inc(s["zinv_stored"], 16)
                sp.wait_ge(s["zinv_stored"], 16 * (b + 1))
                sp.wait_ge(s["on_ready"], b)
                for g in range(2):
                    for e in range(2):
                        sp.dma_start(spread[DH * e:DH * (e + 1), 4 * g:4 * g + 4], spread_from(zinv_d, b, g, e)).then_inc(s["zinv_spread"], 16)
            with sp.Fori(0, B) as b:
                sp.wait_ge(s["res_done"], b + 1)
                sp.dma_start(out_d.rearrange("(b n p) d -> p b n d", p=P, n=T)[:, b], tiles(x, b)).then_inc(s["stored"], 16)
            sp.wait_ge(s["stored"], 16 * B)


        @block.gpsimd
        def _(pool):
            n = [0]

            def step(ins):
                n[0] += 1
                ins.then_inc(s["zeroed"], 1)
                pool.wait_ge(s["zeroed"], n[0])

            pool.iota(pos[:], pattern=[[P, T]], base=0, channel_multiplier=1,
                      allow_small_or_imprecise_dtypes=True).then_inc(s["pos_ready"], 1)
            for buf, value in ((half_ones, 0.5), (minus_half, -0.5), (ln_eps, 1e-5), (rms_eps, EPS * D), (ident, 0.0), (sum_rows, 0.0),
                               (head_of, 1.0), (causal, 1.0), (xk[:, :, P - 1:P], 0.0), (last_row, 0.0), (px, 0.0), (v2f, 0.0), (keo, 0.0), (tri, 1.0), (vn, 0.0)):
                pool.memset(buf[:], value)
            pool.memset(table[:], 0.0)
            pool.memset(ebx[:], 0.0)
            step(pool.memset(zeros[:], 0.0))
            pool.affine_select(out=ident[:], in_=ident[:], compare_op=ALU.not_equal, fill=1.0, base=0,
                               pattern=[[-1, P]], channel_multiplier=1)
            pool.affine_select(out=causal[:], in_=causal[:], compare_op=ALU.is_ge, fill=0.0, base=0,
                               pattern=[[1, P]], channel_multiplier=-1)
            pool.memset(last_row[:, P - 1:P], 1.0)
            for k in range(4):
                pool.memset(sum_rows[:, k, k:k + 1], 1.0)
            pool.affine_select(out=tri[:], in_=tri[:], compare_op=ALU.is_ge, fill=0.0, base=-1,
                               pattern=[[1, E], [-1, E]], channel_multiplier=0)
            step(pool.affine_select(out=head_of[:], in_=head_of[:], compare_op=ALU.is_ge, fill=0.0, base=0,
                                    pattern=[[-HD, H]], channel_multiplier=1))
            pool.affine_select(out=head_of[:], in_=head_of[:], compare_op=ALU.is_ge, fill=0.0, base=HD - 1,
                               pattern=[[HD, H]], channel_multiplier=-1).then_inc(s["consts"], 1)
            pool.wait_ge(s["consts"], 1)

            def rstd(var, eps, ve_, out, ready, done, count, base):
                pool.wait_ge(ready, base + 1)
                pool.tensor_tensor(ve_, var, eps[:, 0:var.shape[1]], ALU.add).then_inc(count, 1)
                pool.wait_ge(count, base + 1)
                pool.tensor_tensor(out, ve_, minus_half[:, 0:var.shape[1]], ALU.pow).then_inc(done, 1)

            for layer in range(2):
                if layer == 1:
                    rstd(mv_x[:, :, 1], ln_eps, ve_x[:], rs_x[:], s["x_stat"], s["x_rstd"], s["x_var"], 0)
                rstd(bmv[:, :, 1], ln_eps, bve[:], brs[:], s["bias_var"], s["bias_rstd"], s["bias_pool"], layer)

            def queries(b):
                pool.wait_ge(s["qinv_spread"], 64 * (b + 1))
                pool.tensor_tensor(qt[:, b], qt[:, b], spread[:], ALU.mult).then_inc(s["q_done"], 1)


            def operands(b):
                pool.wait_ge(s["keo_done"], 2 * (b + 1))
                pool.wait_ge(s["vn_done"], T)
                pool.wait_ge(s["mask_ready"], 1)
                pool.wait_ge(s["qk_chunk"], 6 * b)
                pool.wait_ge(s["qk_x"], b)
                pool.tensor_copy(kf[:], keo[:, b]).then_inc(s["kf_ready"], 1)
                pool.wait_ge(s["z_done"], 2 * b)
                pool.tensor_copy(vf[:], vn[:, b])
                pool.tensor_tensor(ocm[:], sum_rows[:, None, :, :].to_broadcast([P, 3, 4, 32]),
                                   mask[:, b, :, None, None].to_broadcast([P, 3, 4, 32]), ALU.mult).then_inc(s["vf_ready"], 1)

            def normalised(b):
                pool.wait_ge(s["zinv_spread"], 64 * (b + 1))
                pool.wait_ge(s["o_evac"], 2 * (b + 1))
                pool.wait_ge(s["y_done"], b)
                pool.tensor_tensor(on[:], o_raw[:], spread[:], ALU.mult).then_inc(s["on_ready"], 1)
                rstd(mv[:, :, 1], ln_eps, ve[:], rs[:], s["y_stat"], s["y_rstd"], s["y_var"], b)

            queries(0)
            operands(0)
            with pool.Fori(1, B) as b:
                queries(b)
            with pool.Fori(1, B) as b:
                operands(b)
                normalised(b - 1)

            rstd(sum_sq[:], rms_eps, ve_rms[:], rs_rms[:], s["r_stat"], s["r_rstd"], s["r_var"], 0)
            normalised(B - 1)
            rstd(sum_sq[:], rms_eps, ve_rms[:], rs_rms[:], s["r_stat"], s["r_rstd"], s["r_var"], 1)

            with pool.Fori(0, B) as b:
                pool.wait_ge(s["v2_done"], 2)
                pool.wait_ge(s["kt2_done"], 2)
                pool.wait_ge(s["qk2_chunk"], 6 * b)
                pool.tensor_copy(k2f[:], kt2[:, b]).then_inc(s["k2f_ready"], 1)
                pool.wait_ge(s["pv2_done"], 2 * b)
                pool.tensor_copy(v2f[:, :, :, 0:HD], v2[:, b]).then_inc(s["v2f_ready"], 1)
                for c in range(6):
                    pool.wait_ge(s["exp2_done"], 6 * b + c + 1)
                    heads = 4 if c % 3 < 2 else 8
                    diag = halves(pb[c], heads)[:, :, 0:P]
                    pool.tensor_tensor(diag, diag, causal[:, None, :].to_broadcast([P, heads, P]), ALU.mult).then_inc(s["masked"], 1)

            for h in range(2):
                rstd(sum_sq[:], rms_eps, ve_rms[:], rs_rms[:], s["f_stat"], s["f_rstd"], s["f_var"], h)
                pool.wait_ge(s["x3_done"], 2 * (h + 1))
                pool.tensor_tensor(quarter(x, h), quarter(x, h), quarter(x2, h), ALU.add).then_inc(s["xs_ready"], 1)

        @block.scalar
        def _(act):
            nc_ = nc.scalar
            def bias_tanh(layer):
                act.wait_ge(s["bias_tanh_in"], layer + 1)
                nc_.activation(ht[:], hb[:], ACT.Tanh, scale=0.5).then_inc(s["bias_tanh"], 1)

            def norms(b):
                def queries(g):
                    act.wait_ge(s["q_proj"], 2 * b + g + 1)
                    nc_.activation(qsq[:, 4 * g:4 * g + 4], halves(sc[:, 1024 * g:1024 * (g + 1)], 4), ACT.Square).then_inc(s["qsq_ready"], 1)
                    nc_.copy(qt[:, b, 4 * g:4 * g + 4], halves(sc[:, 1024 * g:1024 * (g + 1)], 4)).then_inc(s["q_raw"], 1)

                nc_.preload_act_table(ACT.Sqrt)
                queries(0)
                act.wait_ge(s["k_proj"], b + 1)
                nc_.activation(ksq[:, 0:P - 1], oa[:, 0:P - 1], ACT.Square)
                nc_.activation(ksq[:, P:KEYS], oa[:, P:KEYS], ACT.Square).then_inc(s["ksq_ready"], 1)
                act.wait_ge(s["keo_done"], 2 * b)
                nc_.copy(kr[:, 0:P - 1], oa[:, 0:P - 1])
                nc_.copy(kr[:, P:KEYS], oa[:, P:KEYS]).then_inc(s["kr_ready"], 1)
                queries(1)
                act.wait_ge(s["kmax_ready"], b + 1)
                nc_.activation(ksr[:], kmx[:], ACT.Sqrt).then_inc(s["ksqrt_ready"], 1)
                act.wait_ge(s["qmax_ready"], b + 1)
                nc_.activation(qsr[:], qmx[:], ACT.Sqrt).then_inc(s["qsqrt_ready"], 1)

            bias_tanh(0)
            act.wait_ge(s["ld_cols"], 16)
            nc_.copy(kr[:, P - 1:P], cols[:, C_NK:C_NK + 1])
            nc_.activation(ksq[:, P - 1:P], cols[:, C_NK:C_NK + 1], ACT.Square)
            bias_tanh(1)
            norms(0)
            act.wait_ge(s["bias_top"], 1)
            nc_.activation(table[:, P - 1:P - 1 + S], mb[0:H, S:2 * S], ACT.Exp, bias=top[:, 3:4]).then_inc(s["table_ready"], 1)
            nc_.activation(null_row[:], zeros[0:H, :], ACT.Exp, bias=top[:, 0:1]).then_inc(s["null_ready"], 1)
            with act.Fori(1, B) as b:
                norms(b)

            act.wait_ge(s["shifts"], 1)
            nc_.preload_act_table(ACT.Exp)

            def exps(b):
                def chunk(c):
                    act.wait_ge(s["qk_chunk"], 6 * b + c + 1)
                    act.wait_ge(s["z_done"], 2 * b)
                    nc_.activation(pb[c], sc[:, 1024 * (c % 2):1024 * (c % 2 + 1)], ACT.Exp,
                                   bias=shift1[:, 3:4]).then_inc(s["exp_done"], 1)

                def evacuate(g):
                    act.wait_ge(s["pv_done"], 2 * b + g + 1)
                    act.wait_ge(s["on_ready"], b)
                    nc_.copy(o_raw[:, 4 * g:4 * g + 4], halves(oa[:], 4)).then_inc(s["o_evac"], 1)

                chunk(0)
                chunk(1)
                act.wait_ge(s["qk_x"], b + 1)
                nc_.activation(px[0:2], mb[0:2, 0:32].rearrange("p (e m q) -> p e m q", e=2, m=M), ACT.Exp,
                               bias=shift1[0:2, 3:4]).then_inc(s["px_exp"], 1)
                chunk(2)
                chunk(3)
                evacuate(0)
                chunk(4)
                chunk(5)
                evacuate(1)

            with act.Fori(0, B) as b:
                exps(b)

            for h in range(2):
                act.wait_ge(s["qkv_done"], h + 1)
                four = halves(sc[:], 4)
                nc_.activation(sq2, four[:, :, 0:2 * D], ACT.Square).then_inc(s["sq2_ready"], 1)
                nc_.copy(v2[:, 2 * h:2 * h + 2].rearrange("p b t h d -> p (b t) (h d)"), four[:, :, 2 * D:3 * D]).then_inc(s["v2_done"], 1)
                act.wait_ge(s["s64_ready"], h + 1)
                nc_.activation(r64[:], v64[:], ACT.Sqrt).then_inc(s["r64_ready"], 1)
                act.wait_ge(s["qk_turned"], h + 1)
                nc_.copy(qt2[:, 2 * h:2 * h + 2], halves(oa[:, 0:512], 2)).then_inc(s["qt2_done"], 1)

            nc_.preload_act_table(ACT.Exp)

            def attend(b, tail):
                def chunk(c):
                    act.wait_ge(s["qk2_chunk"], 6 * b + c + 1)
                    act.wait_ge(s["pv2_done"], 2 * b)
                    nc_.activation(pb[c], sc[:, 1024 * (c % 2):1024 * (c % 2 + 1)], ACT.Exp,
                                   bias=shift2[:, 3:4]).then_inc(s["exp2_done"], 1)

                def evacuate(g):
                    act.wait_ge(s["pv2_done"], 2 * b + g + 1)
                    act.wait_ge(s["o2_turned"], b)
                    nc_.copy(o2s[:, g], oa[:, 512 * g:512 * (g + 1)]).then_inc(s["o2_evac"], 1)

                for c in range(4):
                    chunk(c)
                if tail:
                    turned(b - 1)
                evacuate(0)
                chunk(4)
                chunk(5)
                evacuate(1)

            def turned(b):
                act.wait_ge(s["ao_turned"], b + 1)
                nc_.copy(aoT[:], tm[:, 0:S]).then_inc(s["aoT_ready"], 1)

            attend(0, False)
            with act.Fori(1, B) as b:
                attend(b, True)

            def unit(b, n, out, func=ACT.Gelu, scale=1.0, width=512):
                act.wait_ge(s["u_done"], 8 * b + n + 1)
                src = sc[:, 512 * (n % 4):512 * (n % 4) + width]
                nc_.activation(out, src if width < 512 else halves(src, 2), func, scale=scale).then_inc(s["u_act"], 1)

            def first_units(b):
                unit(b, 0, h2a)
                unit(b, 1, h3a, width=S)
                act.wait_ge(s["down_done"], 2 * b)
                unit(b, 2, h0)
                unit(b, 3, h2b)

            def last_units(b):
                unit(b, 4, th1, ACT.Tanh, 0.5)
                unit(b, 6, h3b)
                unit(b, 7, h2c)

            nc_.preload_act_table(ACT.Gelu)
            first_units(0)
            turned(B - 1)
            last_units(0)
            act.wait_ge(s["gates"], 7)
            nc_.activation(ga[2][:], lg[:], ACT.Exp).then_inc(s["gate_exp"], 1)
            nc_.preload_act_table(ACT.Gelu)
            with act.Fori(1, B) as b:
                first_units(b)
                last_units(b)

        @block.vector
        def _(dve):
            v = nc.vector
            n = [0]

            def step(ins):
                n[0] += 1
                ins.then_inc(s["bias_dve"], 1)
                dve.wait_ge(s["bias_dve"], n[0])

            def row(r, width=D):
                return rows[:, r:r + width]

            step(v.memset(pair_rows[:], 0.0))
            for g in range(2):
                for e in range(2):
                    v.memset(pair_rows[DH * e:DH * (e + 1), g, 2 * g + e:2 * g + e + 1], 1.0)
            def bias_stats():
                for t in range(T):
                    last = v.bn_stats(bst[:, t], hb[:, t])
                step(last)
                for t in range(T):
                    last = v.bn_aggr(bmv[:, t], bst[:, t])
                last.then_inc(s["bias_var"], 1)

            def bias_norm(layer, gain):
                dve.wait_ge(s["bias_rstd"], layer + 1)
                for t in range(T):
                    last = v.tensor_scalar(hb[:, t], hb[:, t], bmv[:, t, 0:1], brs[:, t:t + 1], ALU.subtract, ALU.mult)
                step(last)
                v.tensor_tensor(hb[:], hb[:], row(gain)[:, None, :].to_broadcast([P, T, D]), ALU.mult).then_inc(s["bias_tanh_in"], 1)

            def bias_silu(layer):
                dve.wait_ge(s["bias_tanh"], layer + 1)
                v.scalar_tensor_tensor(hb[:], ht[:], 1.0, hb[:], ALU.add, ALU.mult).then_inc(s["bias_turn_in"], 1)

            def bias_transposed(layer):
                dve.wait_ge(s["bias_turned"], layer + 1)
                v.tensor_scalar(hT[:], mb[:, 0:S], 0.5, None, ALU.mult).then_inc(s["bias_hT"], 1)

            def transposed(h):
                dve.wait_ge(s["xt_done"], h + 1)
                gain = cols[:, C_GN:C_GN + 1]
                src = halves(sc[:, 512 * h:512 * (h + 1)], T)
                dst = xk[:, T * h:T * (h + 1)]
                v.tensor_scalar(xb[:, T * h:T * (h + 1)], src, gain, None, ALU.mult)
                v.tensor_scalar(dst[:, :, 0:P - 1], src[:, :, P - 2::-1], gain, None, ALU.mult)
                v.tensor_scalar(dst[:, :, P:S], src[:, :, S - 2:P - 2:-1], gain, None, ALU.mult)
                v.tensor_scalar(dst[:, :, S:KEYS], src[:, :, S - 1:S], gain, None, ALU.mult).then_inc(s["xb_ready"], 1)

            def values(h):
                dve.wait_ge(s["v_proj"], h + 1)
                for i in range(T):
                    b, at = T * h + i, 512 * h + 3 * DH * i
                    v.tensor_tensor(vn[:, b, 0:2], halves(oa[:, at:at + 2 * DH], 2), mask[:, b, 0:2, None].to_broadcast([P, 2, DH]), ALU.mult)
                    last = v.tensor_tensor(vn[0:2, b, 2:3], oa[0:2, None, at + 2 * DH:at + 3 * DH], mask[0:2, b, 2:3, None].to_broadcast([2, 1, DH]),
                                           ALU.mult)
                last.then_inc(s["vn_done"], 1)

            dve.wait_ge(s["ld_rows"], 16)
            dve.wait_ge(s["pos_ready"], 1)
            for t in range(T):
                last = v.scalar_tensor_tensor(hb[:, t], row(R_W0), pos[:, t:t + 1], row(R_B0), ALU.mult, ALU.add)
            step(last)
            bias_stats()
            dve.wait_ge(s["ld_x"], 16)
            for t in range(B * T):
                last = v.bn_stats(st_x[:, t], x[:, t])
            last.then_inc(s["x_parts"], 1)
            dve.wait_ge(s["x_parts"], 1)
            for t in range(B * T):
                last = v.bn_aggr(mv_x[:, t], st_x[:, t])
            last.then_inc(s["x_stat"], 1)
            bias_norm(0, R_G0)
            dve.wait_ge(s["x_rstd"], 1)
            for t in range(B * T):
                v.tensor_scalar(xc[:, t], x[:, t], mv_x[:, t, 0:1], rs_x[:, t:t + 1], ALU.subtract, ALU.mult).then_inc(s["xc_ready"], 1)
            bias_silu(0)
            dve.wait_ge(s["ld_cols"], 16)
            dve.wait_ge(s["zeroed"], 1)
            transposed(0)
            bias_transposed(0)
            transposed(1)
            dve.wait_ge(s["bias_mm1"], 1)
            step(v.tensor_tensor(hb[:], halves(zb[:, 0:S], T), row(R_B1)[:, None, :].to_broadcast([P, T, D]), ALU.add))
            bias_stats()
            dve.wait_ge(s["ld_mask"], 16)
            v.tensor_copy(mask[:], mask_u8[:]).then_inc(s["mask_ready"], 1)
            dve.wait_ge(s["mask_ready"], 1)
            values(0)
            bias_norm(1, R_G1)
            values(1)
            for sh, (rq, rk, width), bound in ((shift1, (R_QS, R_KS, DH), 8.0), (shift2, (R_QN, R_KN, HD), HD ** 0.5)):
                for i, r in enumerate((rq, rk)):
                    last = v.tensor_reduce(sh[:, i:i + 1], row(r, width), AX.X, ALU.max, apply_absolute_value=True)
                step(last)
                step(v.tensor_tensor(sh[:, 2:3], sh[:, 0:1], sh[:, 1:2], ALU.mult))
                v.tensor_scalar(sh[:, 3:4], sh[:, 2:3], -bound, ROOM, ALU.mult, ALU.add)
            v.scalar_tensor_tensor(qk_scale[:], cols[:, C_QS:C_QS + 1], 8.0, cols[:, C_KS:C_KS + 1], ALU.mult, ALU.mult)
            step(v.scalar_tensor_tensor(qk2_scale[:], cols[:, C_QN:C_QN + 1], HD ** -0.5, cols[:, C_KN:C_KN + 1], ALU.mult, ALU.mult))
            v.memset(zmx[:], 1.0).then_inc(s["shifts"], 1)

            def inverses(b):
                dve.wait_ge(s["kss_done"], b + 1)
                v.tensor_scalar(kmx[:], oa[:, 512:512 + KEYS], 1e-24, None, ALU.max).then_inc(s["kmax_ready"], 1)
                dve.wait_ge(s["qss_done"], 2 * b + 2)
                v.tensor_scalar(qmx[:], zb[:, 0:S], 1e-24, None, ALU.max).then_inc(s["qmax_ready"], 1)
                dve.wait_ge(s["ksqrt_ready"], b + 1)
                v.reciprocal(kin[:], ksr[:]).then_inc(s["kin_ready"], 1)
                dve.wait_ge(s["consts"], 1)
                dve.wait_ge(s["qsqrt_ready"], b + 1)
                v.reciprocal(qin[:, b], qsr[:]).then_inc(s["qinv_ready"], 1)
                dve.wait_ge(s["kr_ready"], b + 1)
                dve.wait_ge(s["kin_ready"], b + 1)
                for e in range(2):
                    r = slice(DH * e, DH * (e + 1))
                    v.scalar_tensor_tensor(keo[r, b, e], kr[r, :], qk_scale[r, 0:1], kin[r, :], ALU.mult, ALU.mult).then_inc(s["keo_done"], 1)

            inverses(0)
            bias_silu(1)
            bias_transposed(1)
            dve.wait_ge(s["ld_small"], 16)
            dve.wait_ge(s["bias_mm2"], 1)
            v.tensor_reduce(top[:, 0:1], mb[0:H, S:2 * S], AX.X, ALU.max)
            step(v.tensor_tensor(top[:, 1:2], small[:, 1:2], small[:, 0:1], ALU.subtract))
            step(v.tensor_tensor(top[:, 2:3], top[:, 0:1], top[:, 1:2], ALU.max))
            v.tensor_scalar(top[:, 3:4], top[:, 2:3], -1.0, None, ALU.mult)
            v.tensor_tensor(top[:, 0:1], top[:, 1:2], top[:, 2:3], ALU.subtract).then_inc(s["bias_top"], 1)
            with dve.Fori(1, B) as b:
                inverses(b)

            dve.wait_ge(s["bias_loaded"], 16 * 10)

            def weigh(b, tail):
                def chunk(c):
                    g, k = divmod(c, 3)
                    dve.wait_ge(s["exp_done"], 6 * b + c + 1)
                    if k < 2:
                        p, w = pb[c].rearrange("p (e m i) -> p e m i", e=2, m=2), eb0[:, :, 4 * g + 2 * k:4 * g + 2 * k + 2]
                    else:
                        p, w = pb[c].rearrange("p (e m i) -> p e m i", e=2, m=4), eb1[:, :, 4 * g:4 * g + 4]
                    v.tensor_tensor(p, p, w, ALU.mult).then_inc(s["mult_done"], 1)

                chunk(0)
                chunk(1)
                dve.wait_ge(s["px_exp"], b + 1)
                v.tensor_tensor(px[0:2], px[0:2], ebx[:], ALU.mult).then_inc(s["px_ready"], 1)
                for c in range(2, 6):
                    chunk(c)
                if tail:
                    norm_y(b - 1)
                dve.wait_ge(s["z_done"], 2 * b + 2)
                v.tensor_scalar(zmx[:], zb[:, 0:S], 1e-37, None, ALU.max).then_inc(s["zmax_done"], 1)
                dve.wait_ge(s["zmax_done"], b + 1)
                dve.wait_ge(s["zinv_stored"], 16 * b)
                v.reciprocal(zin[:], zmx[:]).then_inc(s["zinv_ready"], 1)

            def norm_y(b):
                dve.wait_ge(s["y_done"], b + 1)
                for t in range(T):
                    last = v.bn_stats(st[:, t], mb[:, S + D * t:S + D * (t + 1)])
                last.then_inc(s["y_parts"], 1)
                dve.wait_ge(s["consts"], 1)
                dve.wait_ge(s["y_parts"], b + 1)
                for t in range(T):
                    last = v.bn_aggr(mv[:, t], st[:, t])
                last.then_inc(s["y_stat"], 1)
                dve.wait_ge(s["y_rstd"], b + 1)
                for t in range(T):
                    last = v.tensor_scalar(yn[:, t], mb[:, S + D * t:S + D * (t + 1)], mv[:, t, 0:1], rs[:, t:t + 1], ALU.subtract, ALU.mult)
                last.then_inc(s["y_norm"], 1)
                dve.wait_ge(s["y_norm"], b + 1)
                v.tensor_tensor(tiles(x2, b), yn[:], row(R_GO)[:, None, :].to_broadcast([P, T, D]), ALU.mult).then_inc(s["x2_done"], 1)

            weigh(0, False)
            with dve.Fori(1, B) as b:
                weigh(b, True)

            def rms_norm(h, stat, rstd_done, turned, ready):
                v.tensor_tensor(sq_x[:], quarter(x2, h), quarter(x2, h), ALU.mult).then_inc(s["sq_x_ready"], 1)
                n_sq[0] += 1
                dve.wait_ge(s["sq_x_ready"], n_sq[0])
                v.tensor_reduce(sum_sq[:, :, None], sq_x[:], AX.X, ALU.add).then_inc(stat, 1)
                dve.wait_ge(rstd_done, h + 1)
                v.tensor_tensor(quarter(xc, h), quarter(x2, h), rs_rms[:, :, None].to_broadcast([P, 4, D]), ALU.mult).then_inc(ready, 1)

            n_sq = [0]

            def head_norms(h):
                dve.wait_ge(s["x2_done"], 2 * h + 2)
                rms_norm(h, s["r_stat"], s["r_rstd"], s["h2_turned"], s["h2_ready"])
                dve.wait_ge(s["h2_turned"], h + 1)
                dve.wait_ge(s["qkv_done"], h) if h else None
                v.tensor_scalar(hT2[:], zb, cols[:, C_N1:C_N1 + 1], D ** 0.5, ALU.mult, ALU.mult).then_inc(s["hT2_ready"], 1)
                dve.wait_ge(s["sq2_ready"], h + 1)
                v.tensor_reduce(s64[:], sq2.rearrange("p t (h d) -> p t h d", d=HD), AX.X, ALU.add).then_inc(s["p3_dve"], 1)
                dve.wait_ge(s["p3_dve"], 2 * h + 1)
                v.tensor_scalar(v64[:], s64[:], 1.0 / HD, EPS, ALU.mult, ALU.add).then_inc(s["s64_ready"], 1)
                dve.wait_ge(s["r64_ready"], h + 1)
                v.reciprocal(i64[:], r64[:]).then_inc(s["p3_dve"], 1)
                dve.wait_ge(s["p3_dve"], 2 * h + 2)
                dve.wait_ge(s["v2_done"], h + 1)
                v.tensor_tensor(qkn.rearrange("p t (h d) -> p t h d", d=HD),
                                halves(sc[:], 4)[:, :, 0:2 * D].rearrange("p t (h d) -> p t h d", d=HD),
                                i64[:, :, :, None].to_broadcast([P, 4, 2 * H, HD]), ALU.mult).then_inc(s["qkn_ready"], 1)
                dve.wait_ge(s["qk_turned"], h + 1)
                v.tensor_scalar(kt2[:, 2 * h:2 * h + 2], halves(oa[:, 512:1024], 2), qk2_scale[:, 0:1], None, ALU.mult).then_inc(s["kt2_done"], 1)

            head_norms(0)
            norm_y(B - 1)
            head_norms(1)

            for_ones = v.memset(v2f[:, :, :, HD:HD + 1], 1.0)
            for_ones.then_inc(s["p4_dve"], 1)

            def masked_queries(b):
                dve.wait_ge(s["qt2_done"], 2)
                for g in range(2):
                    dve.wait_ge(s["qk2_chunk"], 6 * b)
                    for k in range(M):
                        last = v.tensor_scalar(qm[:, g, k], qt2[:, b], head_of[:, M * g + k:M * g + k + 1], None, ALU.mult)
                    last.then_inc(s["qm_ready"], 1)

            def weighted_outputs(b):
                dve.wait_ge(s["o2_turned"], b + 1)
                view = tm[:].rearrange("p (n r k) -> p n r k", n=2 * 4, r=4)
                v.reciprocal(rz2[:], view[:, :, :, HD:HD + 1]).then_inc(s["p4_dve"], 1)
                dve.wait_ge(s["p4_dve"], b + 2)
                v.tensor_tensor(ao[:].rearrange("p t (g r d) -> p (t g) r d", g=4, r=4), view[:, :, :, 0:HD],
                                rz2[:].to_broadcast([P, 2 * 4, 4, HD]), ALU.mult).then_inc(s["ao_ready"], 1)

            def add_attention(b):
                dve.wait_ge(s["wo_done"], b + 1)
                v.tensor_tensor(tiles(x2, b)[:, :, OFF:D], tiles(x2, b)[:, :, OFF:D],
                                halves(tm[:, 512:512 + T * DN], T), ALU.add).then_inc(s["x3_done"], 1)

            masked_queries(0)
            with dve.Fori(1, B) as b:
                masked_queries(b)
                weighted_outputs(b - 1)
                add_attention(b - 1)

            def gate_inputs(h, turned, logits):
                dve.wait_ge(s["x3_done"], 2 * h + 2)
                rms_norm(h, s["f_stat"], s["f_rstd"], s["f_turned"], s["f_ready"])
                dve.wait_ge(s["f_turned"], h + 1)
                v.tensor_scalar(xfT[:, 2 * h:2 * h + 2], halves(turned, 2), cols[:, C_N2:C_N2 + 1], D ** 0.5, ALU.mult, ALU.mult).then_inc(s["xfT_ready"], 1)
                dve.wait_ge(s["gate_done"], h + 1)
                v.tensor_copy(quarter(lg, h), halves(logits, 4)).then_inc(s["lg_ready"], 1)

            def silu_expert(b):
                dve.wait_ge(s["u_act"], 7 * b + 5)
                v.scalar_tensor_tensor(si1, th1, 1.0, halves(sc[:, 0:512], 2), ALU.add, ALU.mult).then_inc(s["silu_a"], 1)
                dve.wait_ge(s["silu_a"], b + 1)
                dve.wait_ge(s["u_done"], 8 * b + 6)
                dve.wait_ge(s["down_done"], 2 * b)
                v.tensor_tensor(h1, si1, halves(sc[:, 512:1024], 2), ALU.mult).then_inc(s["h1_ready"], 1)

            gate_inputs(0, sc[:, 0:512], oa[:, 512:512 + 4 * E])
            weighted_outputs(B - 1)
            silu_expert(0)
            add_attention(B - 1)
            gate_inputs(1, zb, mb[:, 0:4 * E])

            m = [0]

            def gate(ins):
                m[0] += 1
                ins.then_inc(s["gates"], 1)
                dve.wait_ge(s["gates"], m[0])

            NT = B * T
            dve.wait_ge(s["lg_ready"], 2)
            clean, num, prob, sel, wts, isn = ga
            gate(v.tensor_scalar(num[:], lg[:], 3.4028235e38, -3.4028235e38, ALU.min, ALU.max))
            gate(v.tensor_tensor(isn[:].bitcast(mybir.dt.int32), lg[:], lg[:], ALU.is_equal))
            gate(v.memset(clean[:], 0.0))
            gate(v.copy_predicated(clean[:], isn[:].bitcast(mybir.dt.int32), num[:]))
            gate(v.tensor_reduce(g1[0][:], clean[:], AX.X, ALU.max))
            gate(v.tensor_tensor(num[:], clean[:], g1[0][:, :, None].to_broadcast([P, NT, E]), ALU.subtract))
            gate(v.tensor_copy(lg[:], num[:]))
            dve.wait_ge(s["gate_exp"], 1)
            gate(v.tensor_reduce(g1[1][:], prob[:], AX.X, ALU.add))
            gate(v.reciprocal(g1[2][:], g1[1][:]))
            gate(v.tensor_tensor(sel[:], prob[:], g1[2][:, :, None].to_broadcast([P, NT, E]), ALU.mult))
            mine = sel[:, :, :, None].to_broadcast([P, NT, E, E])
            other = sel[:, :, None, :].to_broadcast([P, NT, E, E])
            before = tri[:, None, :, :].to_broadcast([P, NT, E, E])
            gate(v.tensor_tensor(gc[0][:], other, mine, ALU.is_gt))
            gate(v.tensor_tensor(gc[1][:], other, mine, ALU.is_equal))
            gate(v.tensor_tensor(gc[2][:], gc[1][:], before, ALU.mult))
            gate(v.tensor_tensor(gc[1][:], gc[0][:], gc[2][:], ALU.add))
            gate(v.tensor_reduce(num[:], gc[1][:], AX.X, ALU.add))
            gate(v.scalar_tensor_tensor(clean[:], num[:], 2.0, sel[:], ALU.is_lt, ALU.mult))
            gate(v.tensor_reduce(g1[0][:], clean[:], AX.X, ALU.add))
            gate(v.tensor_scalar(g1[1][:], g1[0][:], 1e-8, None, ALU.add))
            gate(v.reciprocal(g1[2][:], g1[1][:]))
            gate(v.tensor_tensor(wts[:], clean[:], g1[2][:, :, None].to_broadcast([P, NT, E]), ALU.mult))
            gate(v.tensor_scalar(wts[:, :, 1:2], wts[:, :, 1:2], 0.5, None, ALU.mult))

            def add_experts(b):
                for t in range(T):
                    dve.wait_ge(s["down_done"], 2 * b + t + 1)
                    for i in range(E):
                        dst = x[:, T * b + t, OFF:D]
                        last = v.scalar_tensor_tensor(dst, oa[:, 512 * t + DN * i:512 * t + DN * (i + 1)],
                                                      wts[:, T * b + t, i:i + 1], dst, ALU.mult, ALU.add)
                        last.then_inc(s["res_part"], 1)
                        dve.wait_ge(s["res_part"], 8 * b + 4 * t + i + 1)
                v.tensor_copy(g1[3][:, 0:1], g1[0][:, 0:1]).then_inc(s["res_done"], 1)

            dve.wait_ge(s["xs_ready"], 2)
            add_experts(0)
            with dve.Fori(1, B) as b:
                silu_expert(b)
                add_experts(b)

        @block.tensor
        def _(pe):
            mm, turn = nc.tensor.matmul, nc.tensor.transpose
            def bias_turn(layer):
                pe.wait_ge(s["bias_turn_in"], layer + 1)
                for t in range(T):
                    last = turn(mb[:, D * t:D * (t + 1)], hb[:, t], ident[:])
                last.then_inc(s["bias_turned"], 1)

            def values_of(h):
                pe.wait_ge(s["xb_ready"], h + 1)
                wv = wa[:, A_V:A_V + DH]
                for i in range(T):
                    xkb, at = xk[:, T * h + i], 512 * h + 3 * DH * i
                    mm(oa[:, at:at + DH], xkb[:, 0:P], wv, start=True, stop=False)
                    mm(oa[:, at:at + DH], last_row[:], rows[0:1, R_NV:R_NV + DH], start=False, stop=True)
                    mm(oa[:, at + DH:at + 2 * DH], xkb[:, P:2 * P], wv, start=True, stop=True)
                    last = mm(oa[0:2, at + 2 * DH:at + 3 * DH], xkb[:, S - 1:KEYS], wv, start=True, stop=True)
                last.then_inc(s["v_proj"], 1)

            pe.wait_ge(s["consts"], 1)
            for h in range(2):
                pe.wait_ge(s["xc_ready"], 4 * (h + 1))
                for t in range(4 * h, 4 * h + 4):
                    last = turn(sc[:, D * t:D * (t + 1)], xc[:, t], ident[:])
                last.then_inc(s["xt_done"], 1)
            bias_turn(0)
            pe.wait_ge(s["ld_wa"], 16)
            pe.wait_ge(s["ld_rows"], 16)
            values_of(0)
            pe.wait_ge(s["bias_hT"], 1)
            for t in range(T):
                last = mm(zb[:, D * t:D * (t + 1)], hT[:, P * t:P * (t + 1)], wa[:, A_W1:A_W1 + D], start=True, stop=True)
            last.then_inc(s["bias_mm1"], 1)
            values_of(1)

            def project(b):
                def queries(g):
                    if not (isinstance(b, int) and b == 0):
                        pe.wait_ge(s["q_raw"], 2 * b - 1 + g)
                    for m in range(4 * g, 4 * g + 4):
                        last = mm(sc[:, S * m:S * (m + 1)], wa[:, A_Q + P * m:A_Q + P * (m + 1)], xb[:, b], start=True, stop=True)
                    last.then_inc(s["q_proj"], 1)

                def query_sums(g):
                    pe.wait_ge(s["qsq_ready"], 2 * b + g + 1)
                    for r in range(4):
                        last = mm(zb[32 * r:32 * (r + 1), 0:S], pair_rows[:, g], qsq[:, 4 * g + r], start=(g == 0), stop=(g == 1))
                    last.then_inc(s["qss_done"], 1)

                queries(0)
                pe.wait_ge(s["kr_ready"], b)
                mm(oa[:, 0:KEYS], wa[:, A_KK:A_KK + P], xk[:, b], start=True, stop=True).then_inc(s["k_proj"], 1)
                queries(1)
                pe.wait_ge(s["ksq_ready"], b + 1)
                pe.wait_ge(s["kmax_ready"], b)
                mm(oa[:, 512:512 + KEYS], half_ones[:], ksq[:], start=True, stop=True).then_inc(s["kss_done"], 1)
                pe.wait_ge(s["qmax_ready"], b)
                query_sums(0)
                query_sums(1)

            pe.wait_ge(s["vn_done"], T)
            project(0)
            bias_turn(1)
            pe.wait_ge(s["bias_hT"], 2)
            mm(mb[0:H, S:2 * S], wa[:, A_W2:A_W2 + H], hT[:], start=True, stop=True).then_inc(s["bias_mm2"], 1)
            with pe.Fori(1, B) as b:
                project(b)

            def scores(b, c):
                g, k = divmod(c, 3)
                if not (isinstance(b, int) and 6 * b + c < 2):
                    pe.wait_ge(s["exp_done"], 6 * b + c - 1)
                for e in range(2):
                    if k < 2:
                        m0 = 4 * g + 2 * k
                        lhs, rhs = kf[:, e, 0:P], qt[:, b, m0:m0 + 2]
                    else:
                        lhs, rhs = kf[:, e, P:2 * P], qt[:, b, 4 * g:4 * g + 4, P:S]
                    out = sc[:, 1024 * (c % 2) + 512 * e:1024 * (c % 2) + 512 * (e + 1)]
                    last = mm(out.rearrange("p (m i) -> p m i", m=rhs.shape[1]), lhs, rhs, start=True, stop=True)
                last.then_inc(s["qk_chunk"], 1)

            def extra_scores(b):
                if not isinstance(b, int):
                    pe.wait_ge(s["y_norm"], b - 1)
                for e in range(2):
                    last = mm(mb[0:2, 16 * e:16 * (e + 1)].rearrange("p (m q) -> p m q", q=2), kf[:, e, S - 1:KEYS],
                              qt[:, b, :, P - 1:S:P], start=True, stop=True)
                last.then_inc(s["qk_x"], 1)

            def values(b, g):
                pe.wait_ge(s["mult_done"], 6 * b + 3 * g + 3)
                pe.wait_ge(s["px_ready"], b + 1)
                pe.wait_ge(s["vf_ready"], b + 1)
                pe.wait_ge(s["o_evac"], 2 * b + g)
                late = pb[3 * g + 2].rearrange("p (e m i) -> p e m i", e=2, m=4)
                for k in range(2):
                    for part in range(3):
                        for e in range(2):
                            out = oa[DH * e:DH * (e + 1), 512 * k:512 * (k + 1)]
                            by_pair = out.rearrange("p (m i) -> p m i", m=2)
                            if part == 0:
                                rhs = pb[3 * g + k][:, 512 * e:512 * (e + 1)]
                            elif part == 1:
                                out, rhs = by_pair[:, :, P:S], late[:, e, 2 * k:2 * k + 2]
                            else:
                                out, rhs = by_pair[:, :, P - 1:S:P], px[:, e, 4 * g + 2 * k:4 * g + 2 * k + 2]
                            last = mm(out, vf[:, part], rhs, start=(part == 0), stop=(part == 2))
                last.then_inc(s["pv_done"], 1)

            def sums(b, g):
                if g == 0:
                    pe.wait_ge(s["zmax_done"], b)
                late = pb[3 * g + 2].rearrange("p (e m i) -> p e m i", e=2, m=4)
                for e in range(2):
                    for part in range(3):
                        for r in range(4):
                            out = zb[32 * r:32 * (r + 1), 0:S]
                            if part == 0:
                                rhs = pb[3 * g + r // 2][:, 512 * e + S * (r % 2):512 * e + S * (r % 2 + 1)]
                            elif part == 1:
                                out, rhs = out[:, P:S], late[:, e, r]
                            else:
                                out, rhs = out[:, P - 1:S:P], px[:, e, 4 * g + r]
                            last = mm(out, ocm[:, part, 2 * g + e], rhs, start=(g == 0 and e == 0 and part == 0),
                                      stop=(g == 1 and e == 1 and part == 2), skip_group_check=True)
                last.then_inc(s["z_done"], 1)

            def out_product(b):
                pe.wait_ge(s["on_ready"], b + 1)
                for t in range(T):
                    for m in range(M):
                        last = mm(mb[:, S + D * t:S + D * (t + 1)], on[:, m, P * t:P * (t + 1)],
                                  wa[:, A_O + D * m:A_O + D * (m + 1)], start=(m == 0), stop=(m == M - 1))
                last.then_inc(s["y_done"], 1)

            def attend(b, tail):
                pe.wait_ge(s["q_done"], b + 1)
                pe.wait_ge(s["kf_ready"], b + 1)
                scores(b, 0)
                scores(b, 1)
                extra_scores(b)
                scores(b, 2)
                scores(b, 3)
                values(b, 0)
                sums(b, 0)
                scores(b, 4)
                scores(b, 5)
                if tail:
                    out_product(b - 1)
                values(b, 1)
                sums(b, 1)

            pe.wait_ge(s["q_raw"], 2 * B)
            attend(0, False)
            with pe.Fori(1, B) as b:
                attend(b, True)

            def project2(h):
                pe.wait_ge(s["h2_ready"], h + 1)
                for t in range(4):
                    last = turn(zb[:, D * t:D * (t + 1)], xc[:, 4 * h + t], ident[:])
                last.then_inc(s["h2_turned"], 1)
                pe.wait_ge(s["hT2_ready"], h + 1)
                for t in range(4):
                    last = mm(sc[:, 512 * t:512 * t + 3 * D], hT2[:, P * t:P * (t + 1)], wb[:, W_QKV:W_QKV + 3 * D], start=True, stop=True)
                last.then_inc(s["qkv_done"], 1)
                pe.wait_ge(s["qkn_ready"], h + 1)
                pe.wait_ge(s["o_evac"], 2 * B)
                if h:
                    pe.wait_ge(s["qt2_done"], h)
                for which in range(2):
                    for t in range(4):
                        last = turn(oa[:, 512 * which + P * t:512 * which + P * (t + 1)], qkn[:, t, D * which:D * (which + 1)], ident[:])
                last.then_inc(s["qk_turned"], 1)

            pe.wait_ge(s["ld_wb"], 16)
            project2(0)
            pe.wait_ge(s["y_norm"], B - 1)
            out_product(B - 1)
            project2(1)

            def scores2(b, c):
                g, k = divmod(c, 3)
                if not (isinstance(b, int) and 6 * b + c < 2):
                    pe.wait_ge(s["exp2_done"], 6 * b + c - 1)
                for j in range(2):
                    if k < 2:
                        lhs, rhs = k2f[:, 0:P], qm[:, g, 4 * k + 2 * j:4 * k + 2 * j + 2]
                    else:
                        lhs, rhs = k2f[:, P:S], qm[:, g, 4 * j:4 * j + 4, P:S]
                    out = sc[:, 1024 * (c % 2) + 512 * j:1024 * (c % 2) + 512 * (j + 1)]
                    last = mm(out.rearrange("p (m i) -> p m i", m=rhs.shape[1]), lhs, rhs, start=True, stop=True)
                last.then_inc(s["qk2_chunk"], 1)

            def values2(b, g):
                pe.wait_ge(s["masked"], 6 * b + 3 * g + 3)
                pe.wait_ge(s["v2f_ready"], b + 1)
                pe.wait_ge(s["p4_dve"], 1)
                pe.wait_ge(s["o2_evac"], 2 * b)
                for k in range(2):
                    for part in range(2):
                        for r in range(4):
                            out = oa[32 * r:32 * (r + 1), 512 * g + S * k:512 * g + S * (k + 1)]
                            if part == 0:
                                rhs = pb[3 * g + k][:, S * r:S * (r + 1)]
                            else:
                                out, rhs = out[:, P:S], pb[3 * g + 2][:, P * (4 * k + r):P * (4 * k + r + 1)]
                            last = mm(out, v2f[:, part, 8 * g + 4 * k + r], rhs, start=(k == 0 and part == 0), stop=(part == 1),
                                      skip_group_check=True)
                last.then_inc(s["pv2_done"], 1)

            def turn_outputs(b):
                pe.wait_ge(s["o2_evac"], 2 * (b + 1))
                if not (isinstance(b, int) and b == 0):
                    pe.wait_ge(s["x3_done"], b)
                for t in range(T):
                    for k in range(4):
                        last = turn(tm[:, 512 * t + P * k:512 * t + P * (k + 1)], o2s[:, k // 2, S * (k % 2) + P * t:S * (k % 2) + P * (t + 1)], ident[:])
                last.then_inc(s["o2_turned"], 1)

            def turn_back(b):
                pe.wait_ge(s["ao_ready"], b + 1)
                for t in range(T):
                    last = turn(tm[:, P * t:P * (t + 1)], ao[:, t], ident[:])
                last.then_inc(s["ao_turned"], 1)

            def out_product2(b):
                pe.wait_ge(s["aoT_ready"], b + 1)
                for t in range(T):
                    last = mm(tm[:, 512 + DN * t:512 + DN * (t + 1)], aoT[:, P * t:P * (t + 1)], wb[:, W_O:W_O + DN], start=True, stop=True)
                last.then_inc(s["wo_done"], 1)

            def attend2(b, tail):
                pe.wait_ge(s["k2f_ready"], b + 1)
                pe.wait_ge(s["qm_ready"], 2 * b + 1)
                scores2(b, 0)
                if tail:
                    turn_outputs(b - 1)
                scores2(b, 1)
                scores2(b, 2)
                if tail:
                    turn_back(b - 1)
                pe.wait_ge(s["qm_ready"], 2 * b + 2)
                scores2(b, 3)
                if tail:
                    out_product2(b - 1)
                values2(b, 0)
                scores2(b, 4)
                scores2(b, 5)
                values2(b, 1)

            attend2(0, False)
            with pe.Fori(1, B) as b:
                attend2(b, True)

            def gate(h, turned, logits):
                pe.wait_ge(s["f_ready"], h + 1)
                for t in range(4):
                    last = turn(turned[:, D * t:D * (t + 1)], xc[:, 4 * h + t], ident[:])
                last.then_inc(s["f_turned"], 1)
                pe.wait_ge(s["xfT_ready"], h + 1)
                for t in range(4):
                    last = mm(logits[:, E * t:E * (t + 1)], xfT[:, 2 * h + t // 2, P * (t % 2):P * (t % 2 + 1)], wb[:, W_G:W_G + E],
                              start=True, stop=True)
                last.then_inc(s["gate_done"], 1)

            def layer(n, w, src, outs=2):
                chunks = len(src)
                for o in range(outs):
                    for i, part in enumerate(src):
                        last = mm(sc[:, 512 * (n % 4) + S * o:512 * (n % 4) + S * (o + 1)],
                                  wb[:, w + HID * i + P * o:w + HID * i + P * (o + 1)], part, start=(i == 0), stop=(i == chunks - 1))
                last.then_inc(s["u_done"], 1)

            def first_layers(b):
                xin = [xfT[:, b]]
                pe.wait_ge(s["silu_a"], b)
                layer(0, W_L1, xin)
                pe.wait_ge(s["h1_ready"], b)
                layer(1, W_D3, xin, 1)
                pe.wait_ge(s["u_act"], 7 * b)
                layer(2, W_E0, xin)
                pe.wait_ge(s["u_act"], 7 * b + 1)
                layer(3, W_L2, [h2a[:, 0], h2a[:, 1]])

            def last_layers(b):
                xin = [xfT[:, b]]
                layer(4, W_E11, xin)
                pe.wait_ge(s["u_act"], 7 * b + 2)
                layer(5, W_E12, xin)
                pe.wait_ge(s["u_act"], 7 * b + 3)
                layer(6, W_U3, [h3a])
                pe.wait_ge(s["u_act"], 7 * b + 4)
                layer(7, W_L3, [h2b[:, 0], h2b[:, 1]])

            def down(b):
                pe.wait_ge(s["h1_ready"], b + 1)
                pe.wait_ge(s["u_act"], 7 * b + 7)
                pe.wait_ge(s["res_done"], b)
                for t in range(T):
                    for i, h in enumerate((h0, h1, h2c, h3b)):
                        for k in range(2):
                            w = W_DN + (2 * i + k) * DN
                            last = mm(oa[:, 512 * t + DN * i:512 * t + DN * (i + 1)], h[:, k, P * t:P * (t + 1)], wb[:, w:w + DN],
                                      start=(k == 0), stop=(k == 1))
                    last.then_inc(s["down_done"], 1)

            pe.wait_ge(s["exp2_done"], 6 * B)
            pe.wait_ge(s["o2_evac"], 2 * B)
            gate(0, sc[:, 0:512], oa[:, 512:512 + 4 * E])
            turn_outputs(B - 1)
            first_layers(0)
            turn_back(B - 1)
            last_layers(0)
            out_product2(B - 1)
            pe.wait_ge(s["lg_ready"], 1)
            down(0)
            pe.wait_ge(s["x3_done"], B)
            gate(1, zb, mb[:, 0:4 * E])
            with pe.Fori(1, B) as b:
                first_layers(b)
                last_layers(b)
                down(b)


def kernel(**a):
    import numpy as np
    from concourse import bacc
    from concourse.bass_utils import run_bass_kernel_spmd

    a = {k: np.asarray(v) for k, v in a.items()}
    c = {k[len("L0_cond_"):]: v for k, v in a.items() if k.startswith("L0_cond_")}
    f = {k[len("L0_ffn_"):]: v for k, v in a.items() if k.startswith("L0_ffn_")}
    cond = a["cond_64"]

    def chunks(w):
        return np.concatenate([w[i:i + P] for i in range(0, w.shape[0], P)], axis=1)

    cols = np.stack([c["g_norm"], f["n1_w"], f["n2_w"], np.tile(c["q_scale"], 2), np.tile(c["k_scale"], 2),
                     np.tile(cond[0], 2), np.tile(f["qn_w"], H), np.tile(f["kn_w"], H)], axis=1)
    rows = np.concatenate([c["g_out"], c["w0"][0], c["b0"], c["g0"], c["b1"], c["g1"], c["q_scale"], c["k_scale"],
                           cond[1], f["qn_w"], f["kn_w"]])[None]
    wk = c["Wkv"][:, :DH]
    wa = np.concatenate([wk, wk, c["Wkv"][:, DH:], c["w1"], c["w2"], c["Wq"], chunks(c["Wout"])], axis=1)
    downs = [chunks(f[n][OFF:].T) for n in ("e0_down", "e1_down", "e2_l4", "e3_out")]
    wb = np.concatenate([f["wq"].T, f["wk"].T, f["wv"].T, f["wo"][OFF:].T, f["gate_w"].T, f["e0_up"].T, f["e1_w1"].T,
                         f["e1_w2"].T, f["e2_l1"].T, chunks(f["e2_l2"].T), chunks(f["e2_l3"].T), f["e3_down"].T,
                         f["e3_up"].T] + downs, axis=1)
    assert wa.shape[1] == A_ALL and wb.shape[1] == W_ALL and rows.shape[1] == R_ALL
    told = a["mask_BxS_bf1"]
    mask = np.zeros((P, B, 3), told.dtype)
    mask[P - 1, :, 0] = True
    mask[:P - 1, :, 0] = told[:, P - 2::-1].T
    mask[:, :, 1] = told[:, S - 2:P - 2:-1].T
    mask[:2, :, 2] = told[:, P - 1::P].T
    arrays = {"x": a["x"].reshape(B * S, D), "cols": cols, "rows": rows, "small": np.stack([c["b2"], c["null_attn_bias"]], axis=1),
              "mask": mask, "wa": wa, "wb": wb}
    arrays = {f"in_{k}": np.ascontiguousarray(v) for k, v in arrays.items()}

    nc = bacc.Bacc("TRN2", target_bir_lowering=False, num_devices=1)
    ins = [nc.dram_tensor(k, v.shape, mybir.dt.from_np(v.dtype), kind="ExternalInput").ap() for k, v in arrays.items()]
    out = nc.dram_tensor("out", (B * S, D), F32, kind="ExternalOutput").ap()
    adaln_ffn(nc, *ins, out)
    r = run_bass_kernel_spmd(nc, [arrays], core_ids=[0])
    return r.results[0]["out"].reshape(B, S, D)
```

```python
from contextlib import ExitStack

import concourse.bass as bass
from concourse import mybir

F32 = mybir.dt.float32
BF16 = mybir.dt.bfloat16
U8 = mybir.dt.uint8
ALU = mybir.AluOpType
ACT = mybir.ActivationFunctionType
AX = mybir.AxisListType

P = 128
B, S, D = 4, 256, 128
T = S // P
H, DH = 16, 64
M = H // 2
HD = D // H
HID = 256
E = 4
SLOT = (0, 1, 0, 0, 1, 0)
PART_STEPS = 8
GROUPS = ((0, 2 * T, 0), (2 * T, T, 3072), (3 * T, T, 3072))
OFF = 32
DN = D - OFF
KEYS = S + 1
GT = 3 * P
EPS = 1.1920929e-07
FAR = 1e30
ROOM = 60.0

C_GN, C_N1, C_N2, C_QS, C_KS, C_NK, C_QN, C_KN = range(8)
R_GO, R_W0, R_B0, R_G0, R_B1, R_G1 = (D * i for i in range(6))
R_QS, R_KS, R_NV = (6 * D + DH * i for i in range(3))
R_QN, R_KN = 6 * D + 3 * DH, 6 * D + 3 * DH + HD
R_ALL = R_KN + HD
A_KK, A_V, A_W1, A_W2 = 0, P, P + DH, 2 * P + DH
A_Q = A_W2 + H
A_O = A_Q + H * DH
A_ALL = A_O + M * D
W_QKV = 0
W_O = W_QKV + 3 * D
W_G = W_O + DN
W_E0 = W_G + E
W_E11 = W_E0 + HID
W_E12 = W_E11 + HID
W_L1 = W_E12 + HID
W_L2 = W_L1 + HID
W_L3 = W_L2 + 2 * HID
W_D3 = W_L3 + 2 * HID
W_U3 = W_D3 + D
W_DN = W_U3 + HID
W_ALL = W_DN + E * 2 * DN


def adaln_ffn(nc, x_d, cols_d, rows_d, small_d, mask_d, wa_d, wb_d, out_d):
    with ExitStack() as ctx:
        def sb(name, shape, dt=F32):
            return ctx.enter_context(nc.sbuf_tensor(name, shape, dt))

        def ps(name, shape):
            return ctx.enter_context(nc.psum_tensor(name, shape, F32))

        def sem(name):
            return ctx.enter_context(nc.semaphore(name))

        table_d = nc.dram_tensor("bias_table", (H, GT), F32, kind="Internal").ap()
        qinv_d = nc.dram_tensor("q_inverse_norms", (B, P, S), F32, kind="Internal").ap()
        null_d = nc.dram_tensor("null_weights", (H, S), F32, kind="Internal").ap()
        zinv_d = nc.dram_tensor("softmax_inverse_sums", (B, P, S), F32, kind="Internal").ap()

        x = sb("x", [P, B * T, D])
        cols = sb("cols", [P, 8])
        rows = sb("rows", [P, R_ALL])
        small = sb("small", [H, 2])
        mask_u8 = sb("mask_u8", [P, B, 3], U8)
        mask = sb("mask", [P, B, 3])
        wa = sb("wa", [P, A_ALL])
        wb = sb("wb", [P, W_ALL])
        ident = sb("ident", [P, P])
        half_ones = sb("half_ones", [P, P])
        pair_rows = sb("pair_rows", [P, 2, 32])
        sum_rows = sb("sum_rows", [P, 4, 32])
        later = sb("later", [P, P])
        minus_half = sb("minus_half", [P, B * T])
        ln_eps = sb("ln_eps", [P, B * T])
        rms_eps = sb("rms_eps", [P, 4])
        zeros = sb("zeros", [P, S])
        shift1 = sb("shift1", [P, 4])
        shift2 = sb("shift2", [P, 4])
        qk_scale = sb("qk_scale", [P, 1])
        pos = sb("pos", [P, T])
        scratch = sb("scratch", [P, 2 * T, D])
        hb = scratch[:, 0:T]
        ht = scratch[:, T:2 * T]
        hT = sb("hT", [P, S])
        bst = sb("bst", [P, T, 6])
        bmv = sb("bmv", [P, T, 2])
        bve = sb("bve", [P, T])
        brs = sb("brs", [P, T])
        top = sb("top", [H, 4])
        table = sb("table", [H, GT])
        null_row = sb("null_row", [H, S])
        eb0 = sb("eb0", [P, 2, M, S])
        eb1 = sb("eb1", [P, 2, M, P])
        ebx = sb("ebx", [2, 2, M, 2])
        st_x = sb("st_x", [P, B * T, 6])
        mv_x = sb("mv_x", [P, B * T, 2])
        ve_x = sb("ve_x", [P, B * T])
        rs_x = sb("rs_x", [P, B * T])
        st = sb("st", [P, T, 6])
        mv = sb("mv", [P, T, 2])
        ve = sb("ve", [P, T])
        rs = sb("rs", [P, T])
        xc = sb("xc", [P, B * T, D])
        last_row = sb("last_row", [1, P])
        kr = sb("kr", [P, KEYS])
        ksq = sb("ksq", [P, KEYS])
        kmx = sb("kmx", [P, KEYS])
        ksr = sb("ksr", [P, KEYS])
        kin = sb("kin", [P, KEYS])
        keo = sb("keo", [P, B, 2, KEYS])
        qt = sb("qt", [P, B, M, S])
        qmx = sb("qmx", [P, S])
        qsr = sb("qsr", [P, S])
        spread = sb("spread", [P, M, S])
        vn = sb("vn", [P, B, 3, DH])
        kf = sb("kf", [P, 2, KEYS])
        vf = sb("vf", [P, 3, DH])
        ocm = sb("ocm", [P, 3, 4, 32])
        probs = sb("probs", [P, 6, 1024])
        pb = [probs[:, i] for i in range(6)]
        px = sb("px", [P, 2, M, 2])
        o_raw = sb("o_raw", [P, M, S])
        qsq = o_raw[:]
        on = sb("on", [P, M, S])
        xb = on[:, 0:B, :]
        xk = probs[:, 0:2, :].rearrange("p a c -> p (a c)")[:, 0:B * KEYS].rearrange("p (b j) -> p b j", b=B)
        zmx = sb("zmx", [P, S])
        zin = sb("zin", [P, S])
        yn = sb("yn", [P, T, D])
        x2 = sb("x2", [P, B * T, D])
        qin = x2[:].rearrange("p (b t) d -> p b (t d)", b=B)
        sq_x = scratch[:]
        sum_sq = sb("sum_sq", [P, 4])
        ve_rms = sb("ve_rms", [P, 4])
        rs_rms = sb("rs_rms", [P, 4])
        hT2 = sb("hT2", [P, 4 * D])
        s64 = sb("s64", [P, 4, 2 * H])
        v64 = sb("v64", [P, 4, 2 * H])
        r64 = sb("r64", [P, 4, 2 * H])
        i64 = sb("i64", [P, 4, 2 * H])
        qk_raw = sb("qk_raw", [P, 4, 2 * D])
        keys_space = keo[:].rearrange("p b e j -> p (b e j)")
        sq2 = keys_space[:, 0:4 * 2 * D].rearrange("p (t c) -> p t c", t=4)
        qkn = qt[:, 2].rearrange("p m i -> p (m i)").rearrange("p (w t c) -> p w t c", w=2, t=B * T)
        parts = sb("parts", [P, 2, T * H, DH // HD, HD], BF16)
        rest = sb("rest", [P, 3, T * H, HD])
        v2 = qt[:, 0].rearrange("p m i -> p (m i)")[:, B * S:2 * B * S].rearrange("p (b t h d) -> p b t h d", b=B, t=T, h=H)
        ident_bf = sb("ident_bf", [P, P], BF16)
        later_bf = sb("later_bf", [P, P], BF16)
        gain2 = sb("gain2", [P, HD])
        v2f = sb("v2f", [P, T, H, 32])
        o2s = keys_space[:, B * S:B * S + 1024].rearrange("p (g c) -> p g c", g=2)
        rz2 = sb("rz2", [P, T * 4, 4, 1])
        ao = sb("ao", [P, T, D])
        aoT = sb("aoT", [P, S])
        lg = sb("lg", [P, B * T, E])
        ga = [sb(f"ga{i}", [P, B * T, E]) for i in range(6)]
        g1 = [sb(f"g1_{i}", [P, B * T]) for i in range(4)]
        gc = [sb(f"gc{i}", [P, B * T, E, E]) for i in range(3)]
        tri = sb("tri", [P, E, E])
        qT2 = qt[:, 0].rearrange("p m i -> p (m i)").bitcast(BF16)[:, 0:M * S].rearrange("p (m i) -> p m i", m=M)
        kT2 = qt[:, 1].rearrange("p m i -> p (m i)").bitcast(BF16).rearrange("p (e m i) -> p e m i", e=2, m=M)
        xfT = keys_space[:, 0:B * S].rearrange("p (b i) -> p b i", b=B)
        h0 = o_raw[:, 0:2, :]
        h1 = o_raw[:, 2:4, :]
        h2a = o_raw[:, 4:6, :]
        h2b = o_raw[:, 6:8, :]
        h2c = on[:, 0:2, :]
        h3a = on[:, 2, :]
        h3b = on[:, 3:5, :]
        th1 = on[:, 5:7, :]
        si1 = spread[:, 0:2, :]

        banks = ps("banks", [P, 4096])
        sc = banks[:, 0:2048]
        oa = banks[:, 2048:3072]
        tm = banks[:, 3072:4096]
        turned_bf = banks[:].bitcast(BF16)[:, 2048:4096]
        zb = tm[:, 0:512]
        mb = tm[:, 512:1024]

        names = """ld_x ld_cols ld_rows ld_small ld_mask ld_wa ld_wb
            consts zeroed mask_ready shifts pos_ready
            bias_dve bias_pool bias_var bias_rstd bias_tanh_in bias_tanh bias_turn_in bias_turned bias_hT bias_mm1 bias_mm2
            bias_top table_ready null_ready table_stored bias_loaded
            x_parts x_stat x_var x_rstd xc_ready xt_done xb_ready k_proj v_proj q_proj kr_ready ksq_ready kss_done
            q_raw qsq_ready qss_done kmax_ready ksqrt_ready qmax_ready qsqrt_ready qinv_ready qinv_stored
            qinv_spread q_done keo_done vn_done kin_ready
            kf_ready vf_ready ocm_ready qk_chunk qk_x exp_done px_exp px_ready mult_done pv_done z_done o_evac
            zmax_done zinv_ready zinv_stored zinv_spread on_ready y_done y_parts y_stat y_var y_rstd y_norm x2_done
            r_stat r_var r_rstd h2_ready h2_turned hT2_ready qkv_done raw_ready sq2_ready s64_ready r64_ready qkn_ready
            v2_done sq_x_ready p3_dve
            v2f_ready operands_zeroed part_done parts_ready parts_turned operands2_ready qk2_chunk exp2_done pv2_done o2_evac o2_turned ao_ready ao_turned
            aoT_ready wo_done x3_done p4_dve
            f_stat f_var f_rstd f_ready f_turned xfT_ready gate_done lg_ready gate_w xs_ready gates
            gate_exp res_part u_done u_act silu_a h1_ready down_done res_done stored""".split()
        s = {n: sem(n) for n in names}

        block = ctx.enter_context(nc.Block())


        def spread_from(dram, b, g, e):
            src = dram[b]
            return bass.AP(tensor=src.tensor, offset=src.offset + (2 * g + e) * S, ap=[[0, DH], [32 * S, 4], [1, S]])

        def nulls_in(e):
            return bass.AP(tensor=null_d.tensor, offset=e * S, ap=[[2 * S, 1], [2 * S, M], [1, S]])

        def tiles(a, b):
            return a[:, bass.ds(T * b, T)]

        def quarter(a, h):
            return a[:, 4 * h:4 * (h + 1)]

        def halves(a, n):
            return a.rearrange("p (a c) -> p a c", a=n)

        @block.sync
        def _(sp):
            sp.dma_start(x[:], x_d.rearrange("(n p) d -> p n d", p=P)).then_inc(s["ld_x"], 16)
            sp.dma_start(rows[:], bass.AP(tensor=rows_d.tensor, offset=0, ap=[[0, P], [1, R_ALL]])).then_inc(s["ld_rows"], 16)
            sp.dma_start(cols[:], cols_d).then_inc(s["ld_cols"], 16)
            sp.dma_start(small[:], small_d).then_inc(s["ld_small"], 16)
            sp.dma_start(wa[:], wa_d).then_inc(s["ld_wa"], 16)
            sp.dma_start(mask_u8[:], mask_d).then_inc(s["ld_mask"], 16)
            sp.dma_start(wb[:], wb_d).then_inc(s["ld_wb"], 16)

            def spread_queries(b):
                sp.wait_ge(s["qinv_ready"], b + 1)
                sp.dma_start(qinv_d[b], qin[:, b]).then_inc(s["qinv_stored"], 16)
                sp.wait_ge(s["qinv_stored"], 16 * (b + 1))
                if not isinstance(b, int):
                    sp.wait_ge(s["q_done"], b)
                for g in range(2):
                    for e in range(2):
                        sp.dma_start(spread[DH * e:DH * (e + 1), 4 * g:4 * g + 4], spread_from(qinv_d, b, g, e)).then_inc(s["qinv_spread"], 16)

            spread_queries(0)
            sp.wait_ge(s["table_ready"], 1)
            sp.dma_start(table_d, table[:]).then_inc(s["table_stored"], 16)
            sp.wait_ge(s["null_ready"], 1)
            sp.dma_start(null_d, null_row[:]).then_inc(s["table_stored"], 16)
            sp.wait_ge(s["table_stored"], 32)
            for e in range(2):
                base = e * GT + 1
                sp.dma_start(eb0[0:P - 1, e], bass.AP(tensor=table_d.tensor, offset=base,
                                                      ap=[[1, P - 1], [2 * GT, M], [1, S]])).then_inc(s["bias_loaded"], 16)
                sp.dma_start(eb0[P - 1:P, e], nulls_in(e)).then_inc(s["bias_loaded"], 16)
                sp.dma_start(eb1[:, e], bass.AP(tensor=table_d.tensor, offset=base,
                                                ap=[[1, P], [2 * GT, M], [1, P]])).then_inc(s["bias_loaded"], 16)
            sp.wait_ge(s["zeroed"], 1)
            for e in range(2):
                for k in range(2):
                    src = bass.AP(tensor=table_d.tensor, offset=e * GT + P - 1, ap=[[2 * GT, 1], [2 * GT, M], [1, 1]])
                    sp.dma_start(ebx[k:k + 1, e, :, k:k + 1], src, allow_slow_non_contiguous=True).then_inc(s["bias_loaded"], 16)

            with sp.Fori(1, B) as b:
                spread_queries(b)
            sp.wait_ge(s["q_done"], B)
            with sp.Fori(0, B) as b:
                sp.wait_ge(s["zinv_ready"], b + 1)
                sp.dma_start(zinv_d[b], zin[:]).then_inc(s["zinv_stored"], 16)
                sp.wait_ge(s["zinv_stored"], 16 * (b + 1))
                sp.wait_ge(s["on_ready"], b)
                for g in range(2):
                    for e in range(2):
                        sp.dma_start(spread[DH * e:DH * (e + 1), 4 * g:4 * g + 4], spread_from(zinv_d, b, g, e)).then_inc(s["zinv_spread"], 16)
            with sp.Fori(0, B) as b:
                sp.wait_ge(s["res_done"], b + 1)
                sp.dma_start(out_d.rearrange("(b n p) d -> p b n d", p=P, n=T)[:, b], tiles(x, b)).then_inc(s["stored"], 16)
            sp.wait_ge(s["stored"], 16 * B)


        @block.gpsimd
        def _(pool):
            n = [0]

            def step(ins):
                n[0] += 1
                ins.then_inc(s["zeroed"], 1)
                pool.wait_ge(s["zeroed"], n[0])

            pool.iota(pos[:], pattern=[[P, T]], base=0, channel_multiplier=1,
                      allow_small_or_imprecise_dtypes=True).then_inc(s["pos_ready"], 1)
            for buf, value in ((half_ones, 0.5), (minus_half, -0.5), (ln_eps, 1e-5), (ident, 0.0), (sum_rows, 0.0),
                               (later, 0.0), (xk[:, :, P - 1:P], 0.0), (last_row, 0.0), (px, 0.0), (v2f, 0.0), (keo, 0.0), (tri, 1.0), (vn, 0.0)):
                pool.memset(buf[:], value)
            pool.memset(table[:], 0.0)
            pool.memset(ebx[:], 0.0)
            step(pool.memset(zeros[:], 0.0))
            pool.affine_select(out=ident[:], in_=ident[:], compare_op=ALU.not_equal, fill=1.0, base=0,
                               pattern=[[-1, P]], channel_multiplier=1)
            pool.affine_select(out=later[:], in_=later[:], compare_op=ALU.is_ge, fill=-FAR, base=0,
                               pattern=[[1, P]], channel_multiplier=-1)
            pool.memset(last_row[:, P - 1:P], 1.0)
            for k in range(4):
                pool.memset(sum_rows[:, k, k:k + 1], 1.0)
            pool.affine_select(out=tri[:], in_=tri[:], compare_op=ALU.is_ge, fill=0.0, base=-1,
                               pattern=[[1, E], [-1, E]], channel_multiplier=0)
            step(pool.memset(rms_eps[:], EPS * D))
            pool.tensor_copy(ident_bf[:], ident[:])
            pool.tensor_copy(later_bf[:], later[:]).then_inc(s["consts"], 1)
            pool.wait_ge(s["consts"], 1)

            def rstd(var, eps, ve_, out, ready, done, count, base):
                pool.wait_ge(ready, base + 1)
                pool.tensor_tensor(ve_, var, eps[:, 0:var.shape[1]], ALU.add).then_inc(count, 1)
                pool.wait_ge(count, base + 1)
                pool.tensor_tensor(out, ve_, minus_half[:, 0:var.shape[1]], ALU.pow).then_inc(done, 1)

            for layer in range(2):
                if layer == 1:
                    rstd(mv_x[:, :, 1], ln_eps, ve_x[:], rs_x[:], s["x_stat"], s["x_rstd"], s["x_var"], 0)
                rstd(bmv[:, :, 1], ln_eps, bve[:], brs[:], s["bias_var"], s["bias_rstd"], s["bias_pool"], layer)

            def queries(b):
                pool.wait_ge(s["qinv_spread"], 64 * (b + 1))
                pool.tensor_tensor(qt[:, b], qt[:, b], spread[:], ALU.mult).then_inc(s["q_done"], 1)


            def operands(b):
                pool.wait_ge(s["keo_done"], 2 * (b + 1))
                pool.wait_ge(s["vn_done"], T)
                pool.wait_ge(s["mask_ready"], 1)
                pool.wait_ge(s["qk_chunk"], 6 * b)
                pool.wait_ge(s["qk_x"], b)
                pool.tensor_copy(kf[:], keo[:, b]).then_inc(s["kf_ready"], 1)
                pool.wait_ge(s["z_done"], 2 * b)
                pool.tensor_copy(vf[:], vn[:, b])
                pool.tensor_tensor(ocm[:], sum_rows[:, None, :, :].to_broadcast([P, 3, 4, 32]),
                                   mask[:, b, :, None, None].to_broadcast([P, 3, 4, 32]), ALU.mult).then_inc(s["vf_ready"], 1)

            def normalised(b):
                pool.wait_ge(s["zinv_spread"], 64 * (b + 1))
                pool.wait_ge(s["o_evac"], 2 * (b + 1))
                pool.wait_ge(s["y_done"], b)
                pool.tensor_tensor(on[:], o_raw[:], spread[:], ALU.mult).then_inc(s["on_ready"], 1)
                rstd(mv[:, :, 1], ln_eps, ve[:], rs[:], s["y_stat"], s["y_rstd"], s["y_var"], b)

            pool.memset(parts[:], 0.0)
            queries(0)
            operands(0)
            with pool.Fori(1, B) as b:
                queries(b)
            with pool.Fori(1, B - 1) as b:
                operands(b)
                normalised(b - 1)

            def group_rstd(i):
                n = GROUPS[i][1]
                rstd(sum_sq[:, 0:n], rms_eps, ve_rms[:, 0:n], rs_rms[:, 0:n], s["r_stat"], s["r_rstd"], s["r_var"], i)

            def values2_in_place(b):
                pool.wait_ge(s["pv2_done"], 2 * b)
                pool.tensor_copy(v2f[:, :, :, 0:HD], v2[:, b]).then_inc(s["v2f_ready"], 1)

            operands(B - 1)
            group_rstd(0)
            normalised(B - 2)
            pool.wait_ge(s["qk_chunk"], 6 * (B - 1))
            pool.memset(qt[:, 1], 0.0).then_inc(s["operands_zeroed"], 1)
            group_rstd(1)
            pool.wait_ge(s["v2_done"], 1)
            values2_in_place(0)
            normalised(B - 1)
            group_rstd(2)
            pool.wait_ge(s["v2_done"], 3)
            with pool.Fori(1, B) as b:
                values2_in_place(b)

            for h in range(2):
                rstd(sum_sq[:], rms_eps, ve_rms[:], rs_rms[:], s["f_stat"], s["f_rstd"], s["f_var"], h)
                pool.wait_ge(s["x3_done"], 2 * (h + 1))
                pool.tensor_tensor(quarter(x, h), quarter(x, h), quarter(x2, h), ALU.add).then_inc(s["xs_ready"], 1)

        @block.scalar
        def _(act):
            nc_ = nc.scalar
            def bias_tanh(layer):
                act.wait_ge(s["bias_tanh_in"], layer + 1)
                nc_.activation(ht, hb, ACT.Tanh, scale=0.5).then_inc(s["bias_tanh"], 1)

            def norms(b):
                def queries(g):
                    act.wait_ge(s["q_proj"], 2 * b + g + 1)
                    nc_.activation(qsq[:, 4 * g:4 * g + 4], halves(sc[:, 1024 * g:1024 * (g + 1)], 4), ACT.Square).then_inc(s["qsq_ready"], 1)
                    nc_.copy(qt[:, b, 4 * g:4 * g + 4], halves(sc[:, 1024 * g:1024 * (g + 1)], 4)).then_inc(s["q_raw"], 1)

                nc_.preload_act_table(ACT.Sqrt)
                queries(0)
                act.wait_ge(s["k_proj"], b + 1)
                nc_.activation(ksq[:, 0:P - 1], oa[:, 0:P - 1], ACT.Square)
                nc_.activation(ksq[:, P:KEYS], oa[:, P:KEYS], ACT.Square).then_inc(s["ksq_ready"], 1)
                act.wait_ge(s["keo_done"], 2 * b)
                nc_.copy(kr[:, 0:P - 1], oa[:, 0:P - 1])
                nc_.copy(kr[:, P:KEYS], oa[:, P:KEYS]).then_inc(s["kr_ready"], 1)
                queries(1)
                act.wait_ge(s["kmax_ready"], b + 1)
                nc_.activation(ksr[:], kmx[:], ACT.Sqrt).then_inc(s["ksqrt_ready"], 1)
                act.wait_ge(s["qmax_ready"], b + 1)
                nc_.activation(qsr[:], qmx[:], ACT.Sqrt).then_inc(s["qsqrt_ready"], 1)

            bias_tanh(0)
            act.wait_ge(s["ld_cols"], 16)
            nc_.copy(kr[:, P - 1:P], cols[:, C_NK:C_NK + 1])
            nc_.activation(ksq[:, P - 1:P], cols[:, C_NK:C_NK + 1], ACT.Square)
            bias_tanh(1)
            norms(0)
            act.wait_ge(s["bias_top"], 1)
            nc_.activation(table[:, P - 1:P - 1 + S], mb[0:H, S:2 * S], ACT.Exp, bias=top[:, 3:4]).then_inc(s["table_ready"], 1)
            nc_.activation(null_row[:], zeros[0:H, :], ACT.Exp, bias=top[:, 0:1]).then_inc(s["null_ready"], 1)
            with act.Fori(1, B) as b:
                norms(b)

            act.wait_ge(s["shifts"], 1)
            nc_.preload_act_table(ACT.Exp)

            def group_read(i):
                first, n, at = GROUPS[i]
                act.wait_ge(s["qkv_done"], i + 1)
                group = halves(banks[:, at:at + 512 * n], n)
                nc_.copy(qk_raw[:, 0:n], group[:, :, 0:2 * D]).then_inc(s["raw_ready"], 1)
                nc_.copy(v2[:, first // T:(first + n) // T].rearrange("p b t h d -> p (b t) (h d)"), group[:, :, 2 * D:3 * D]).then_inc(s["v2_done"], 1)
                act.wait_ge(s["raw_ready"], i + 1)
                nc_.activation(sq2[:, 0:n], qk_raw[:, 0:n], ACT.Square).then_inc(s["sq2_ready"], 1)

            def group_roots(i):
                n = GROUPS[i][1]
                act.wait_ge(s["s64_ready"], i + 1)
                nc_.activation(r64[:, 0:n], v64[:, 0:n], ACT.Sqrt).then_inc(s["r64_ready"], 1)
                nc_.preload_act_table(ACT.Exp)

            def exps(b, last=False):
                def chunk(c):
                    act.wait_ge(s["qk_chunk"], 6 * b + c + 1)
                    if not (isinstance(b, int) and b == 0):
                        act.wait_ge(s["z_done"], 2 * b - 1 + c // 3)
                    nc_.activation(pb[c], sc[:, 1024 * (c % 2):1024 * (c % 2 + 1)], ACT.Exp,
                                   bias=shift1[:, 3:4]).then_inc(s["exp_done"], 1)

                def evacuate(g):
                    act.wait_ge(s["pv_done"], 2 * b + g + 1)
                    act.wait_ge(s["on_ready"], b)
                    nc_.copy(o_raw[:, 4 * g:4 * g + 4], halves(oa, 4)).then_inc(s["o_evac"], 1)

                chunk(0)
                chunk(1)
                act.wait_ge(s["qk_x"], b + 1)
                nc_.activation(px[0:2], mb[0:2, 0:32].rearrange("p (e m q) -> p e m q", e=2, m=M), ACT.Exp,
                               bias=shift1[0:2, 3:4]).then_inc(s["px_exp"], 1)
                chunk(2)
                chunk(3)
                evacuate(0)
                if last:
                    group_read(0)
                chunk(4)
                chunk(5)
                if last:
                    group_roots(0)
                evacuate(1)

            exps(0)
            with act.Fori(1, B - 1) as b:
                exps(b)
            exps(B - 1, True)

            def chunk2(b, c):
                act.wait_ge(s["qk2_chunk"], 6 * b + c + 1)
                if not (isinstance(b, int) and b == 0):
                    act.wait_ge(s["pv2_done"], 2 * b - 1 + c // 3)
                nc_.activation(pb[c], sc[:, 1024 * SLOT[c]:1024 * (SLOT[c] + 1)], ACT.Exp, bias=shift2[:, 3:4]).then_inc(s["exp2_done"], 1)

            def evacuate2(b, g):
                act.wait_ge(s["pv2_done"], 2 * b + g + 1)
                act.wait_ge(s["o2_turned"], b)
                nc_.copy(o2s[:, g], oa[:, 512 * g:512 * (g + 1)]).then_inc(s["o2_evac"], 1)

            def turned(b):
                act.wait_ge(s["ao_turned"], b + 1)
                nc_.copy(aoT[:], tm[:, 0:S]).then_inc(s["aoT_ready"], 1)

            def second_group(b, group=None):
                chunk2(b, 3)
                if group:
                    group_read(group)
                    group_roots(group)
                chunk2(b, 4)
                evacuate2(b, 0)
                chunk2(b, 5)
                evacuate2(b, 1)

            for c in range(3):
                chunk2(0, c)
            second_group(0, 1)
            group_read(2)
            group_roots(2)
            with act.Fori(1, B) as b:
                for c in range(3):
                    chunk2(b, c)
                turned(b - 1)
                second_group(b)

            def unit(b, n, out, func=ACT.Gelu, scale=1.0, width=512):
                act.wait_ge(s["u_done"], 8 * b + n + 1)
                src = sc[:, 512 * (n % 4):512 * (n % 4) + width]
                nc_.activation(out, src if width < 512 else halves(src, 2), func, scale=scale).then_inc(s["u_act"], 1)

            def first_units(b):
                unit(b, 0, h2a)
                unit(b, 1, h3a, width=S)
                act.wait_ge(s["down_done"], 2 * b)
                unit(b, 2, h0)
                unit(b, 3, h2b)

            def last_units(b):
                unit(b, 4, th1, ACT.Tanh, 0.5)
                unit(b, 6, h3b)
                unit(b, 7, h2c)

            nc_.preload_act_table(ACT.Gelu)
            first_units(0)
            turned(B - 1)
            last_units(0)
            act.wait_ge(s["gates"], 7)
            nc_.activation(ga[2][:], lg[:], ACT.Exp).then_inc(s["gate_exp"], 1)
            nc_.preload_act_table(ACT.Gelu)
            with act.Fori(1, B) as b:
                first_units(b)
                last_units(b)

        @block.vector
        def _(dve):
            v = nc.vector
            n = [0]

            def step(ins):
                n[0] += 1
                ins.then_inc(s["bias_dve"], 1)
                dve.wait_ge(s["bias_dve"], n[0])

            def row(r, width=D):
                return rows[:, r:r + width]

            step(v.memset(pair_rows[:], 0.0))
            for g in range(2):
                for e in range(2):
                    v.memset(pair_rows[DH * e:DH * (e + 1), g, 2 * g + e:2 * g + e + 1], 1.0)
            def bias_stats():
                for t in range(T):
                    last = v.bn_stats(bst[:, t], hb[:, t])
                step(last)
                for t in range(T):
                    last = v.bn_aggr(bmv[:, t], bst[:, t])
                last.then_inc(s["bias_var"], 1)

            def bias_norm(layer, gain):
                dve.wait_ge(s["bias_rstd"], layer + 1)
                for t in range(T):
                    last = v.tensor_scalar(hb[:, t], hb[:, t], bmv[:, t, 0:1], brs[:, t:t + 1], ALU.subtract, ALU.mult)
                step(last)
                v.tensor_tensor(hb, hb, row(gain)[:, None, :].to_broadcast([P, T, D]), ALU.mult).then_inc(s["bias_tanh_in"], 1)

            def bias_silu(layer):
                dve.wait_ge(s["bias_tanh"], layer + 1)
                v.scalar_tensor_tensor(hb, ht, 1.0, hb, ALU.add, ALU.mult).then_inc(s["bias_turn_in"], 1)

            def bias_transposed(layer):
                dve.wait_ge(s["bias_turned"], layer + 1)
                v.tensor_scalar(hT[:], mb[:, 0:S], 0.5, None, ALU.mult).then_inc(s["bias_hT"], 1)

            def transposed(h):
                dve.wait_ge(s["xt_done"], h + 1)
                gain = cols[:, C_GN:C_GN + 1]
                src = halves(sc[:, 512 * h:512 * (h + 1)], T)
                dst = xk[:, T * h:T * (h + 1)]
                v.tensor_scalar(xb[:, T * h:T * (h + 1)], src, gain, None, ALU.mult)
                v.tensor_scalar(dst[:, :, 0:P - 1], src[:, :, P - 2::-1], gain, None, ALU.mult)
                v.tensor_scalar(dst[:, :, P:S], src[:, :, S - 2:P - 2:-1], gain, None, ALU.mult)
                v.tensor_scalar(dst[:, :, S:KEYS], src[:, :, S - 1:S], gain, None, ALU.mult).then_inc(s["xb_ready"], 1)

            def values(h):
                dve.wait_ge(s["v_proj"], h + 1)
                for i in range(T):
                    b, at = T * h + i, 512 * h + 3 * DH * i
                    v.tensor_tensor(vn[:, b, 0:2], halves(oa[:, at:at + 2 * DH], 2), mask[:, b, 0:2, None].to_broadcast([P, 2, DH]), ALU.mult)
                    last = v.tensor_tensor(vn[0:2, b, 2:3], oa[0:2, None, at + 2 * DH:at + 3 * DH], mask[0:2, b, 2:3, None].to_broadcast([2, 1, DH]),
                                           ALU.mult)
                last.then_inc(s["vn_done"], 1)

            dve.wait_ge(s["ld_rows"], 16)
            dve.wait_ge(s["pos_ready"], 1)
            for t in range(T):
                last = v.scalar_tensor_tensor(hb[:, t], row(R_W0), pos[:, t:t + 1], row(R_B0), ALU.mult, ALU.add)
            step(last)
            bias_stats()
            dve.wait_ge(s["ld_x"], 16)
            for t in range(B * T):
                last = v.bn_stats(st_x[:, t], x[:, t])
            last.then_inc(s["x_parts"], 1)
            dve.wait_ge(s["x_parts"], 1)
            for t in range(B * T):
                last = v.bn_aggr(mv_x[:, t], st_x[:, t])
            last.then_inc(s["x_stat"], 1)
            bias_norm(0, R_G0)
            dve.wait_ge(s["x_rstd"], 1)
            for t in range(B * T):
                v.tensor_scalar(xc[:, t], x[:, t], mv_x[:, t, 0:1], rs_x[:, t:t + 1], ALU.subtract, ALU.mult).then_inc(s["xc_ready"], 1)
            bias_silu(0)
            dve.wait_ge(s["ld_cols"], 16)
            dve.wait_ge(s["zeroed"], 1)
            transposed(0)
            bias_transposed(0)
            transposed(1)
            dve.wait_ge(s["bias_mm1"], 1)
            step(v.tensor_tensor(hb, halves(zb[:, 0:S], T), row(R_B1)[:, None, :].to_broadcast([P, T, D]), ALU.add))
            bias_stats()
            dve.wait_ge(s["ld_mask"], 16)
            v.tensor_copy(mask[:], mask_u8[:]).then_inc(s["mask_ready"], 1)
            dve.wait_ge(s["mask_ready"], 1)
            values(0)
            bias_norm(1, R_G1)
            values(1)
            for sh, (rq, rk, width), bound in ((shift1, (R_QS, R_KS, DH), 8.0), (shift2, (R_QN, R_KN, HD), HD ** 0.5)):
                for i, r in enumerate((rq, rk)):
                    last = v.tensor_reduce(sh[:, i:i + 1], row(r, width), AX.X, ALU.max, apply_absolute_value=True)
                step(last)
                step(v.tensor_tensor(sh[:, 2:3], sh[:, 0:1], sh[:, 1:2], ALU.mult))
                v.tensor_scalar(sh[:, 3:4], sh[:, 2:3], -bound, ROOM, ALU.mult, ALU.add)
            v.scalar_tensor_tensor(gain2[:], row(R_QN, HD), HD ** -0.5, row(R_KN, HD), ALU.mult, ALU.mult)
            step(v.scalar_tensor_tensor(qk_scale[:], cols[:, C_QS:C_QS + 1], 8.0, cols[:, C_KS:C_KS + 1], ALU.mult, ALU.mult))
            v.memset(zmx[:], 1.0).then_inc(s["shifts"], 1)

            def inverses(b):
                dve.wait_ge(s["kss_done"], b + 1)
                v.tensor_scalar(kmx[:], oa[:, 512:512 + KEYS], 1e-24, None, ALU.max).then_inc(s["kmax_ready"], 1)
                dve.wait_ge(s["qss_done"], 2 * b + 2)
                v.tensor_scalar(qmx[:], zb[:, 0:S], 1e-24, None, ALU.max).then_inc(s["qmax_ready"], 1)
                dve.wait_ge(s["ksqrt_ready"], b + 1)
                v.reciprocal(kin[:], ksr[:]).then_inc(s["kin_ready"], 1)
                dve.wait_ge(s["consts"], 1)
                dve.wait_ge(s["qsqrt_ready"], b + 1)
                v.reciprocal(qin[:, b], qsr[:]).then_inc(s["qinv_ready"], 1)
                dve.wait_ge(s["kr_ready"], b + 1)
                dve.wait_ge(s["kin_ready"], b + 1)
                for e in range(2):
                    r = slice(DH * e, DH * (e + 1))
                    v.scalar_tensor_tensor(keo[r, b, e], kr[r, :], qk_scale[r, 0:1], kin[r, :], ALU.mult, ALU.mult).then_inc(s["keo_done"], 1)

            inverses(0)
            bias_silu(1)
            bias_transposed(1)
            dve.wait_ge(s["ld_small"], 16)
            dve.wait_ge(s["bias_mm2"], 1)
            v.tensor_reduce(top[:, 0:1], mb[0:H, S:2 * S], AX.X, ALU.max)
            step(v.tensor_tensor(top[:, 1:2], small[:, 1:2], small[:, 0:1], ALU.subtract))
            step(v.tensor_tensor(top[:, 2:3], top[:, 0:1], top[:, 1:2], ALU.max))
            v.tensor_scalar(top[:, 3:4], top[:, 2:3], -1.0, None, ALU.mult)
            v.tensor_tensor(top[:, 0:1], top[:, 1:2], top[:, 2:3], ALU.subtract).then_inc(s["bias_top"], 1)
            with dve.Fori(1, B) as b:
                inverses(b)

            dve.wait_ge(s["bias_loaded"], 16 * 10)

            n_sq = [0]

            def square_sums(first, n, stat):
                part = x2[:, first:first + n]
                v.tensor_tensor(sq_x[:, 0:n], part, part, ALU.mult).then_inc(s["sq_x_ready"], 1)
                n_sq[0] += 1
                dve.wait_ge(s["sq_x_ready"], n_sq[0])
                v.tensor_reduce(sum_sq[:, 0:n, None], sq_x[:, 0:n], AX.X, ALU.add).then_inc(stat, 1)

            def over_rms(first, n, ready):
                v.tensor_tensor(xc[:, first:first + n], x2[:, first:first + n], rs_rms[:, 0:n, None].to_broadcast([P, n, D]),
                                ALU.mult).then_inc(ready, 1)

            def group_sums(i):
                first, n, _ = GROUPS[i]
                dve.wait_ge(s["x2_done"], (first + n) // T)
                square_sums(first, n, s["r_stat"])

            def group_scaled(i):
                first, n, _ = GROUPS[i]
                dve.wait_ge(s["r_rstd"], i + 1)
                over_rms(first, n, s["h2_ready"])

            def group_gain(i):
                n = GROUPS[i][1]
                dve.wait_ge(s["h2_turned"], i + 1)
                v.tensor_scalar(hT2[:, 0:D * n], (zb if i else mb)[:, 0:D * n], cols[:, C_N1:C_N1 + 1], D ** 0.5, ALU.mult, ALU.mult).then_inc(s["hT2_ready"], 1)

            def group_head_sums(i):
                n = GROUPS[i][1]
                dve.wait_ge(s["sq2_ready"], i + 1)
                v.tensor_reduce(s64[:, 0:n], sq2[:, 0:n].rearrange("p t (h d) -> p t h d", d=HD), AX.X, ALU.add).then_inc(s["p3_dve"], 1)
                dve.wait_ge(s["p3_dve"], 2 * i + 1)
                v.tensor_scalar(v64[:, 0:n], s64[:, 0:n], 1.0 / HD, EPS, ALU.mult, ALU.add).then_inc(s["s64_ready"], 1)

            def group_normalised(i):
                first, n, _ = GROUPS[i]
                dve.wait_ge(s["r64_ready"], i + 1)
                v.reciprocal(i64[:, 0:n], r64[:, 0:n]).then_inc(s["p3_dve"], 1)
                dve.wait_ge(s["p3_dve"], 2 * i + 2)
                for w in range(2):
                    last = v.tensor_tensor(qkn[:, w, first:first + n].rearrange("p t (h d) -> p t h d", d=HD),
                                           qk_raw[:, 0:n, D * w:D * (w + 1)].rearrange("p t (h d) -> p t h d", d=HD),
                                           i64[:, 0:n, H * w:H * (w + 1), None].to_broadcast([P, n, H, HD]), ALU.mult)
                last.then_inc(s["qkn_ready"], 1)
                dve.wait_ge(s["qkn_ready"], i + 1)

            def weigh(b, tail, last=False):
                def chunk(c):
                    g, k = divmod(c, 3)
                    dve.wait_ge(s["exp_done"], 6 * b + c + 1)
                    if k < 2:
                        p, w = pb[c].rearrange("p (e m i) -> p e m i", e=2, m=2), eb0[:, :, 4 * g + 2 * k:4 * g + 2 * k + 2]
                    else:
                        p, w = pb[c].rearrange("p (e m i) -> p e m i", e=2, m=4), eb1[:, :, 4 * g:4 * g + 4]
                    v.tensor_tensor(p, p, w, ALU.mult).then_inc(s["mult_done"], 1)

                chunk(0)
                chunk(1)
                dve.wait_ge(s["px_exp"], b + 1)
                v.tensor_tensor(px[0:2], px[0:2], ebx[:], ALU.mult).then_inc(s["px_ready"], 1)
                if last:
                    group_sums(0)
                chunk(2)
                if last:
                    group_scaled(0)
                chunk(3)
                if last:
                    group_gain(0)
                    group_head_sums(0)
                chunk(4)
                chunk(5)
                if tail:
                    norm_y(b - 1)
                if last:
                    group_normalised(0)
                    split(0)
                dve.wait_ge(s["z_done"], 2 * b + 2)
                v.tensor_scalar(zmx[:], zb[:, 0:S], 1e-37, None, ALU.max).then_inc(s["zmax_done"], 1)
                dve.wait_ge(s["zmax_done"], b + 1)
                dve.wait_ge(s["zinv_stored"], 16 * b)
                v.reciprocal(zin[:], zmx[:]).then_inc(s["zinv_ready"], 1)

            def norm_y(b):
                dve.wait_ge(s["y_done"], b + 1)
                for t in range(T):
                    last = v.bn_stats(st[:, t], mb[:, S + D * t:S + D * (t + 1)])
                last.then_inc(s["y_parts"], 1)
                dve.wait_ge(s["consts"], 1)
                dve.wait_ge(s["y_parts"], b + 1)
                for t in range(T):
                    last = v.bn_aggr(mv[:, t], st[:, t])
                last.then_inc(s["y_stat"], 1)
                dve.wait_ge(s["y_rstd"], b + 1)
                for t in range(T):
                    last = v.tensor_scalar(yn[:, t], mb[:, S + D * t:S + D * (t + 1)], mv[:, t, 0:1], rs[:, t:t + 1], ALU.subtract, ALU.mult)
                last.then_inc(s["y_norm"], 1)
                dve.wait_ge(s["y_norm"], b + 1)
                v.tensor_tensor(tiles(x2, b), yn[:], row(R_GO)[:, None, :].to_broadcast([P, T, D]), ALU.mult).then_inc(s["x2_done"], 1)

            v.memset(v2f[:, :, :, HD:HD + 1], 1.0).then_inc(s["p4_dve"], 1)

            def split(b):
                q, k = (tiles(qkn[:, w], b).rearrange("p t (h d) -> p (t h) d", d=HD) for w in range(2))
                kg, pq, pk = rest[:, 0], parts[:, 0], parts[:, 1]
                n = [0]

                def part(ins):
                    ins.then_inc(s["part_done"], 1)
                    n[0] += 1
                    return n[0]

                def after(i):
                    dve.wait_ge(s["part_done"], PART_STEPS * b + i)

                def times(a, n):
                    return a[:, :, None, :].to_broadcast([P, T * H, n, HD])

                dve.wait_ge(s["parts_turned"], 2 * b)
                k_scaled = part(v.tensor_tensor(kg, k, gain2[:, None, :].to_broadcast([P, T * H, HD]), ALU.mult))
                q1 = part(v.tensor_copy(pq[:, :, 0:3], times(q, 3)))
                after(k_scaled)
                k1 = part(v.tensor_copy(pk[:, :, 2:5], times(kg, 3)))
                after(q1)
                q_less_1 = part(v.tensor_tensor(rest[:, 1], q, pq[:, :, 0], ALU.subtract))
                after(k1)
                k_less_1 = part(v.tensor_tensor(rest[:, 2], kg, pk[:, :, 2], ALU.subtract))
                after(q_less_1)
                q2 = part(v.tensor_copy(pq[:, :, 3:6:2], times(rest[:, 1], 2)))
                after(k_less_1)
                k2 = part(v.tensor_copy(pk[:, :, 1:6:4], times(rest[:, 2], 2)))
                after(q2)
                part(v.tensor_tensor(pq[:, :, 4], rest[:, 1], pq[:, :, 3], ALU.subtract))
                after(k2)
                v.tensor_tensor(pk[:, :, 0], rest[:, 2], pk[:, :, 1], ALU.subtract).then_inc(s["parts_ready"], 1)
                assert n[0] == PART_STEPS

            weigh(0, False)
            with dve.Fori(1, B - 1) as b:
                weigh(b, True)
            weigh(B - 1, True, True)

            def operands_out(b, g):
                dve.wait_ge(s["parts_turned"], 2 * b + g + 1)
                v.tensor_copy(qT2[:, 4 * g:4 * g + 4], halves(turned_bf[:, 0:1024], 4))
                for e in range(2):
                    r = slice(DH * e, DH * (e + 1))
                    last = v.tensor_copy(kT2[r, e, 4 * g:4 * g + 4], halves(turned_bf[r, 1024:2048], 4))
                last.then_inc(s["operands2_ready"], 1)

            def weighted_outputs(b):
                dve.wait_ge(s["o2_turned"], b + 1)
                view = tm.rearrange("p (n r k) -> p n r k", n=2 * 4, r=4)
                v.reciprocal(rz2[:], view[:, :, :, HD:HD + 1]).then_inc(s["p4_dve"], 1)
                dve.wait_ge(s["p4_dve"], b + 2)
                v.tensor_tensor(ao[:].rearrange("p t (g r d) -> p (t g) r d", g=4, r=4), view[:, :, :, 0:HD],
                                rz2[:].to_broadcast([P, 2 * 4, 4, HD]), ALU.mult).then_inc(s["ao_ready"], 1)

            def add_attention(b):
                dve.wait_ge(s["wo_done"], b + 1)
                v.tensor_tensor(tiles(x2, b)[:, :, OFF:D], tiles(x2, b)[:, :, OFF:D],
                                halves(tm[:, 512:512 + T * DN], T), ALU.add).then_inc(s["x3_done"], 1)

            dve.wait_ge(s["operands_zeroed"], 1)
            operands_out(0, 0)
            operands_out(0, 1)
            group_sums(1)
            group_scaled(1)
            split(1)
            group_gain(1)
            operands_out(1, 0)
            group_head_sums(1)
            group_normalised(1)
            operands_out(1, 1)
            norm_y(B - 1)
            group_sums(2)
            group_scaled(2)
            group_gain(2)
            group_head_sums(2)
            group_normalised(2)
            with dve.Fori(1, B - 1) as b:
                split(b + 1)
                weighted_outputs(b - 1)
                operands_out(b + 1, 0)
                add_attention(b - 1)
                operands_out(b + 1, 1)
            weighted_outputs(B - 2)
            add_attention(B - 2)

            def gate_inputs(h, turned, logits):
                dve.wait_ge(s["x3_done"], 2 * h + 2)
                square_sums(4 * h, 4, s["f_stat"])
                dve.wait_ge(s["f_rstd"], h + 1)
                over_rms(4 * h, 4, s["f_ready"])
                dve.wait_ge(s["f_turned"], h + 1)
                v.tensor_scalar(xfT[:, 2 * h:2 * h + 2], halves(turned, 2), cols[:, C_N2:C_N2 + 1], D ** 0.5, ALU.mult, ALU.mult).then_inc(s["xfT_ready"], 1)
                dve.wait_ge(s["gate_done"], h + 1)
                v.tensor_copy(quarter(lg, h), halves(logits, 4)).then_inc(s["lg_ready"], 1)

            def silu_expert(b):
                dve.wait_ge(s["u_act"], 7 * b + 5)
                v.scalar_tensor_tensor(si1, th1, 1.0, halves(sc[:, 0:512], 2), ALU.add, ALU.mult).then_inc(s["silu_a"], 1)
                dve.wait_ge(s["silu_a"], b + 1)
                dve.wait_ge(s["u_done"], 8 * b + 6)
                dve.wait_ge(s["down_done"], 2 * b)
                v.tensor_tensor(h1, si1, halves(sc[:, 512:1024], 2), ALU.mult).then_inc(s["h1_ready"], 1)

            gate_inputs(0, sc[:, 0:512], oa[:, 512:512 + 4 * E])
            weighted_outputs(B - 1)
            silu_expert(0)
            add_attention(B - 1)
            gate_inputs(1, zb, mb[:, 0:4 * E])

            m = [0]

            def gate(ins):
                m[0] += 1
                ins.then_inc(s["gates"], 1)
                dve.wait_ge(s["gates"], m[0])

            NT = B * T
            dve.wait_ge(s["lg_ready"], 2)
            clean, num, prob, sel, wts, isn = ga
            gate(v.tensor_scalar(num[:], lg[:], 3.4028235e38, -3.4028235e38, ALU.min, ALU.max))
            gate(v.tensor_tensor(isn[:].bitcast(mybir.dt.int32), lg[:], lg[:], ALU.is_equal))
            gate(v.memset(clean[:], 0.0))
            gate(v.copy_predicated(clean[:], isn[:].bitcast(mybir.dt.int32), num[:]))
            gate(v.tensor_reduce(g1[0][:], clean[:], AX.X, ALU.max))
            gate(v.tensor_tensor(num[:], clean[:], g1[0][:, :, None].to_broadcast([P, NT, E]), ALU.subtract))
            gate(v.tensor_copy(lg[:], num[:]))
            dve.wait_ge(s["gate_exp"], 1)
            gate(v.tensor_reduce(g1[1][:], prob[:], AX.X, ALU.add))
            gate(v.reciprocal(g1[2][:], g1[1][:]))
            gate(v.tensor_tensor(sel[:], prob[:], g1[2][:, :, None].to_broadcast([P, NT, E]), ALU.mult))
            mine = sel[:, :, :, None].to_broadcast([P, NT, E, E])
            other = sel[:, :, None, :].to_broadcast([P, NT, E, E])
            before = tri[:, None, :, :].to_broadcast([P, NT, E, E])
            gate(v.tensor_tensor(gc[0][:], other, mine, ALU.is_gt))
            gate(v.tensor_tensor(gc[1][:], other, mine, ALU.is_equal))
            gate(v.tensor_tensor(gc[2][:], gc[1][:], before, ALU.mult))
            gate(v.tensor_tensor(gc[1][:], gc[0][:], gc[2][:], ALU.add))
            gate(v.tensor_reduce(num[:], gc[1][:], AX.X, ALU.add))
            gate(v.scalar_tensor_tensor(clean[:], num[:], 2.0, sel[:], ALU.is_lt, ALU.mult))
            gate(v.tensor_reduce(g1[0][:], clean[:], AX.X, ALU.add))
            gate(v.tensor_scalar(g1[1][:], g1[0][:], 1e-8, None, ALU.add))
            gate(v.reciprocal(g1[2][:], g1[1][:]))
            gate(v.tensor_tensor(wts[:], clean[:], g1[2][:, :, None].to_broadcast([P, NT, E]), ALU.mult))
            gate(v.tensor_scalar(wts[:, :, 1:2], wts[:, :, 1:2], 0.5, None, ALU.mult))

            def add_experts(b):
                for t in range(T):
                    dve.wait_ge(s["down_done"], 2 * b + t + 1)
                    for i in range(E):
                        dst = x[:, T * b + t, OFF:D]
                        last = v.scalar_tensor_tensor(dst, oa[:, 512 * t + DN * i:512 * t + DN * (i + 1)],
                                                      wts[:, T * b + t, i:i + 1], dst, ALU.mult, ALU.add)
                        last.then_inc(s["res_part"], 1)
                        dve.wait_ge(s["res_part"], 8 * b + 4 * t + i + 1)
                v.tensor_copy(g1[3][:, 0:1], g1[0][:, 0:1]).then_inc(s["res_done"], 1)

            dve.wait_ge(s["xs_ready"], 2)
            add_experts(0)
            with dve.Fori(1, B) as b:
                silu_expert(b)
                add_experts(b)

        @block.tensor
        def _(pe):
            mm, turn = nc.tensor.matmul, nc.tensor.transpose
            def bias_turn(layer):
                pe.wait_ge(s["bias_turn_in"], layer + 1)
                for t in range(T):
                    last = turn(mb[:, D * t:D * (t + 1)], hb[:, t], ident[:])
                last.then_inc(s["bias_turned"], 1)

            def values_of(h):
                pe.wait_ge(s["xb_ready"], h + 1)
                wv = wa[:, A_V:A_V + DH]
                for i in range(T):
                    xkb, at = xk[:, T * h + i], 512 * h + 3 * DH * i
                    mm(oa[:, at:at + DH], xkb[:, 0:P], wv, start=True, stop=False)
                    mm(oa[:, at:at + DH], last_row[:], rows[0:1, R_NV:R_NV + DH], start=False, stop=True)
                    mm(oa[:, at + DH:at + 2 * DH], xkb[:, P:2 * P], wv, start=True, stop=True)
                    last = mm(oa[0:2, at + 2 * DH:at + 3 * DH], xkb[:, S - 1:KEYS], wv, start=True, stop=True)
                last.then_inc(s["v_proj"], 1)

            pe.wait_ge(s["consts"], 1)
            for h in range(2):
                pe.wait_ge(s["xc_ready"], 4 * (h + 1))
                for t in range(4 * h, 4 * h + 4):
                    last = turn(sc[:, D * t:D * (t + 1)], xc[:, t], ident[:])
                last.then_inc(s["xt_done"], 1)
            bias_turn(0)
            pe.wait_ge(s["ld_wa"], 16)
            pe.wait_ge(s["ld_rows"], 16)
            values_of(0)
            pe.wait_ge(s["bias_hT"], 1)
            for t in range(T):
                last = mm(zb[:, D * t:D * (t + 1)], hT[:, P * t:P * (t + 1)], wa[:, A_W1:A_W1 + D], start=True, stop=True)
            last.then_inc(s["bias_mm1"], 1)
            values_of(1)

            def project(b):
                def queries(g):
                    if not (isinstance(b, int) and b == 0):
                        pe.wait_ge(s["q_raw"], 2 * b - 1 + g)
                    for m in range(4 * g, 4 * g + 4):
                        last = mm(sc[:, S * m:S * (m + 1)], wa[:, A_Q + P * m:A_Q + P * (m + 1)], xb[:, b], start=True, stop=True)
                    last.then_inc(s["q_proj"], 1)

                def query_sums(g):
                    pe.wait_ge(s["qsq_ready"], 2 * b + g + 1)
                    for r in range(4):
                        last = mm(zb[32 * r:32 * (r + 1), 0:S], pair_rows[:, g], qsq[:, 4 * g + r], start=(g == 0), stop=(g == 1))
                    last.then_inc(s["qss_done"], 1)

                queries(0)
                pe.wait_ge(s["kr_ready"], b)
                mm(oa[:, 0:KEYS], wa[:, A_KK:A_KK + P], xk[:, b], start=True, stop=True).then_inc(s["k_proj"], 1)
                queries(1)
                pe.wait_ge(s["ksq_ready"], b + 1)
                pe.wait_ge(s["kmax_ready"], b)
                mm(oa[:, 512:512 + KEYS], half_ones[:], ksq[:], start=True, stop=True).then_inc(s["kss_done"], 1)
                pe.wait_ge(s["qmax_ready"], b)
                query_sums(0)
                query_sums(1)

            pe.wait_ge(s["vn_done"], T)
            project(0)
            bias_turn(1)
            pe.wait_ge(s["bias_hT"], 2)
            mm(mb[0:H, S:2 * S], wa[:, A_W2:A_W2 + H], hT[:], start=True, stop=True).then_inc(s["bias_mm2"], 1)
            with pe.Fori(1, B) as b:
                project(b)

            def scores(b, c):
                g, k = divmod(c, 3)
                if not (isinstance(b, int) and 6 * b + c < 2):
                    pe.wait_ge(s["exp_done"], 6 * b + c - 1)
                for e in range(2):
                    if k < 2:
                        m0 = 4 * g + 2 * k
                        lhs, rhs = kf[:, e, 0:P], qt[:, b, m0:m0 + 2]
                    else:
                        lhs, rhs = kf[:, e, P:2 * P], qt[:, b, 4 * g:4 * g + 4, P:S]
                    out = sc[:, 1024 * (c % 2) + 512 * e:1024 * (c % 2) + 512 * (e + 1)]
                    last = mm(out.rearrange("p (m i) -> p m i", m=rhs.shape[1]), lhs, rhs, start=True, stop=True)
                last.then_inc(s["qk_chunk"], 1)

            def extra_scores(b):
                if not (isinstance(b, int) and b < 2):
                    pe.wait_ge(s["y_norm"], b - 1)
                for e in range(2):
                    last = mm(mb[0:2, 16 * e:16 * (e + 1)].rearrange("p (m q) -> p m q", q=2), kf[:, e, S - 1:KEYS],
                              qt[:, b, :, P - 1:S:P], start=True, stop=True)
                last.then_inc(s["qk_x"], 1)

            def values(b, g):
                pe.wait_ge(s["mult_done"], 6 * b + 3 * g + 3)
                pe.wait_ge(s["px_ready"], b + 1)
                pe.wait_ge(s["vf_ready"], b + 1)
                pe.wait_ge(s["o_evac"], 2 * b + g)
                late = pb[3 * g + 2].rearrange("p (e m i) -> p e m i", e=2, m=4)
                for k in range(2):
                    for part in range(3):
                        for e in range(2):
                            out = oa[DH * e:DH * (e + 1), 512 * k:512 * (k + 1)]
                            by_pair = out.rearrange("p (m i) -> p m i", m=2)
                            if part == 0:
                                rhs = pb[3 * g + k][:, 512 * e:512 * (e + 1)]
                            elif part == 1:
                                out, rhs = by_pair[:, :, P:S], late[:, e, 2 * k:2 * k + 2]
                            else:
                                out, rhs = by_pair[:, :, P - 1:S:P], px[:, e, 4 * g + 2 * k:4 * g + 2 * k + 2]
                            last = mm(out, vf[:, part], rhs, start=(part == 0), stop=(part == 2))
                last.then_inc(s["pv_done"], 1)

            def sums(b, g):
                if g == 0:
                    pe.wait_ge(s["zmax_done"], b)
                late = pb[3 * g + 2].rearrange("p (e m i) -> p e m i", e=2, m=4)
                for e in range(2):
                    for part in range(3):
                        for r in range(4):
                            out = zb[32 * r:32 * (r + 1), 0:S]
                            if part == 0:
                                rhs = pb[3 * g + r // 2][:, 512 * e + S * (r % 2):512 * e + S * (r % 2 + 1)]
                            elif part == 1:
                                out, rhs = out[:, P:S], late[:, e, r]
                            else:
                                out, rhs = out[:, P - 1:S:P], px[:, e, 4 * g + r]
                            last = mm(out, ocm[:, part, 2 * g + e], rhs, start=(g == 0 and e == 0 and part == 0),
                                      stop=(g == 1 and e == 1 and part == 2), skip_group_check=True)
                last.then_inc(s["z_done"], 1)

            def out_product(b):
                pe.wait_ge(s["on_ready"], b + 1)
                for t in range(T):
                    for m in range(M):
                        last = mm(mb[:, S + D * t:S + D * (t + 1)], on[:, m, P * t:P * (t + 1)],
                                  wa[:, A_O + D * m:A_O + D * (m + 1)], start=(m == 0), stop=(m == M - 1))
                last.then_inc(s["y_done"], 1)

            def project2(i):
                first, n, at = GROUPS[i]
                pe.wait_ge(s["h2_ready"], i + 1)
                for t in range(n):
                    last = turn((zb if i else mb)[:, D * t:D * (t + 1)], xc[:, first + t], ident[:])
                last.then_inc(s["h2_turned"], 1)
                pe.wait_ge(s["hT2_ready"], i + 1)
                for t in range(n):
                    last = mm(banks[:, at + 512 * t:at + 512 * t + 3 * D], hT2[:, P * t:P * (t + 1)], wb[:, W_QKV:W_QKV + 3 * D], start=True, stop=True)
                last.then_inc(s["qkv_done"], 1)

            def attend(b, tail, last=False):
                pe.wait_ge(s["q_done"], b + 1)
                pe.wait_ge(s["kf_ready"], b + 1)
                scores(b, 0)
                scores(b, 1)
                extra_scores(b)
                scores(b, 2)
                scores(b, 3)
                values(b, 0)
                sums(b, 0)
                if last:
                    pe.wait_ge(s["ld_wb"], 16)
                    pe.wait_ge(s["px_exp"], b + 1)
                    pe.wait_ge(s["exp_done"], 6 * b + 4)
                    project2(0)
                    pe.wait_ge(s["v2_done"], 1)
                scores(b, 4)
                scores(b, 5)
                if tail:
                    out_product(b - 1)
                values(b, 1)
                sums(b, 1)

            pe.wait_ge(s["q_raw"], 2 * B)
            attend(0, False)
            with pe.Fori(1, B - 1) as b:
                attend(b, True)
            attend(B - 1, True, True)

            def turn_parts(b, g):
                pe.wait_ge(s["parts_ready"], b + 1)
                if not (isinstance(b, int) and b == 0):
                    pe.wait_ge(s["exp2_done"], 6 * b - 4 + 3 * g)
                elif g:
                    pe.wait_ge(s["operands2_ready"], 1)
                for w in range(2):
                    by_token = parts[:, w].rearrange("p (t h) s d -> p t (h s d)", t=T)
                    for m in range(4):
                        for t in range(T):
                            at = 1024 * w + S * m + P * t
                            last = turn(turned_bf[:, at:at + P], by_token[:, t, P * (4 * g + m):P * (4 * g + m + 1)], ident_bf[:])
                last.then_inc(s["parts_turned"], 1)

            def scores2(b, c, following=True):
                g, k = divmod(c, 3)
                start = isinstance(b, int) and b == 0
                if c == 0:
                    pe.wait_ge(s["operands2_ready"], 2 * b + 1)
                    if not start:
                        pe.wait_ge(s["exp2_done"], 6 * b)
                elif c == 1:
                    pe.wait_ge(s["operands2_ready"], 2 * b + 2)
                elif c == 4 and following:
                    pe.wait_ge(s["operands2_ready"], 2 * b + 3)
                else:
                    pe.wait_ge(s["exp2_done"], 6 * b + {2: 1, 3: 3, 4: 2, 5: 4}[c])
                at = 1024 * SLOT[c]
                n = 4 if k < 2 else 8
                wide = 1024 // n
                for i in range(n):
                    m, e = divmod(8 * g + (4 * k if k < 2 else 0) + i, 2)
                    if k < 2:
                        lhs, rhs = kT2[:, e, m, 0:P], qT2[:, m]
                    else:
                        lhs, rhs = kT2[:, e, m, P:S], qT2[:, m, P:S]
                    mm(sc[:, at + wide * i:at + wide * (i + 1)], lhs, rhs, start=(i % (n // 2) == 0), stop=False, skip_group_check=True)
                for j in range(2):
                    bank = halves(sc[:, at + 512 * j:at + 512 * (j + 1)], n // 2)
                    last = mm(bank[:, :, 0:P], ident_bf[:], later_bf[:, None, :].to_broadcast([P, n // 2, P]), start=False, stop=True,
                              skip_group_check=True)
                last.then_inc(s["qk2_chunk"], 1)

            def values2(b, g):
                pe.wait_ge(s["exp2_done"], 6 * b + 3 * g + 3)
                pe.wait_ge(s["v2f_ready"], b + 1)
                pe.wait_ge(s["p4_dve"], 1)
                if not (isinstance(b, int) and b == 0):
                    pe.wait_ge(s["o2_evac"], 2 * b - 1 + g)
                for k in range(2):
                    for part in range(2):
                        for r in range(4):
                            out = oa[32 * r:32 * (r + 1), 512 * g + S * k:512 * g + S * (k + 1)]
                            if part == 0:
                                rhs = pb[3 * g + k][:, S * r:S * (r + 1)]
                            else:
                                out, rhs = out[:, P:S], pb[3 * g + 2][:, P * (4 * k + r):P * (4 * k + r + 1)]
                            last = mm(out, v2f[:, part, 8 * g + 4 * k + r], rhs, start=(k == 0 and part == 0), stop=(part == 1),
                                      skip_group_check=True)
                last.then_inc(s["pv2_done"], 1)

            def turn_outputs(b):
                pe.wait_ge(s["o2_evac"], 2 * (b + 1))
                if not (isinstance(b, int) and b == 0):
                    pe.wait_ge(s["x3_done"], b)
                for t in range(T):
                    for k in range(4):
                        last = turn(tm[:, 512 * t + P * k:512 * t + P * (k + 1)], o2s[:, k // 2, S * (k % 2) + P * t:S * (k % 2) + P * (t + 1)], ident[:])
                last.then_inc(s["o2_turned"], 1)

            def turn_back(b):
                pe.wait_ge(s["ao_ready"], b + 1)
                for t in range(T):
                    last = turn(tm[:, P * t:P * (t + 1)], ao[:, t], ident[:])
                last.then_inc(s["ao_turned"], 1)

            def out_product2(b):
                pe.wait_ge(s["aoT_ready"], b + 1)
                for t in range(T):
                    last = mm(tm[:, 512 + DN * t:512 + DN * (t + 1)], aoT[:, P * t:P * (t + 1)], wb[:, W_O:W_O + DN], start=True, stop=True)
                last.then_inc(s["wo_done"], 1)

            def attend2(b, tail, following):
                scores2(b, 0)
                scores2(b, 1)
                if tail:
                    turn_outputs(b - 1)
                scores2(b, 2)
                if following:
                    turn_parts(b + 1, 0)
                if tail:
                    turn_back(b - 1)
                scores2(b, 3)
                if not tail:
                    project2(1)
                values2(b, 0)
                scores2(b, 4, following)
                if tail:
                    out_product2(b - 1)
                scores2(b, 5)
                if following:
                    turn_parts(b + 1, 1)
                values2(b, 1)

            pe.wait_ge(s["exp_done"], 6 * B)
            turn_parts(0, 0)
            turn_parts(0, 1)
            attend2(0, False, True)
            pe.wait_ge(s["v2_done"], 2)
            out_product(B - 1)
            project2(2)
            pe.wait_ge(s["v2_done"], 3)
            with pe.Fori(1, B - 1) as b:
                attend2(b, True, True)
            attend2(B - 1, True, False)

            def gate(h, turned, logits):
                pe.wait_ge(s["f_ready"], h + 1)
                for t in range(4):
                    last = turn(turned[:, D * t:D * (t + 1)], xc[:, 4 * h + t], ident[:])
                last.then_inc(s["f_turned"], 1)
                pe.wait_ge(s["xfT_ready"], h + 1)
                for t in range(4):
                    last = mm(logits[:, E * t:E * (t + 1)], xfT[:, 2 * h + t // 2, P * (t % 2):P * (t % 2 + 1)], wb[:, W_G:W_G + E],
                              start=True, stop=True)
                last.then_inc(s["gate_done"], 1)

            def layer(n, w, src, outs=2):
                chunks = len(src)
                for o in range(outs):
                    for i, part in enumerate(src):
                        last = mm(sc[:, 512 * (n % 4) + S * o:512 * (n % 4) + S * (o + 1)],
                                  wb[:, w + HID * i + P * o:w + HID * i + P * (o + 1)], part, start=(i == 0), stop=(i == chunks - 1))
                last.then_inc(s["u_done"], 1)

            def first_layers(b):
                xin = [xfT[:, b]]
                pe.wait_ge(s["silu_a"], b)
                layer(0, W_L1, xin)
                pe.wait_ge(s["h1_ready"], b)
                layer(1, W_D3, xin, 1)
                pe.wait_ge(s["u_act"], 7 * b)
                layer(2, W_E0, xin)
                pe.wait_ge(s["u_act"], 7 * b + 1)
                layer(3, W_L2, [h2a[:, 0], h2a[:, 1]])

            def last_layers(b):
                xin = [xfT[:, b]]
                layer(4, W_E11, xin)
                pe.wait_ge(s["u_act"], 7 * b + 2)
                layer(5, W_E12, xin)
                pe.wait_ge(s["u_act"], 7 * b + 3)
                layer(6, W_U3, [h3a])
                pe.wait_ge(s["u_act"], 7 * b + 4)
                layer(7, W_L3, [h2b[:, 0], h2b[:, 1]])

            def down(b):
                pe.wait_ge(s["h1_ready"], b + 1)
                pe.wait_ge(s["u_act"], 7 * b + 7)
                pe.wait_ge(s["res_done"], b)
                for t in range(T):
                    for i, h in enumerate((h0, h1, h2c, h3b)):
                        for k in range(2):
                            w = W_DN + (2 * i + k) * DN
                            last = mm(oa[:, 512 * t + DN * i:512 * t + DN * (i + 1)], h[:, k, P * t:P * (t + 1)], wb[:, w:w + DN],
                                      start=(k == 0), stop=(k == 1))
                    last.then_inc(s["down_done"], 1)

            pe.wait_ge(s["exp2_done"], 6 * B)
            pe.wait_ge(s["o2_evac"], 2 * B)
            gate(0, sc[:, 0:512], oa[:, 512:512 + 4 * E])
            turn_outputs(B - 1)
            first_layers(0)
            turn_back(B - 1)
            last_layers(0)
            out_product2(B - 1)
            pe.wait_ge(s["lg_ready"], 1)
            down(0)
            pe.wait_ge(s["x3_done"], B)
            gate(1, zb, mb[:, 0:4 * E])
            with pe.Fori(1, B) as b:
                first_layers(b)
                last_layers(b)
                down(b)


def kernel(**a):
    import numpy as np
    from concourse import bacc
    from concourse.bass_utils import run_bass_kernel_spmd

    a = {k: np.asarray(v) for k, v in a.items()}
    c = {k[len("L0_cond_"):]: v for k, v in a.items() if k.startswith("L0_cond_")}
    f = {k[len("L0_ffn_"):]: v for k, v in a.items() if k.startswith("L0_ffn_")}
    cond = a["cond_64"]

    def chunks(w):
        return np.concatenate([w[i:i + P] for i in range(0, w.shape[0], P)], axis=1)

    cols = np.stack([c["g_norm"], f["n1_w"], f["n2_w"], np.tile(c["q_scale"], 2), np.tile(c["k_scale"], 2),
                     np.tile(cond[0], 2), np.tile(f["qn_w"], H), np.tile(f["kn_w"], H)], axis=1)
    rows = np.concatenate([c["g_out"], c["w0"][0], c["b0"], c["g0"], c["b1"], c["g1"], c["q_scale"], c["k_scale"],
                           cond[1], f["qn_w"], f["kn_w"]])[None]
    wk = c["Wkv"][:, :DH]
    wa = np.concatenate([wk, wk, c["Wkv"][:, DH:], c["w1"], c["w2"], c["Wq"], chunks(c["Wout"])], axis=1)
    downs = [chunks(f[n][OFF:].T) for n in ("e0_down", "e1_down", "e2_l4", "e3_out")]
    wb = np.concatenate([f["wq"].T, f["wk"].T, f["wv"].T, f["wo"][OFF:].T, f["gate_w"].T, f["e0_up"].T, f["e1_w1"].T,
                         f["e1_w2"].T, f["e2_l1"].T, chunks(f["e2_l2"].T), chunks(f["e2_l3"].T), f["e3_down"].T,
                         f["e3_up"].T] + downs, axis=1)
    assert wa.shape[1] == A_ALL and wb.shape[1] == W_ALL and rows.shape[1] == R_ALL
    told = a["mask_BxS_bf1"]
    mask = np.zeros((P, B, 3), told.dtype)
    mask[P - 1, :, 0] = True
    mask[:P - 1, :, 0] = told[:, P - 2::-1].T
    mask[:, :, 1] = told[:, S - 2:P - 2:-1].T
    mask[:2, :, 2] = told[:, P - 1::P].T
    arrays = {"x": a["x"].reshape(B * S, D), "cols": cols, "rows": rows, "small": np.stack([c["b2"], c["null_attn_bias"]], axis=1),
              "mask": mask, "wa": wa, "wb": wb}
    arrays = {f"in_{k}": np.ascontiguousarray(v) for k, v in arrays.items()}

    nc = bacc.Bacc("TRN2", target_bir_lowering=False, num_devices=1)
    ins = [nc.dram_tensor(k, v.shape, mybir.dt.from_np(v.dtype), kind="ExternalInput").ap() for k, v in arrays.items()]
    out = nc.dram_tensor("out", (B * S, D), F32, kind="ExternalOutput").ap()
    adaln_ffn(nc, *ins, out)
    r = run_bass_kernel_spmd(nc, [arrays], core_ids=[0])
    return r.results[0]["out"].reshape(B, S, D)
```
